# Optimizing a Trainium2 kernel written in Bass

```python
import numpy as np
import jax
import jax.numpy as jnp

def _softmax(x, axis=-1):
    return jax.nn.softmax(x, axis=axis)

def _gelu(x):
    return jax.nn.gelu(x, approximate=True)

def _silu(x):
    return jax.nn.silu(x)

def _sigmoid(x):
    return jax.nn.sigmoid(x)

def _layernorm(x, axis=-1, eps=1e-05):
    m = jnp.mean(x, axis=axis, keepdims=True)
    v = jnp.var(x, axis=axis, keepdims=True)
    return (x - m) / jnp.sqrt(v + eps)

def _scatter_add(tgt, idx, src, axis=0):
    return tgt.at[idx].add(src)

def _segment_sum(src, seg, n):
    return jax.ops.segment_sum(src, seg, n)
kernel_name = 'mk_gnn_ffn_d1_gnn_r8_e57853'

def setup_inputs(seed: int=0):
    np.random.seed(seed)
    _w = jnp.asarray

    def _rec_inputs():
        import jax
        import jax.numpy as jnp
        _gk = jax.random.key(seed)
        x = -0.0003713 + 1 * jax.random.normal(jax.random.fold_in(_gk, 1), (6250, 256), jnp.float32)
        src = jax.random.randint(jax.random.fold_in(_gk, 2), (200000,), 0, 6250, jnp.int32)
        dst = jax.random.randint(jax.random.fold_in(_gk, 3), (200000,), 0, 6250, jnp.int32)
        _o = jnp.argsort(dst, stable=True)
        src = src[_o]
        dst = dst[_o]
        edge_attr_3 = -1.09012e-05 + 0.99985 * jax.random.normal(jax.random.fold_in(_gk, 11), (200000, 3), jnp.float32)
        return (x, src, dst, edge_attr_3)
    x, src, dst, edge_attr_3 = _rec_inputs()

    def _L0_gnn_setup():
        import jax, jax.numpy as jnp
        import numpy as np
        N = 6250
        E = 50000
        IN = 256
        H = 8
        D = 32
        EF = 3
        key = jax.random.key(seed)
        ks = jax.random.split(key, 8)
        x = jax.random.normal(ks[0], (N, IN), dtype=jnp.float32)
        edge_index = jax.random.randint(ks[1], (2, E), 0, N, dtype=jnp.int64)
        edge_attr = jax.random.normal(ks[2], (E, EF), dtype=jnp.float32)
        W = jax.random.normal(ks[3], (H * D, IN), dtype=jnp.float32) * np.float32(np.sqrt(2.0 / (IN + H * D)))
        a_src = jax.random.normal(ks[4], (H, D), dtype=jnp.float32) * np.float32(np.sqrt(2.0 / (H + D)))
        a_dst = jax.random.normal(ks[5], (H, D), dtype=jnp.float32) * np.float32(np.sqrt(2.0 / (H + D)))
        edge_W = jax.random.normal(ks[6], (H * D, EF), dtype=jnp.float32) * np.float32(np.sqrt(2.0 / (EF + H * D)))
        edge_b = jnp.zeros((H * D,), dtype=jnp.float32)
        bias = jnp.zeros((H * D,), dtype=jnp.float32)
        return {'x': x, 'W': W, 'a_src': a_src, 'a_dst': a_dst, 'edge_W': edge_W, 'edge_b': edge_b, 'bias': bias, 'edge_attr': edge_attr, 'edge_index': edge_index}
    _L0_gnn_all = _L0_gnn_setup()
    _L0_gnn_in = {k: v for k, v in _L0_gnn_all.items() if k in ('W', 'a_src', 'a_dst', 'edge_W', 'edge_b', 'bias')}
    del _L0_gnn_all

    def _L0_ffn_setup():
        import math
        import jax, jax.numpy as jnp
        import numpy as np
        CAPACITY_FACTOR = 1.25
        TOP_K = 2
        LN_EPS = 1e-05

        def _layer_norm(x, gamma, beta):
            mu = jnp.mean(x, axis=-1, keepdims=True)
            var = jnp.var(x, axis=-1, keepdims=True)
            return (x - mu) * jax.lax.rsqrt(var + LN_EPS) * gamma + beta
        key = jax.random.key(seed)
        ks = jax.random.split(key, 4)
        B, S, D, F, E = (8, 512, 256, 512, 8)
        x = jax.random.normal(ks[0], (B, S, D), dtype=jnp.float32)
        Wr = jax.random.normal(ks[1], (D, E), dtype=jnp.float32) / np.sqrt(D)
        br = jnp.zeros((E,), jnp.float32)
        W1 = jax.random.normal(ks[2], (E, D, F), dtype=jnp.float32) / np.sqrt(D)
        b1 = jnp.zeros((E, F), jnp.float32)
        W2 = jax.random.normal(ks[3], (E, F, D), dtype=jnp.float32) / np.sqrt(F)
        b2 = jnp.zeros((E, D), jnp.float32)
        gamma = jnp.ones((D,), jnp.float32)
        beta = jnp.zeros((D,), jnp.float32)
        return {'x': x, 'Wr': Wr, 'br': br, 'W1': W1, 'b1': b1, 'W2': W2, 'b2': b2, 'gamma': gamma, 'beta': beta}
    _L0_ffn_all = _L0_ffn_setup()
    _L0_ffn_in = {k: v for k, v in _L0_ffn_all.items() if k in ('Wr', 'br', 'W1', 'b1', 'W2', 'b2', 'gamma', 'beta')}
    del _L0_ffn_all
    return {'x': x, 'src': src, 'dst': dst, 'edge_attr_3': edge_attr_3, 'L0_gnn_W': _L0_gnn_in['W'], 'L0_gnn_a_src': _L0_gnn_in['a_src'], 'L0_gnn_a_dst': _L0_gnn_in['a_dst'], 'L0_gnn_edge_W': _L0_gnn_in['edge_W'], 'L0_gnn_edge_b': _L0_gnn_in['edge_b'], 'L0_gnn_bias': _L0_gnn_in['bias'], 'L0_ffn_Wr': _L0_ffn_in['Wr'], 'L0_ffn_br': _L0_ffn_in['br'], 'L0_ffn_W1': _L0_ffn_in['W1'], 'L0_ffn_b1': _L0_ffn_in['b1'], 'L0_ffn_W2': _L0_ffn_in['W2'], 'L0_ffn_b2': _L0_ffn_in['b2'], 'L0_ffn_gamma': _L0_ffn_in['gamma'], 'L0_ffn_beta': _L0_ffn_in['beta']}

def reference(x, src, dst, edge_attr_3, L0_gnn_W, L0_gnn_a_src, L0_gnn_a_dst, L0_gnn_edge_W, L0_gnn_edge_b, L0_gnn_bias, L0_ffn_Wr, L0_ffn_br, L0_ffn_W1, L0_ffn_b1, L0_ffn_W2, L0_ffn_b2, L0_ffn_gamma, L0_ffn_beta):
    import jax
    import jax.numpy as jnp

    def _L0_gnn_ref(x, W, a_src, a_dst, edge_W, edge_b, bias, edge_attr, edge_index):
        import jax, jax.numpy as jnp
        import numpy as np
        N = 6250
        E = 50000
        IN = 256
        H = 8
        D = 32
        EF = 3
        n = x.shape[0]
        h = (x @ W.T).reshape(n, H, D)
        src, dst = (edge_index[0], edge_index[1])
        h_src = h[src]
        h_dst = h[dst]
        alpha = jnp.einsum('ehd,hd->eh', h_src, a_src) + jnp.einsum('ehd,hd->eh', h_dst, a_dst)
        enc = jax.nn.relu(edge_attr @ edge_W.T + edge_b).reshape(-1, H, D)
        alpha = alpha + jnp.sum(enc * h_dst, axis=-1)
        alpha = jnp.where(alpha >= 0, alpha, 0.2 * alpha)
        amax = jax.ops.segment_max(alpha, dst, num_segments=n)
        ex = jnp.exp(alpha - amax[dst])
        denom = jax.ops.segment_sum(ex, dst, num_segments=n)
        attn = ex / jnp.maximum(denom[dst], 1e-10)
        out = jax.ops.segment_sum(h_src * attn[..., None], dst, num_segments=n)
        return out.reshape(n, H * D) + bias

    def _L0_ffn_ref(x, Wr, br, W1, b1, W2, b2, gamma, beta):
        import math
        import jax, jax.numpy as jnp
        import numpy as np
        CAPACITY_FACTOR = 1.25
        TOP_K = 2
        LN_EPS = 1e-05

        def _layer_norm(x, gamma, beta):
            mu = jnp.mean(x, axis=-1, keepdims=True)
            var = jnp.var(x, axis=-1, keepdims=True)
            return (x - mu) * jax.lax.rsqrt(var + LN_EPS) * gamma + beta
        B, S, D = x.shape
        E = Wr.shape[1]
        N = B * S
        K = TOP_K
        logits = jnp.mean(x, axis=1) @ Wr + br
        routing_weights = jax.nn.softmax(logits, axis=-1)
        capacity = float(math.ceil(N * CAPACITY_FACTOR / E))
        expected_loads = routing_weights.sum(axis=0) * (N / B)
        scale = jnp.where(expected_loads > capacity, capacity / expected_loads, 1.0)
        routing_weights = jax.nn.softmax(routing_weights * scale, axis=-1)
        rw_tok = jnp.broadcast_to(routing_weights[:, None, :], (B, S, E)).reshape(N, E)
        top_w, top_i = jax.lax.top_k(rw_tok, K)
        top_w = jax.nn.softmax(top_w, axis=-1)
        xf = x.reshape(N, D)
        h = jax.nn.gelu(jnp.einsum('nd,edf->enf', xf, W1) + b1[:, None, :], approximate=False)
        y = jnp.einsum('enf,efd->end', h, W2) + b2[:, None, :]
        w_dense = jnp.zeros((N, E), x.dtype).at[jnp.arange(N)[:, None], top_i].add(top_w)
        out = jnp.einsum('ne,end->nd', w_dense, y).reshape(B, S, D)
        out = _layer_norm(out + x, gamma, beta)
        return out
    edge_index = jnp.stack([src, dst])
    x = x + _L0_gnn_ref(_layernorm(x, axis=-1), L0_gnn_W, L0_gnn_a_src, L0_gnn_a_dst, L0_gnn_edge_W, L0_gnn_edge_b, L0_gnn_bias, edge_attr_3, edge_index)
    x = x + _L0_ffn_ref(_layernorm(x, axis=-1)[None], L0_ffn_Wr, L0_ffn_br, L0_ffn_W1, L0_ffn_b1, L0_ffn_W2, L0_ffn_b2, L0_ffn_gamma, L0_ffn_beta)[0]
    return x

_drawn_inputs = setup_inputs


def setup_inputs(seed=0):
    import zlib

    import numpy as np

    out = dict(_drawn_inputs(seed))
    spreads = {'L0_gnn_edge_b': (0.0, 0.1),
     'L0_gnn_bias': (0.0, 0.1),
     'L0_ffn_br': (0.0, 2.0),
     'L0_ffn_b1': (0.0, 0.38),
     'L0_ffn_b2': (0.0, 0.1),
     'L0_ffn_gamma': (1.0, 0.2),
     'L0_ffn_beta': (0.0, 0.1)}
    factors = {'L0_ffn_Wr': 64.0}
    for name, (base, spread) in spreads.items():
        noise = np.random.default_rng([zlib.crc32(name.encode()), seed]).standard_normal(out[name].shape)
        drawn = base * np.exp(spread * noise) if base else spread * noise
        out[name] = jnp.asarray(drawn.astype(out[name].dtype))
    for name, factor in factors.items():
        out[name] = (out[name] * factor).astype(out[name].dtype)
    return out
```

```python
from contextlib import ExitStack

import concourse.bass as bass
from concourse import mybir

F32, BF16, I32, U32 = mybir.dt.float32, mybir.dt.bfloat16, mybir.dt.int32, mybir.dt.uint32
ALU, ACT, AX = mybir.AluOpType, mybir.ActivationFunctionType, mybir.AxisListType

P = 128
N, E = 6250, 200000
D, H, HD = 256, 8, 32
EF = 3
FF, NX, TOPK = 512, 8, 2
LN_EPS = 1e-5
CAPACITY = float(-(-N * 5 // (4 * NX)))

C = 8
CHUNK = P * C
NC = -(-E // CHUNK)
FULL = E // CHUNK
REST = E - FULL * CHUNK
TILES = -(-N // P)
STEPS = NC + TILES - 1
NT = TILES + TILES % 2
LASTROWS = N - (TILES - 1) * P
GROUPS = [(g, min(P, NC - g)) for g in range(0, NC, P)]

ROW = H * (HD + 1)
PART = D + H
KA = 12
KE = 3 * KA
REC = C * (3 + KE // 2)
DST, LAST, SRC, ATTR = 0, C, 2 * C, 3 * C
BIG = 1e30
PAD_DST = 1 << 20
assert C == 8 and NC <= 2 * P


def at(ap, t):
    return ap[:, t, :] if isinstance(t, int) else ap[:, bass.ds(t, 1), :].rearrange("p o n -> p (o n)")


def block_of(ap, t):
    return ap[t, :, :] if isinstance(t, int) else ap[bass.ds(t, 1), :, :].rearrange("o p n -> p (o n)")


def merge_moments(nc, dve, stats, halves, moments, made):
    m0, v0, m1, v1 = (stats[:, :, i] for i in (1, 2, 4, 5))
    nc.vector.tensor_tensor(halves[:, 0, :], m0, m1, ALU.add).then_inc(made, 1)
    nc.vector.tensor_tensor(halves[:, 1, :], m0, m1, ALU.subtract).then_inc(made, 1)
    nc.vector.tensor_tensor(halves[:, 2, :], v0, v1, ALU.add).then_inc(made, 1)
    dve.wait_ge(made, 3)
    nc.vector.tensor_scalar(moments[:, :, 0], halves[:, 0, :], 0.5, None, ALU.mult)
    nc.vector.scalar_tensor_tensor(halves[:, 3, :], halves[:, 1, :], 0.25, halves[:, 1, :], ALU.mult, ALU.mult).then_inc(made, 1)
    dve.wait_ge(made, 4)
    nc.vector.scalar_tensor_tensor(moments[:, :, 1], halves[:, 2, :], 1.0 / D, halves[:, 3, :], ALU.mult, ALU.add).then_inc(made, 2)


def spread(ap, n):
    return ap.unsqueeze(ap.ndim).broadcast_to([*ap.shape, n])


class Scope(ExitStack):

    def __init__(self, nc):
        super().__init__()
        self.nc = nc

    def sb(self, name, shape, dt=F32):
        return self.enter_context(self.nc.sbuf_tensor(name, shape, dt))

    def ps(self, name, shape, dt=F32):
        return self.enter_context(self.nc.psum_tensor(name, shape, dt))

    def sem(self, name):
        return self.enter_context(self.nc.semaphore(name))


def prologue(nc, a, scr, keep):
    with Scope(nc) as m:
        x_all = keep["acc"][:, :, 0:D]
        dst_rows = m.sb("dst_rows", [P, CHUNK], I32)
        src_rows = m.sb("src_rows", [P, CHUNK], I32)
        attr_rows = m.sb("attr_rows", [P, CHUNK * EF])
        rec = m.sb("rec", [P, P, REC])
        start_rows = m.sb("start_rows", [P, C, P])
        changed = m.sb("changed", [P, P, C])
        steps_at = m.sb("steps_at", [P, STEPS])
        started = m.sb("started", [P, 2, STEPS])
        tile_edges = m.sb("tile_edges", [P, TILES - 1])
        reached = m.sb("reached", [P, TILES - 1])
        chunk_tile = m.sb("chunk_tile", [P, 2])
        chunk_start = m.sb("chunk_start", [P, 2])
        chunk_no = m.sb("chunk_no", [P, 2])
        step_c = m.sb("step_c", [P, STEPS])
        step_t = m.sb("step_t", [P, STEPS])
        ones = m.sb("ones", [P, P])
        stats = m.sb("stats", [P, NT, 6])
        moments = m.sb("moments", [P, NT, 2])
        halves = m.sb("halves", [P, 4, NT])
        std = m.sb("std", [P, NT])
        rstd = m.sb("rstd", [P, NT, 1])
        eps = m.sb("eps", [P, 1])
        xn = m.sb("xn", [P, 2, D])
        xnT = m.sb("xnT", [P, 2, 2, P])
        w_nat = m.sb("w_nat", [P, 2, D])
        w_ext = m.sb("w_ext", [P, 2, D + 2 * H])
        a_diag = m.sb("a_diag", [P, 2, 2, H])
        a_col = m.sb("a_col", [P, 2, 2])
        out_rows = m.sb("out_rows", [P, 2, ROW])
        dst_score = m.sb("dst_score", [P, 2, H])
        out_parts = m.sb("out_parts", [P, 2, 3 * PART], BF16)
        part_left = m.sb("part_left", [P, PART])
        enc_f = m.sb("enc_f", [KA, D])
        enc_left = m.sb("enc_left", [KA, D])
        enc_p = m.sb("enc_p", [KA, 3, D], BF16)
        p_xT = [m.ps(f"p_xT{i}", [P, 2, P]) for i in range(2)]
        p_h = [m.ps(f"p_h{i}", [P, D + 2 * H]) for i in range(2)]
        p_w = m.ps("p_w", [P, 512])
        p_v = m.ps("p_v", [P, 4 * H])
        p_s = m.ps("p_s", [P, STEPS])

        names = """w_loaded x_loaded enc_loaded zeros_made ones_made consts_made ident_made ident_filled row_pad enc_hi enc_l enc_mid
            enc_parts enc_moved rec_made rec_stored started_at counted starts_made rec_copied diag_zero diag_made wT_made v_made
            wext_made stats_made moments_made std_made rstd_made xn_made xT_made xT_moved h_made rows_made
            hi_made left_made mid_made parts_made dst_made chg_made a_hi a_left a_mid reached_s ctile_s cfix_s cstart_s
            stepc_s stept_s tables_s rec_const zero_acc""".split()
        s = {n: m.sem("s_" + n) for n in names}
        s_edges = [m.sem(f"s_edges_loaded{g}") for g in range(len(GROUPS))]
        s_stored = [m.sem(f"s_tables_stored{i}") for i in range(2)]
        rec_i = rec[:, :, :].bitcast(I32)
        attr_w = rec[:, :, :].bitcast(BF16)[:, :, 2 * ATTR:].rearrange("c p (k j w) -> c p k j w", k=C, j=3)
        attr_p = rec[:, :, :].bitcast(BF16)[:, :, 2 * ATTR:].rearrange("c p (k j i f) -> c p k j i f", k=C, j=3, i=3)[:, :, :, 0, :, :]

        block = m.enter_context(nc.Block())

        def store_records(sp, g):
            c0, n = GROUPS[g]
            sp.wait_ge(s["rec_copied"], 2 * g + 2)
            sp.dma_start(scr["edges"][c0:c0 + n, :, :], rec[0:n, :, :]).then_inc(s["rec_stored"], 16)
            for h in range(H):
                sp.dma_start(scr["starts"][c0:c0 + n, :, :].rearrange("c (k h) p -> c k h p", h=H)[:, :, h, :],
                             start_rows[0:n, :, :]).then_inc(s["rec_stored"], 16)

        @block.sync
        def _(sp):
            sp.dma_start(w_nat[:, :, :], a["W"].rearrange("(c p) n -> p c n", p=P)).then_inc(s["w_loaded"], 16)
            for half in range(2):
                for i, name in enumerate(("a_src", "a_dst")):
                    v = a[name].rearrange("h (d o) -> (h d) o", o=1)[half * P:(half + 1) * P, :]
                    sp.dma_start(a_col[:, half, i:i + 1], v).then_inc(s["w_loaded"], 16)
            sp.wait_ge(s["zeros_made"], 1)
            full = (TILES - 1) * P
            sp.dma_start(x_all[:, 0:TILES - 1, :], a["x"][0:full, :].rearrange("(t p) n -> p t n", p=P)).then_inc(s["x_loaded"], 16)
            sp.dma_start(x_all[0:LASTROWS, TILES - 1, :], a["x"][full:N, :]).then_inc(s["x_loaded"], 16)
            for g, (c0, n) in enumerate(GROUPS):
                if g:
                    sp.wait_ge(s["row_pad"], 1)
                whole = min(n, FULL - c0)
                for rows, name, w in ((dst_rows, "dst", 1), (src_rows, "src", 1), (attr_rows, "attr", EF)):
                    flat = a[name] if w == 1 else a[name].rearrange("e f -> (e f)")
                    sp.dma_start(rows[0:whole, :], flat[c0 * CHUNK * w:(c0 + whole) * CHUNK * w]
                                 .rearrange("(c e) -> c e", c=whole)).then_inc(s_edges[g], 16)
                    if c0 + n > FULL:
                        sp.dma_start(rows[whole:whole + 1, 0:REST * w], flat[FULL * CHUNK * w:E * w]
                                     .rearrange("(c e) -> c e", c=1)).then_inc(s_edges[g], 16)
                if g == 0:
                    continue
                store_records(sp, g - 1)
            store_records(sp, len(GROUPS) - 1)
            sp.wait_ge(s["rec_stored"], 16 * (1 + H) * len(GROUPS))

        @block.gpsimd
        def _(pool):
            nc.gpsimd.memset(x_all[:, TILES - 1:NT, :], 0.0).then_inc(s["zeros_made"], 1)
            nc.gpsimd.memset(keep["ident"][:, :], 0.0).then_inc(s["ident_made"], 1)
            nc.gpsimd.memset(keep["identb"][:, :], 0.0).then_inc(s["ident_made"], 1)
            pool.wait_ge(s["ident_made"], 2)
            for one in (keep["ident"], keep["identb"]):
                nc.gpsimd.affine_select(out=one[:, :], in_=one[:, :], compare_op=ALU.not_equal, fill=1.0, base=0,
                                        pattern=[[-1, P]], channel_multiplier=1).then_inc(s["ident_filled"], 1)
            nc.gpsimd.memset(ones[:, :], 1.0).then_inc(s["ones_made"], 1)
            nc.gpsimd.memset(eps[:, :], LN_EPS).then_inc(s["consts_made"], 1)
            for i in range(3):
                for f in range(EF):
                    pool.dma_start(enc_f[4 * i + f:4 * i + f + 1, :], a["edge_W"].rearrange("n f -> f n")[f:f + 1, :],
                                   allow_slow_non_contiguous=True).then_inc(s["enc_loaded"], 16)
                pool.dma_start(enc_f[4 * i + EF:4 * i + 4, :], a["edge_b"].rearrange("(o n) -> o n", o=1)).then_inc(s["enc_loaded"], 16)
            nc.gpsimd.iota(steps_at[:, :], pattern=[[1, STEPS]], base=0, channel_multiplier=0,
                           allow_small_or_imprecise_dtypes=True).then_inc(s["consts_made"], 1)
            nc.gpsimd.iota(tile_edges[:, :], pattern=[[P, TILES - 1]], base=P, channel_multiplier=0,
                           allow_small_or_imprecise_dtypes=True).then_inc(s["consts_made"], 1)
            nc.gpsimd.iota(keep["node_at"][:, :], pattern=[[1, P]], base=0, channel_multiplier=0,
                           allow_small_or_imprecise_dtypes=True).then_inc(s["consts_made"], 1)
            for g, (c0, n) in enumerate(GROUPS):
                nc.gpsimd.iota(chunk_no[:, g:g + 1], pattern=[[0, 1]], base=c0, channel_multiplier=1,
                               allow_small_or_imprecise_dtypes=True).then_inc(s["consts_made"], 1)
            pool.wait_ge(s["enc_parts"], 1)
            for j in range(3):
                pool.dma_start(keep["expander"][KA * j:KA * (j + 1), :], enc_p[:, j, :]).then_inc(s["enc_moved"], 16)
            pool.wait_ge(s["enc_moved"], 48)
            for g, (c0, n) in enumerate(GROUPS):
                pool.wait_ge(s["rec_made"], g + 1)
                nc.gpsimd.tensor_copy(attr_w[0:n, :, :, 2, :], attr_w[0:n, :, :, 0, :]).then_inc(s["rec_copied"], 1)
            pool.wait_ge(s["xn_made"], NT)
            nc.gpsimd.memset(keep["acc"][:, :, :], 0.0).then_inc(s["zero_acc"], 1)
            pool.wait_ge(s["zero_acc"], 2)

        @block.tensor
        def _(pe):
            pe.wait_ge(s["w_loaded"], 80)
            pe.wait_ge(s["ident_filled"], 2)
            for i in range(2):
                for o in range(2):
                    last = nc.tensor.transpose(p_w[:, (2 * i + o) * P:(2 * i + o + 1) * P],
                                               w_nat[:, o, i * P:(i + 1) * P], keep["ident"][:, :])
            last.then_inc(s["wT_made"], 1)
            pe.wait_ge(s["diag_made"], 1)
            for i in range(2):
                for o in range(2):
                    last = nc.tensor.matmul(p_v[:, i * 2 * H:(i + 1) * 2 * H], w_nat[:, o, i * P:(i + 1) * P],
                                            a_diag[:, o, :, :].rearrange("p i h -> p (i h)"), start=(o == 0), stop=(o == 1))
            last.then_inc(s["v_made"], 1)

            def transpose_tile(t, b):
                pe.wait_ge(s["xn_made"], t + 1)
                if not (isinstance(t, int) and t < 2):
                    pe.wait_ge(s["xT_moved"], t - 1)
                for i in range(2):
                    last = nc.tensor.transpose(p_xT[b][:, i, :], xn[:, b, i * P:(i + 1) * P], keep["ident"][:, :])
                last.then_inc(s["xT_made"], 1)

            def project_tile(t, b):
                pe.wait_ge(s["xT_moved"], t + 1)
                if not (isinstance(t, int) and t < 2):
                    pe.wait_ge(s["rows_made"], t - 1)
                for i in range(2):
                    last = nc.tensor.matmul(p_h[b][:, :], xnT[:, b, i, :], w_ext[:, i, :], start=(i == 0), stop=(i == 1))
                last.then_inc(s["h_made"], 1)

            pe.wait_ge(s["wext_made"], 2)
            transpose_tile(0, 0)
            transpose_tile(1, 1)
            project_tile(0, 0)
            with nc.tensor.Fori(0, (NT - 2) // 2) as i:
                for u in range(2):
                    transpose_tile(2 * i + 2 + u, u)
                    project_tile(2 * i + 1 + u, 1 - u)
            project_tile(NT - 1, 1)
            pe.wait_ge(s["ones_made"], 1)
            for g, (c0, n) in enumerate(GROUPS):
                pe.wait_ge(s["started_at"], g + 1)
                nc.tensor.matmul(p_s[:, :], ones[0:n, :], started[0:n, g, :], start=(g == 0),
                                 stop=(g == len(GROUPS) - 1)).then_inc(s["counted"], 1)

        @block.scalar
        def _(act):
            act.wait_ge(s["moments_made"], 6)
            act.wait_ge(s["consts_made"], 1)
            nc.scalar.activation(std[:, :], moments[:, :, 1], ACT.Sqrt, bias=eps[:, 0:1]).then_inc(s["std_made"], 1)

            def move_transposed(t, b):
                act.wait_ge(s["xT_made"], t + 1)
                if not (isinstance(t, int) and t < 2):
                    act.wait_ge(s["h_made"], t - 1)
                nc.scalar.copy(xnT[:, b, :, :], p_xT[b][:, :, :]).then_inc(s["xT_moved"], 1)

            def make_rows(t, b, stored):
                act.wait_ge(s["h_made"], t + 1)
                if not (isinstance(stored, int) and stored == 0):
                    act.wait_ge(s_stored[b], stored * 32)
                    act.wait_ge(s["left_made"], 2 * t - 2)
                v = out_rows[:, b, :].rearrange("p (h d) -> p h d", h=H)
                nc.scalar.copy(v[:, :, 0:HD], p_h[b][:, 0:D].rearrange("p (h d) -> p h d", h=H))
                nc.scalar.copy(v[:, :, HD], p_h[b][:, D:D + H])
                nc.scalar.copy(dst_score[:, b, :], p_h[b][:, D + H:D + 2 * H]).then_inc(s["rows_made"], 1)

            def store(t, b):
                act.wait_ge(s["rows_made"], t + 1)
                act.wait_ge(s["parts_made"], t + 1)
                act.dma_start(block_of(scr["rows"].rearrange("(t p) n -> t p n", p=P), t), out_rows[:, b, :]).then_inc(s_stored[b], 16)
                act.dma_start(block_of(scr["parts"], t), out_parts[:, b, :]).then_inc(s_stored[b], 16)

            move_transposed(0, 0)
            move_transposed(1, 1)
            make_rows(0, 0, 0)
            store(0, 0)
            make_rows(1, 1, 0)
            with nc.scalar.Fori(0, (NT - 2) // 2) as i:
                move_transposed(2 * i + 2, 0)
                store(2 * i + 1, 1)
                make_rows(2 * i + 2, 0, i + 1)
                move_transposed(2 * i + 3, 1)
                store(2 * i + 2, 0)
                make_rows(2 * i + 3, 1, i + 1)
            store(NT - 1, 1)
            for b in range(2):
                act.wait_ge(s_stored[b], 32 * (NT // 2))
            for g, (c0, n) in enumerate(GROUPS):
                act.wait_ge(s["rec_made"], g + 1)
                nc.scalar.copy(attr_w[0:n, :, :, 1, :], attr_w[0:n, :, :, 0, :]).then_inc(s["rec_copied"], 1)

        @block.vector
        def _(dve):
            nc.vector.memset(keep["top"][:, :, :], -BIG).then_inc(s["zero_acc"], 1)
            nc.vector.memset(a_diag[:, :, :, :], 0.0).then_inc(s["diag_zero"], 1)
            dve.wait_ge(s["w_loaded"], 80)
            dve.wait_ge(s["diag_zero"], 1)
            for half in range(2):
                for q in range(P // HD):
                    last = nc.vector.tensor_copy(a_diag[q * HD:(q + 1) * HD, half, :, half * (P // HD) + q],
                                                 a_col[q * HD:(q + 1) * HD, half, :])
            last.then_inc(s["diag_made"], 1)
            dve.wait_ge(s["enc_loaded"], 16 * 3 * (EF + 1))
            nc.vector.tensor_copy(enc_p[:, 0, :], enc_f[:, :]).then_inc(s["enc_hi"], 1)
            dve.wait_ge(s["enc_hi"], 1)
            nc.vector.tensor_tensor(enc_left[:, :], enc_f[:, :], enc_p[:, 0, :], ALU.subtract).then_inc(s["enc_l"], 1)
            dve.wait_ge(s["enc_l"], 1)
            nc.vector.tensor_copy(enc_p[:, 1, :], enc_left[:, :]).then_inc(s["enc_mid"], 1)
            dve.wait_ge(s["enc_mid"], 1)
            nc.vector.tensor_tensor(enc_p[:, 2, :], enc_left[:, :], enc_p[:, 1, :], ALU.subtract).then_inc(s["enc_parts"], 1)
            dve.wait_ge(s["wT_made"], 1)
            nc.vector.tensor_copy(w_ext[:, :, 0:D], p_w[:, :].rearrange("p (i n) -> p i n", i=2)).then_inc(s["wext_made"], 1)
            dve.wait_ge(s["v_made"], 1)
            nc.vector.tensor_copy(w_ext[:, :, D:D + 2 * H], p_v[:, :].rearrange("p (i n) -> p i n", i=2)).then_inc(s["wext_made"], 1)

            dve.wait_ge(s["x_loaded"], 32)
            with nc.vector.Fori(0, NT) as t:
                nc.vector.bn_stats(at(stats, t), at(x_all, t)).then_inc(s["stats_made"], 1)
            dve.wait_ge(s["stats_made"], NT)
            merge_moments(nc, dve, stats, halves, moments, s["moments_made"])
            dve.wait_ge(s["std_made"], 1)
            nc.vector.reciprocal(rstd[:, :, 0], std[:, :]).then_inc(s["rstd_made"], 1)
            dve.wait_ge(s["rstd_made"], 1)

            def normalize(t, b):
                if not (isinstance(t, int) and t < 2):
                    dve.wait_ge(s["xT_made"], t - 1)
                mean = moments[:, t, 0:1] if isinstance(t, int) else moments[:, bass.ds(t, 1), 0]
                nc.vector.tensor_scalar(xn[:, b, :], at(x_all, t), mean, at(rstd, t), ALU.subtract, ALU.mult).then_inc(s["xn_made"], 1)

            def make_parts(t, b, stored):
                dve.wait_ge(s["rows_made"], t + 1)
                if not (isinstance(stored, int) and stored == 0):
                    dve.wait_ge(s_stored[b], stored * 32)
                o = out_parts[:, b, :].rearrange("p (i n) -> p i n", i=3)
                h_v = out_rows[:, b, :].rearrange("p (h d) -> p h d", h=H)[:, :, 0:HD]
                hi_v = o[:, 0, 0:D].rearrange("p (h d) -> p h d", h=H)
                nc.vector.tensor_copy(hi_v, h_v).then_inc(s["hi_made"], 1)
                nc.vector.tensor_copy(o[:, 0, D:PART], dst_score[:, b, :]).then_inc(s["hi_made"], 1)
                dve.wait_ge(s["hi_made"], 2 * t + 2)
                if not (isinstance(t, int) and t == 0):
                    dve.wait_ge(s["parts_made"], t)
                nc.vector.tensor_tensor(part_left[:, 0:D].rearrange("p (h d) -> p h d", h=H), h_v, hi_v, ALU.subtract).then_inc(s["left_made"], 1)
                nc.vector.tensor_tensor(part_left[:, D:PART], dst_score[:, b, :], o[:, 0, D:PART], ALU.subtract).then_inc(s["left_made"], 1)
                dve.wait_ge(s["left_made"], 2 * t + 2)
                nc.vector.tensor_copy(o[:, 1, :], part_left[:, :]).then_inc(s["mid_made"], 1)
                dve.wait_ge(s["mid_made"], t + 1)
                nc.vector.tensor_tensor(o[:, 2, :], part_left[:, :], o[:, 1, :], ALU.subtract).then_inc(s["parts_made"], 1)

            normalize(0, 0)
            normalize(1, 1)
            make_parts(0, 0, 0)
            normalize(2, 0)
            make_parts(1, 1, 0)
            normalize(3, 1)
            make_parts(2, 0, 1)
            with nc.vector.Fori(0, (NT - 4) // 2) as i:
                normalize(2 * i + 4, 0)
                make_parts(2 * i + 3, 1, i + 1)
                normalize(2 * i + 5, 1)
                make_parts(2 * i + 4, 0, i + 2)
            make_parts(NT - 1, 1, NT // 2 - 1)

            nc.vector.memset(attr_p[:, :, :, 1, EF], 0.0).then_inc(s["rec_const"], 1)
            nc.vector.memset(attr_p[:, :, :, 2, EF], 0.0).then_inc(s["rec_const"], 1)
            nc.vector.memset(attr_p[:, :, :, 0, EF], 1.0).then_inc(s["rec_const"], 1)
            dve.wait_ge(s["consts_made"], 4 + len(GROUPS))
            for g, (c0, n) in enumerate(GROUPS):
                dve.wait_ge(s_edges[g], 96 if c0 + n > FULL else 48)
                if g:
                    dve.wait_ge(s["rec_stored"], 16 * (1 + H) * g)
                dst = rec[0:n, :, DST:DST + C]
                nc.vector.tensor_copy(dst, dst_rows[0:n, :].rearrange("c (p k) -> c p k", k=C)).then_inc(s["dst_made"], 1)
                nc.vector.tensor_copy(rec_i[0:n, :, SRC:SRC + C], src_rows[0:n, :].rearrange("c (p k) -> c p k", k=C))
                dve.wait_ge(s["dst_made"], g + 1)
                ch = changed[0:n, 0:P - 1, :]
                nc.vector.tensor_tensor(ch, dst[:, 1:P, :], dst[:, 0:P - 1, :], ALU.not_equal).then_inc(s["chg_made"], 1)
                nc.vector.tensor_scalar(reached[0:n, :], tile_edges[0:n, :], rec[0:n, 0, 0:1], None, ALU.is_le).then_inc(s["reached_s"], 1)
                av = attr_rows[0:n, :].rearrange("c (p k f) -> c p k f", k=C, f=EF)
                nc.vector.tensor_copy(attr_p[0:n, :, :, 0, 0:EF], av).then_inc(s["a_hi"], 1)
                dve.wait_ge(s["chg_made"], g + 1)
                nc.vector.tensor_copy(rec[0:n, 0:P - 1, LAST:LAST + C], ch)
                nc.vector.memset(rec[0:n, P - 1, LAST:LAST + C], 1.0)
                nc.vector.memset(start_rows[0:n, :, 0:1], -BIG)
                nc.vector.tensor_scalar(start_rows[0:n, :, 1:P].rearrange("c k p -> c p k"), ch, -BIG, None, ALU.mult).then_inc(s["starts_made"], 1)
                dve.wait_ge(s["reached_s"], g + 1)
                nc.vector.tensor_reduce(chunk_tile[0:n, g:g + 1], reached[0:n, :], AX.X, ALU.add).then_inc(s["ctile_s"], 1)
                dve.wait_ge(s["ctile_s"], g + 1)
                if g == 0:
                    nc.vector.memset(chunk_tile[0:1, 0:1], 0.0).then_inc(s["cfix_s"], 1)
                    dve.wait_ge(s["cfix_s"], 1)
                nc.vector.tensor_tensor(chunk_start[0:n, g:g + 1], chunk_tile[0:n, g:g + 1], chunk_no[0:n, g:g + 1], ALU.add).then_inc(s["cstart_s"], 1)
                dve.wait_ge(s["a_hi"], g + 1)
                nc.vector.tensor_tensor(av, av, attr_p[0:n, :, :, 0, 0:EF], ALU.subtract).then_inc(s["a_left"], 1)
                dve.wait_ge(s["cstart_s"], g + 1)
                nc.vector.tensor_scalar(started[0:n, g, :], steps_at[0:n, :], chunk_start[0:n, g:g + 1], None, ALU.is_ge).then_inc(s["started_at"], 1)
                dve.wait_ge(s["a_left"], g + 1)
                nc.vector.tensor_copy(attr_p[0:n, :, :, 1, 0:EF], av).then_inc(s["a_mid"], 1)
                dve.wait_ge(s["a_mid"], g + 1)
                dve.wait_ge(s["rec_const"], 3)
                nc.vector.tensor_tensor(attr_p[0:n, :, :, 2, 0:EF], av, attr_p[0:n, :, :, 1, 0:EF], ALU.subtract).then_inc(s["rec_made"], 1)
                if g == 0:
                    dve.wait_ge(s["rec_made"], 1)
                    nc.vector.memset(dst_rows[:, :], PAD_DST)
                    nc.vector.memset(src_rows[:, :], 0)
                    nc.vector.memset(attr_rows[:, :], 0.0).then_inc(s["row_pad"], 1)
            dve.wait_ge(s["counted"], len(GROUPS))
            nc.vector.tensor_scalar(step_c[:, :], p_s[:, :], -1.0, None, ALU.add).then_inc(s["stepc_s"], 1)
            dve.wait_ge(s["stepc_s"], 1)
            nc.vector.tensor_tensor(step_t[:, :], steps_at[:, :], step_c[:, :], ALU.subtract).then_inc(s["stept_s"], 1)
            nc.vector.tensor_copy(keep["step_chunk"][:, :], step_c[0:1, :]).then_inc(s["tables_s"], 1)
            dve.wait_ge(s["stept_s"], 1)
            nc.vector.tensor_copy(keep["step_tile"][:, :], step_t[0:1, :]).then_inc(s["tables_s"], 1)
            nc.vector.tensor_scalar(keep["tile_base"][:, :], step_t[:, :], float(P), None, ALU.mult).then_inc(s["tables_s"], 1)
            dve.wait_ge(s["tables_s"], 3)
            dve.wait_ge(s["zero_acc"], 2)


RING = 4
PAIRS = C // 2


class Step:

    def __init__(self, s, slot, turn):
        self.s, self.slot, self.turn = s, slot, turn
        self.parity = slot % 2

    def next(self):
        wraps = self.slot == RING - 1
        return Step(self.s + 1, (self.slot + 1) % RING, self.turn + 1 if wraps else self.turn)

    def prev(self):
        wraps = self.slot == 0
        return Step(self.s - 1, (self.slot - 1) % RING, self.turn - 1 if wraps else self.turn)

    def column(self, ap):
        return ap[:, self.s:self.s + 1] if isinstance(self.s, int) else ap[:, bass.ds(self.s, 1)]

    def since(self, n):
        return not isinstance(self.s, int) or self.s >= n


def edge_loop(nc, scr, keep):
    with Scope(nc) as m:
        rec = m.sb("rec_in", [P, RING, REC])
        rec_i = rec[:, :, :].bitcast(I32)
        rec_b = rec[:, :, :].bitcast(BF16)
        starts = m.sb("starts_in", [C * H, RING, P])
        node = m.sb("node_in", [P, RING, 3 * PART], BF16)
        src = m.sb("src_in", [P, RING, C, ROW])
        local = m.sb("local", [P, 2, C])
        hot = m.sb("hot", [P, RING, C, P])
        hotT = m.sb("hotT", [P, 2, C * P], BF16)
        attrT = m.sb("attrT", [KE, 2, C * P], BF16)
        enc = m.sb("enc", [P, 2, 2 * D])
        prod = m.sb("prod", [P, C, D])
        dots = m.sb("dots", [P, 2, C * H])
        with_dst = m.sb("with_dst", [P, C * H])
        with_src = m.sb("with_src", [P, C * H])
        score = m.sb("score", [P, P])
        running = m.sb("running", [P, P])
        lasts = m.sb("lasts", [P, C, H + 1])
        absent = m.sb("absent", [P, C])
        masked = m.sb("masked", [P, C, H])
        chunk_top = m.sb("chunk_top", [P, H])
        new_top = m.sb("new_top", [P, H])
        drop = m.sb("drop", [P, H])
        keep_by = m.sb("keep_by", [P, 2, H])
        top_left = m.sb("top_left", [P, H])
        top_p = m.sb("top_p", [P, 3, H], BF16)
        below = m.sb("below", [P, C * H])
        capped = m.sb("capped", [P, C * H])
        weight = m.sb("weight", [P, C * H])
        weighted = m.sb("weighted", [P, C, ROW])
        scaled = m.sb("scaled", [P, ROW])

        p_enc = [m.ps(f"p_enc{i}", [P, 2 * D]) for i in range(2)]
        p_dst = [m.ps(f"p_dst{i}", [P, 2 * D]) for i in range(2)]
        p_turn = m.ps("p_turn", [P, 4, P])
        p_chain = m.ps("p_chain", [P, 512])
        p_score = m.ps("p_score", [P, 2, C * H])
        p_sum = m.ps("p_sum", [P, ROW])
        p_scoreT, p_back = p_chain[:, 0:P], p_chain[:, P:2 * P]
        p_lasts = p_back[:, 0:C * H]
        p_top = p_chain[:, 256:256 + C * (H + 1)].rearrange("p (k h) -> p k h", k=C)
        p_ref = p_chain[:, 384:384 + C * H]

        s_loaded = [m.sem(f"s_loaded{i}") for i in range(RING)]
        s_gathered = [m.sem(f"s_gathered{i}") for i in range(RING)]
        names = """gathering zeros local hot attr_turned attr_moved hot_turned hot_moved enc dst_picked relu prod dots with_dst with_src score
            scoreT running lasts_back lasts chunk_tops absent masked chunk_top new_top drop top_hi top_left top_mid
            top_parts top_kept kept refs below capped weight weight_row weighted sums scaled merged""".split()
        s = {n: m.sem("s_" + n) for n in names}

        block = m.enter_context(nc.Block())

        def loop(engine, body, first, last):
            def straight(k):
                return Step(k, k % RING, k // RING)

            first()
            for k in range(1, RING):
                body(straight(k))
            turns = (STEPS - 1 - RING) // RING
            with engine.Fori(0, turns) as i:
                for u in range(RING):
                    body(Step(i * RING + RING + u, u, i + 1))
            for k in range((turns + 1) * RING, STEPS - 1):
                body(straight(k))
            last(straight(STEPS - 1))

        first_step = Step(0, 0, 0)

        @block.sync
        def _(sp):
            def load(q):
                chunk = nc.sync.value_load(q.column(keep["step_chunk"]), min_val=0, max_val=NC - 1)
                tile = nc.sync.value_load(q.column(keep["step_tile"]), min_val=0, max_val=TILES - 1)
                if q.since(RING):
                    sp.wait_ge(s["refs"], q.s - RING + 1)
                sp.dma_start(rec[:, q.slot, :], block_of(scr["edges"], chunk)).then_inc(s_loaded[q.slot], 16)
                sp.dma_start(node[:, q.slot, :], block_of(scr["parts"], tile)).then_inc(s_loaded[q.slot], 16)
                sp.dma_start(starts[:, q.slot, :], block_of(scr["starts"], chunk)).then_inc(s_loaded[q.slot], 16)

            loop(nc.sync, load, lambda: load(first_step), load)

        @block.gpsimd
        def _(pool):
            def gather(q):
                if q.since(RING):
                    pool.wait_ge(s["weighted"], 2 * (q.s - RING + 1))
                pool.wait_ge(s_loaded[q.slot], 48 * (q.turn + 1))
                nc.gpsimd.sem_inc(s["gathering"], 1)
                for k in range(C):
                    pool.indirect_dma_start(src[:, q.slot, k, :], None, scr["rows"],
                                            bass.IndirectOffsetOnAxis(ap=rec_i[:, q.slot, SRC + k:SRC + k + 1], axis=0)
                                            ).then_inc(s_gathered[q.slot], 16)

            loop(nc.gpsimd, gather, lambda: gather(first_step), gather)

        @block.tensor
        def _(pe):
            def turn_edges(q, half):
                b = q.parity
                n = 2 * q.s + half
                ks = range(4 * half, 4 * half + 4)
                if half == 0:
                    pe.wait_ge(s_loaded[q.slot], 48 * (q.turn + 1))
                if q.since(1) or half:
                    pe.wait_ge(s["hot_moved"], n)
                for j, k in enumerate(ks):
                    rows = rec_b[:, q.slot, 2 * ATTR + KE * k:2 * ATTR + KE * (k + 1)]
                    last = nc.tensor.matmul(p_turn[0:KE, j, :], rows, keep["identb"][:, :], start=True, stop=True)
                last.then_inc(s["attr_turned"], 1)
                pe.wait_ge(s["hot"], q.s + 1)
                pe.wait_ge(s["attr_moved"], n + 1)
                for j, k in enumerate(ks):
                    last = nc.tensor.transpose(p_turn[:, j, :], hot[:, q.slot, k, :], keep["ident"][:, :])
                last.then_inc(s["hot_turned"], 1)

            def pair(q, r):
                b, n = q.parity, PAIRS * q.s + r
                pe.wait_ge(s["attr_moved"], 2 * q.s + (2 * r) // 4 + 1)
                if q.since(1) or r >= 2:
                    pe.wait_ge(s["relu"], n - 1)
                for j in range(2):
                    k = 2 * r + j
                    last = nc.tensor.matmul(p_enc[r % 2][:, j * D:(j + 1) * D], attrT[:, b, k * P:(k + 1) * P],
                                            keep["expander"][:, :], start=True, stop=True)
                last.then_inc(s["enc"], 1)
                pe.wait_ge(s["hot_moved"], 2 * q.s + (2 * r) // 4 + 1)
                if q.since(1) or r >= 2:
                    pe.wait_ge(s["prod"], n - 1)
                for j in range(2):
                    k = 2 * r + j
                    for i in range(3):
                        nc.tensor.matmul(p_dst[r % 2][:, j * D:(j + 1) * D], hotT[:, b, k * P:(k + 1) * P],
                                         node[:, q.slot, i * PART:i * PART + D], start=(i == 0), stop=(i == 2))
                    for i in range(3):
                        last = nc.tensor.matmul(p_score[:, b, k * H:(k + 1) * H], hotT[:, b, k * P:(k + 1) * P],
                                                node[:, q.slot, i * PART + D:(i + 1) * PART], start=(i == 0), stop=(i == 2))
                last.then_inc(s["dst_picked"], 1)

            def turn_scores(q):
                pe.wait_ge(s["score"], q.s + 1)
                if q.since(1):
                    pe.wait_ge(s["below"], q.s)
                nc.tensor.transpose(p_scoreT, score[:, :], keep["ident"][:, :]).then_inc(s["scoreT"], 1)

            def turn_back(q):
                pe.wait_ge(s["running"], q.s + 1)
                nc.tensor.transpose(p_back, running[:, :], keep["ident"][:, :]).then_inc(s["lasts_back"], 1)

            def tops(q):
                pe.wait_ge(s["lasts"], q.s + 1)
                for k in range(C):
                    last = nc.tensor.matmul(p_top[:, k, :], hot[:, q.slot, k, :], lasts[:, k, :], start=True, stop=True)
                last.then_inc(s["chunk_tops"], 1)

            def refs(q):
                b = q.parity
                pe.wait_ge(s["top_parts"], q.s + 1)
                for k in range(C):
                    for i in range(3):
                        last = nc.tensor.matmul(p_ref[:, k * H:(k + 1) * H], hotT[:, b, k * P:(k + 1) * P], top_p[:, i, :],
                                                start=(i == 0), stop=(i == 2))
                last.then_inc(s["refs"], 1)

            def sums(q, half):
                pe.wait_ge(s["weight_row"], q.s + 1)
                pe.wait_ge(s["weighted"], 2 * q.s + half + 1)
                if half == 0 and q.since(1):
                    pe.wait_ge(s["merged"], q.s)
                for k in range(4 * half, 4 * half + 4):
                    last = nc.tensor.matmul(p_sum[:, :], hot[:, q.slot, k, :], weighted[:, k, :], start=(k == 0), stop=(k == C - 1))
                if half:
                    last.then_inc(s["sums"], 1)

            def first():
                for half in range(2):
                    turn_edges(first_step, half)
                for r in range(PAIRS):
                    pair(first_step, r)
                body(first_step)

            def body(q):
                n = q.next()
                turn_scores(q)
                turn_edges(n, 0)
                turn_edges(n, 1)
                pair(n, 0)
                turn_back(q)
                pair(n, 1)
                if q.since(1):
                    sums(q.prev(), 0)
                tops(q)
                pair(n, 2)
                if q.since(1):
                    sums(q.prev(), 1)
                refs(q)
                pair(n, 3)

            def last(q):
                turn_scores(q)
                sums(q.prev(), 0)
                sums(q.prev(), 1)
                turn_back(q)
                tops(q)
                refs(q)
                sums(q, 0)
                sums(q, 1)

            loop(nc.tensor, body, first, last)

        @block.scalar
        def _(act):
            def move_turned(q, half):
                b, n = q.parity, 2 * q.s + half
                cols = slice(half * 4 * P, (half + 1) * 4 * P)
                act.wait_ge(s["attr_turned"], n + 1)
                if q.since(2):
                    act.wait_ge(s["refs"], q.s - 1)
                    act.wait_ge(s["enc"], PAIRS * (q.s - 1))
                nc.scalar.copy(attrT[:, b, cols], p_turn[0:KE, :, :].rearrange("p j n -> p (j n)")).then_inc(s["attr_moved"], 1)
                act.wait_ge(s["hot_turned"], n + 1)
                nc.scalar.copy(hotT[:, b, cols], p_turn[:, :, :].rearrange("p j n -> p (j n)")).then_inc(s["hot_moved"], 1)

            def relu(q, r):
                n = PAIRS * q.s + r
                act.wait_ge(s["enc"], n + 1)
                if q.since(1) or r >= 2:
                    act.wait_ge(s["prod"], n - 1)
                nc.scalar.activation(enc[:, r % 2, :], p_enc[r % 2][:, :], ACT.Relu).then_inc(s["relu"], 1)

            def rescale(q):
                act.wait_ge(s["drop"], q.s + 1)
                nc.scalar.activation(keep_by[:, q.parity, :], drop[:, :], ACT.Exp).then_inc(s["kept"], 1)

            def weights(q):
                act.wait_ge(s["capped"], q.s + 1)
                if q.since(1):
                    act.wait_ge(s["weighted"], 2 * q.s)
                nc.scalar.activation(weight[:, :], capped[:, :], ACT.Exp).then_inc(s["weight"], 1)
                if q.since(1):
                    act.wait_ge(s["sums"], q.s)
                nc.scalar.activation(weighted[:, :, :].rearrange("p k (h d) -> p k h d", h=H)[:, :, :, HD],
                                     capped[:, :].rearrange("p (k h) -> p k h", k=C), ACT.Exp).then_inc(s["weight_row"], 1)

            def first():
                for half in range(2):
                    move_turned(first_step, half)
                for r in range(PAIRS):
                    relu(first_step, r)
                body(first_step)

            def body(q):
                n = q.next()
                move_turned(n, 0)
                move_turned(n, 1)
                relu(n, 0)
                relu(n, 1)
                rescale(q)
                relu(n, 2)
                weights(q)
                relu(n, 3)

            def last(q):
                rescale(q)
                weights(q)

            loop(nc.scalar, body, first, last)

        @block.vector
        def _(dve):
            def make_hot(q):
                dve.wait_ge(s_loaded[q.slot], 48 * (q.turn + 1))
                nc.vector.tensor_scalar(local[:, q.parity, :], rec[:, q.slot, DST:DST + C], q.column(keep["tile_base"]), None,
                                        ALU.subtract).then_inc(s["local"], 1)
                if q.since(RING):
                    dve.wait_ge(s["sums"], q.s - RING + 1)
                dve.wait_ge(s["local"], q.s + 1)
                for k in range(C):
                    last = nc.vector.tensor_scalar(hot[:, q.slot, k, :], keep["node_at"][:, :], local[:, q.parity, k:k + 1], None, ALU.is_equal)
                last.then_inc(s["hot"], 1)

            def product(q, r):
                n = PAIRS * q.s + r
                dve.wait_ge(s["relu"], n + 1)
                dve.wait_ge(s["dst_picked"], n + 1)
                if q.since(1):
                    dve.wait_ge(s["dots"], q.s)
                nc.vector.tensor_tensor(prod[:, 2 * r:2 * r + 2, :].rearrange("p k n -> p (k n)"), enc[:, r % 2, :],
                                        p_dst[r % 2][:, :], ALU.mult).then_inc(s["prod"], 1)

            def sum_heads(q):
                dve.wait_ge(s["prod"], PAIRS * (q.s + 1))
                nc.vector.tensor_reduce(dots[:, q.parity, :], prod[:, :, :].rearrange("p k (h d) -> p (k h) d", h=H), AX.X,
                                        ALU.add).then_inc(s["dots"], 1)

            def scores(q):
                b = q.parity
                dve.wait_ge(s["dots"], q.s + 1)
                nc.vector.tensor_tensor(with_dst[:, :], dots[:, b, :], p_score[:, b, :], ALU.add).then_inc(s["with_dst"], 1)
                dve.wait_ge(s["with_dst"], q.s + 1)
                dve.wait_ge(s_gathered[q.slot], 16 * C * (q.turn + 1))
                nc.vector.tensor_tensor(with_src[:, :].rearrange("p (k h) -> p k h", k=C), with_dst[:, :].rearrange("p (k h) -> p k h", k=C),
                                        src[:, q.slot, :, :].rearrange("p k (h d) -> p k h d", h=H)[:, :, :, HD], ALU.add).then_inc(s["with_src"], 1)
                dve.wait_ge(s["with_src"], q.s + 1)
                nc.vector.scalar_tensor_tensor(score[:, 0:C * H], with_src[:, :], 0.2, with_src[:, :], ALU.mult, ALU.max).then_inc(s["score"], 1)

            def scan(q):
                dve.wait_ge(s["scoreT"], q.s + 1)
                nc.vector.tensor_tensor_scan(running[0:C * H, :], starts[:, q.slot, :], p_scoreT[0:C * H, :], -BIG, ALU.add, ALU.max).then_inc(s["running"], 1)

            def mask_lasts(q):
                last_v = rec[:, q.slot, LAST:LAST + C]
                nc.vector.tensor_copy(lasts[:, :, H], last_v)
                dve.wait_ge(s["lasts_back"], q.s + 1)
                nc.vector.tensor_tensor(lasts[:, :, 0:H], p_lasts.rearrange("p (k h) -> p k h", k=C),
                                        spread(last_v, H), ALU.mult).then_inc(s["lasts"], 1)

            def update_top(q):
                top = at(keep["top"], load_tile(q))
                dve.wait_ge(s["chunk_tops"], q.s + 1)
                nc.vector.tensor_scalar(absent[:, :], p_top[:, :, H], BIG, -BIG, ALU.mult, ALU.add).then_inc(s["absent"], 1)
                dve.wait_ge(s["absent"], q.s + 1)
                nc.vector.tensor_tensor(masked[:, :, :], p_top[:, :, 0:H], spread(absent[:, :], H), ALU.add).then_inc(s["masked"], 1)
                dve.wait_ge(s["masked"], q.s + 1)
                nc.vector.tensor_reduce(chunk_top[:, :], masked[:, :, :].rearrange("p k h -> p h k"), AX.X, ALU.max).then_inc(s["chunk_top"], 1)
                dve.wait_ge(s["chunk_top"], q.s + 1)
                nc.vector.tensor_tensor(new_top[:, :], chunk_top[:, :], top, ALU.max).then_inc(s["new_top"], 1)
                dve.wait_ge(s["new_top"], q.s + 1)
                nc.vector.tensor_copy(top_p[:, 0, :], new_top[:, :]).then_inc(s["top_hi"], 1)
                if q.since(1):
                    dve.wait_ge(s["kept"], q.s)
                nc.vector.tensor_tensor(drop[:, :], top, new_top[:, :], ALU.subtract).then_inc(s["drop"], 1)
                dve.wait_ge(s["top_hi"], q.s + 1)
                nc.vector.tensor_tensor(top_left[:, :], new_top[:, :], top_p[:, 0, :], ALU.subtract).then_inc(s["top_left"], 1)
                dve.wait_ge(s["drop"], q.s + 1)
                nc.vector.tensor_scalar(top, new_top[:, :], 1.0, None, ALU.mult).then_inc(s["top_kept"], 1)
                dve.wait_ge(s["top_left"], q.s + 1)
                nc.vector.tensor_copy(top_p[:, 1, :], top_left[:, :]).then_inc(s["top_mid"], 1)
                dve.wait_ge(s["top_mid"], q.s + 1)
                nc.vector.tensor_tensor(top_p[:, 2, :], top_left[:, :], top_p[:, 1, :], ALU.subtract).then_inc(s["top_parts"], 1)

            def exponents(q):
                dve.wait_ge(s["refs"], q.s + 1)
                nc.vector.tensor_tensor(below[:, :], score[:, 0:C * H], p_ref, ALU.subtract).then_inc(s["below"], 1)
                dve.wait_ge(s["below"], q.s + 1)
                if q.since(1):
                    dve.wait_ge(s["weight_row"], q.s)
                nc.vector.tensor_scalar(capped[:, :], below[:, :], 0.0, None, ALU.min).then_inc(s["capped"], 1)

            def apply_weights(q):
                dve.wait_ge(s["weight"], q.s + 1)
                if q.since(1):
                    dve.wait_ge(s["sums"], q.s)
                for half in range(2):
                    ks = slice(4 * half, 4 * half + 4)
                    w = weight[:, :].rearrange("p (k h) -> p k h", k=C)[:, ks, :].rearrange("p k h -> p (k h)")
                    nc.vector.tensor_tensor(weighted[:, ks, :].rearrange("p k (h d) -> p (k h) d", h=H)[:, :, 0:HD],
                                            src[:, q.slot, ks, :].rearrange("p k (h d) -> p (k h) d", h=H)[:, :, 0:HD],
                                            spread(w, HD), ALU.mult).then_inc(s["weighted"], 1)

            def merge(q):
                acc = at(keep["acc"], load_tile(q))
                dve.wait_ge(s["kept"], q.s + 1)
                if q.since(1):
                    dve.wait_ge(s["merged"], q.s)
                heads = lambda v: v.rearrange("p (h d) -> p h d", h=H)
                nc.vector.tensor_tensor(heads(scaled[:, :]), heads(acc), spread(keep_by[:, q.parity, :], HD + 1),
                                        ALU.mult).then_inc(s["scaled"], 1)
                dve.wait_ge(s["scaled"], q.s + 1)
                dve.wait_ge(s["sums"], q.s + 1)
                nc.vector.tensor_tensor(acc, scaled[:, :], p_sum[:, :], ALU.add).then_inc(s["merged"], 1)

            def load_tile(q):
                return nc.vector.value_load(q.column(keep["step_tile"]), min_val=0, max_val=TILES - 1)

            def first():
                nc.vector.memset(score[:, :], 0.0).then_inc(s["zeros"], 1)
                nc.vector.memset(running[:, :], 0.0).then_inc(s["zeros"], 1)
                dve.wait_ge(s["zeros"], 2)
                make_hot(first_step)
                for r in range(PAIRS):
                    product(first_step, r)
                sum_heads(first_step)
                body(first_step)

            def body(q):
                n = q.next()
                scores(q)
                make_hot(n)
                scan(q)
                product(n, 0)
                mask_lasts(q)
                product(n, 1)
                update_top(q)
                product(n, 2)
                exponents(q)
                product(n, 3)
                sum_heads(n)
                if q.since(1):
                    merge(q.prev())
                apply_weights(q)

            def last(q):
                scores(q)
                scan(q)
                mask_lasts(q)
                update_top(q)
                exponents(q)
                merge(q.prev())
                apply_weights(q)
                merge(q)
                dve.wait_ge(s["merged"], STEPS)

            loop(nc.vector, body, first, last)


EXP_AT = (3, 17, 24)
INDEX_AT = 22


def epilogue(nc, a, keep, out):
    hidden = FF // P
    blocks = -(-N // (2 * P))
    last_cols = N - (blocks - 1) * 2 * P
    assert last_cols <= P and NT == 2 * blocks and TOPK == 2
    with Scope(nc) as m:
        x1 = m.sb("x1", [P, NT, D])
        moe = keep["acc"][:, :, 0:D]
        x2T = m.sb("x2T", [P, 2, NT * P])
        fresh = m.sb("fresh", [P, 2, D])
        denom = m.sb("denom", [P, NT, H])
        inverse = m.sb("inverse", [P, NT, H])
        bias = m.sb("bias", [P, D])
        gamma = m.sb("gamma", [P, D])
        beta = m.sb("beta", [P, D])
        stats = m.sb("e_stats", [P, NT, 6])
        halves = m.sb("e_halves", [P, 4, NT])
        moments = m.sb("e_moments", [P, NT, 2])
        std = m.sb("e_std", [P, NT])
        rstd = m.sb("e_rstd", [P, NT, 1])
        shift = m.sb("e_shift", [P, NT, 1])
        eps = m.sb("e_eps", [P, 1])
        col_sums = m.sb("col_sums", [P, 2, TILES])
        mean = m.sb("mean", [P, 2])
        total = m.sb("total", [P, 2])
        wr = m.sb("wr", [P, 2, NX])
        r_ = {n: m.sb("r_" + n, [1, w], dt) for n, w, dt in (
            ("br", NX, F32), ("logits", NX, F32), ("top", 1, F32), ("d", NX, F32), ("e", NX, F32), ("sum", 1, F32),
            ("p", NX, F32), ("load", NX, F32), ("q", NX, F32), ("over", NX, F32), ("under", NX, F32),
            ("scale", NX, F32), ("t", NX, F32), ("best", NX, F32), ("index", NX, U32), ("w2", TOPK, F32), ("ones", P, F32))}
        share = m.sb("share", [P, TOPK])
        w1 = m.sb("w1", [P, TOPK, 2, FF])
        w2 = m.sb("w2", [P, TOPK, hidden, D])
        b1 = m.sb("b1", [P, TOPK, hidden])
        b2 = m.sb("b2", [P, TOPK, D])
        b2_mix = m.sb("b2_mix", [P, D])
        act_h = m.sb("act_h", [P, 2, TOPK * hidden, 2 * P])
        normed = m.sb("normed", [P, 2, D])

        p_T = [m.ps(f"p_T{i}", [P, 2, P]) for i in range(2)]
        p_up = [m.ps(f"p_up{i}", [P, 2 * P]) for i in range(4)]
        p_y = [m.ps(f"p_y{i}", [P, D]) for i in range(2)]
        p_r = p_y[0]

        names = """eps cap ones x bias vec x_biased denom inverse gnn x1 stats moments std rstd fresh x2T x2T_moved x2_kept pad
            wr total mean logits  share expert b2a b2_mix w2_scaled x1_beta b2_added up act_h down moe stats2
            moments2 std2 rstd2 mean_r shift normed scaled result small stored expo shared""".split()
        s = {n: m.sem("e_" + n) for n in names}
        heads = lambda v: v.rearrange("p (h d) -> p h d", h=H)
        block = m.enter_context(nc.Block())

        @block.sync
        def _(sp):
            full = (TILES - 1) * P
            sp.dma_start(x1[:, 0:TILES - 1, :], a["x"][0:full, :].rearrange("(t p) n -> p t n", p=P)).then_inc(s["x"], 16)
            sp.wait_ge(s["pad"], 1)
            sp.dma_start(x1[0:LASTROWS, TILES - 1, :], a["x"][full:N, :]).then_inc(s["x"], 16)
            sp.dma_start(bias[:, :], a["gnn_bias"].partition_broadcast(P)).then_inc(s["bias"], 16)
            sp.dma_start(gamma[:, :], a["gamma"].partition_broadcast(P)).then_inc(s["vec"], 16)
            sp.dma_start(beta[:, :], a["beta"].partition_broadcast(P)).then_inc(s["vec"], 16)
            sp.dma_start(wr[:, :, :], a["Wr"].rearrange("(c p) n -> p c n", p=P)).then_inc(s["wr"], 16)
            sp.dma_start(r_["br"][:, :], a["br"].rearrange("(o n) -> o n", o=1)).then_inc(s["wr"], 16)
            sp.wait_ge(s["small"], INDEX_AT)
            for k in range(TOPK):
                e = nc.sync.value_load(r_["index"][0:1, k:k + 1], min_val=0, max_val=NX - 1)
                one = lambda v: v[bass.ds(e, 1)]
                sp.dma_start(w1[:, k, :, :], one(a["W1"]).rearrange("o (c p) f -> p (o c) f", p=P)).then_inc(s["expert"], 16)
                sp.dma_start(w2[:, k, :, :], one(a["W2"]).rearrange("o (c p) f -> p (o c) f", p=P)).then_inc(s["expert"], 16)
                sp.dma_start(b1[:, k, :], one(a["b1"]).rearrange("o (c p) -> p (o c)", p=P), allow_slow_non_contiguous=True).then_inc(s["expert"], 16)
                sp.dma_start(b2[:, k, :], one(a["b2"]).rearrange("o n -> (o n)").partition_broadcast(P)).then_inc(s["expert"], 16)
            def store(t, rows=P):
                dst = out[t * P:t * P + rows, :] if isinstance(t, int) else out[bass.ds(t * P, P), :]
                sp.wait_ge(s["result"], t + 1)
                sp.dma_start(dst, at(x1, t)[0:rows, :]).then_inc(s["stored"], 16)

            with nc.sync.Fori(0, TILES - 1) as t:
                store(t)
            store(TILES - 1, LASTROWS)
            sp.wait_ge(s["stored"], 16 * TILES)

        @block.gpsimd
        def _(pool):
            nc.gpsimd.memset(x1[:, TILES - 1:NT, :], 0.0).then_inc(s["pad"], 1)
            nc.gpsimd.memset(x2T[:, :, (TILES - 1) * P:], 0.0).then_inc(s["pad"], 1)
            nc.gpsimd.memset(eps[:, :], LN_EPS).then_inc(s["eps"], 1)
            nc.gpsimd.memset(r_["ones"][:, :], 1.0).then_inc(s["ones"], 1)
            pool.wait_ge(s["x"], 32)
            pool.wait_ge(s["bias"], 16)
            with nc.gpsimd.Fori(0, NT) as t:
                nc.gpsimd.tensor_tensor(at(x1, t), at(x1, t), bias[:, :], ALU.add).then_inc(s["x_biased"], 1)
            pool.wait_ge(s["b2_mix"], 1)
            pool.wait_ge(s["x2_kept"], NT)
            pool.wait_ge(s["fresh"], NT)
            pool.wait_ge(s["vec"], 32)
            with nc.gpsimd.Fori(0, NT) as t:
                nc.gpsimd.tensor_tensor(at(moe, t), at(moe, t), b2_mix[:, :], ALU.add).then_inc(s["b2_added"], 1)
                nc.gpsimd.tensor_tensor(at(x1, t), at(x1, t), beta[:, :], ALU.add).then_inc(s["x1_beta"], 1)

        @block.tensor
        def _(pe):
            def turn(t, b):
                pe.wait_ge(s["fresh"], t + 1)
                if not (isinstance(t, int) and t < 2):
                    pe.wait_ge(s["x2T_moved"], 2 * (t - 1))
                for i in range(2):
                    last = nc.tensor.transpose(p_T[b][:, i, :], fresh[:, b, i * P:(i + 1) * P], keep["ident"][:, :])
                last.then_inc(s["x2T"], 1)

            turn(0, 0)
            turn(1, 1)
            with nc.tensor.Fori(0, (TILES - 3) // 2) as i:
                for u in range(2):
                    turn(2 * i + 2 + u, u)
            turn(TILES - 1, 0)
            pe.wait_ge(s["mean"], 1)
            pe.wait_ge(s["wr"], 32)
            for i in range(2):
                last = nc.tensor.matmul(p_r[0:1, 0:NX], mean[:, i:i + 1], wr[:, i, :], start=(i == 0), stop=(i == 1))
            last.then_inc(s["logits"], 1)
            pe.wait_ge(s["ones"], 1)
            pe.wait_ge(s["small"], EXP_AT[2] + 3)
            nc.tensor.matmul(p_r[:, 64:64 + TOPK], r_["ones"][:, :], r_["w2"][:, :], start=True, stop=True).then_inc(s["share"], 1)

            def up(j, cols=2 * P):
                for n in range(TOPK * hidden):
                    k, f = n // hidden, n % hidden
                    if not (isinstance(j, int) and j == 0 and n < 4):
                        pe.wait_ge(s["act_h"], TOPK * hidden * j + n - 3)
                    for i in range(2):
                        x = x2T[:, i, j * 2 * P:j * 2 * P + cols] if isinstance(j, int) else x2T[:, i, bass.ds(j * 2 * P, cols)]
                        last = nc.tensor.matmul(p_up[n % 4][:, 0:cols], w1[:, k, i, f * P:(f + 1) * P], x, start=(i == 0), stop=(i == 1))
                    last.then_inc(s["up"], 1)

            def down(j, b, tiles=2):
                for u in range(tiles):
                    pe.wait_ge(s["act_h"], TOPK * hidden * (j + 1))
                    if not (isinstance(j, int) and j == 0):
                        pe.wait_ge(s["moe"], 2 * j + u - 1)
                    for n in range(TOPK * hidden):
                        k, f = n // hidden, n % hidden
                        last = nc.tensor.matmul(p_y[u][:, :], act_h[:, b, n, u * P:(u + 1) * P], w2[:, k, f, :], start=(n == 0), stop=(n == TOPK * hidden - 1))
                    last.then_inc(s["down"], 1)

            pe.wait_ge(s["expert"], 64 * TOPK)
            up(0)
            up(1)
            pe.wait_ge(s["w2_scaled"], TOPK)
            down(0, 0)
            with nc.tensor.Fori(0, (blocks - 3) // 2) as i:
                for u in range(2):
                    up(2 * i + 2 + u)
                    down(2 * i + 1 + u, 1 - u)
            up(blocks - 1, last_cols)
            down(blocks - 2, 1)
            down(blocks - 1, 0, 1)

        @block.scalar
        def _(act):
            act.wait_ge(s["eps"], 1)
            act.wait_ge(s["moments"], 6)
            nc.scalar.activation(std[:, :], moments[:, :, 1], ACT.Sqrt, bias=eps[:, 0:1]).then_inc(s["std"], 1)

            def move(t, b, cols=P):
                act.wait_ge(s["x2T"], t + 1)
                for i in range(2):
                    to = x2T[:, i, t * P:t * P + cols] if isinstance(t, int) else x2T[:, i, bass.ds(t * P, P)]
                    total_at = col_sums[:, i, t:t + 1] if isinstance(t, int) else col_sums[:, i, bass.ds(t, 1)]
                    nc.scalar.activation(to, p_T[b][:, i, 0:cols], ACT.Copy, accum_out=total_at).then_inc(s["x2T_moved"], 1)
                nc.scalar.copy(at(moe, t), fresh[:, b, :]).then_inc(s["x2_kept"], 1)

            act.wait_ge(s["pad"], 2)
            with nc.scalar.Fori(0, (TILES - 1) // 2) as i:
                for u in range(2):
                    move(2 * i + u, u)
            move(TILES - 1, 0, LASTROWS)
            act.wait_ge(s["fresh"], NT)
            nc.scalar.copy(moe[:, NT - 1, :], fresh[:, 1, :]).then_inc(s["x2_kept"], 1)
            for n in range(3):
                act.wait_ge(s["small"], EXP_AT[n])
                w = NX if n < 2 else TOPK
                nc.scalar.activation(r_["e"][:, 0:w], r_["d"][:, 0:w], ACT.Exp).then_inc(s["expo"], 1)

            def gelu(j, b, cols=2 * P):
                for n in range(TOPK * hidden):
                    act.wait_ge(s["up"], TOPK * hidden * j + n + 1)
                    if n == 0 and not (isinstance(j, int) and j < 2):
                        act.wait_ge(s["down"], 2 * (j - 1))
                    k, f = n // hidden, n % hidden
                    nc.scalar.activation(act_h[:, b, n, 0:cols], p_up[n % 4][:, 0:cols], ACT.Gelu,
                                         bias=b1[:, k, f:f + 1]).then_inc(s["act_h"], 1)

            act.wait_ge(s["expert"], 64 * TOPK)
            gelu(0, 0)
            gelu(1, 1)
            with nc.scalar.Fori(0, (blocks - 3) // 2) as i:
                for u in range(2):
                    gelu(2 * i + 2 + u, u)
            gelu(blocks - 1, 0, last_cols)

            act.wait_ge(s["moments2"], 6)
            nc.scalar.activation(std[:, 0:TILES], moments[:, 0:TILES, 1], ACT.Sqrt, bias=eps[:, 0:1]).then_inc(s["std2"], 1)
            act.wait_ge(s["shift"], 1)

            def normalize(t, b):
                if not (isinstance(t, int) and t < 2):
                    act.wait_ge(s["scaled"], t - 1)
                nc.scalar.activation(normed[:, b, :], at(moe, t), ACT.Identity, bias=at(shift, t), scale=at(rstd, t)).then_inc(s["normed"], 1)

            normalize(0, 0)
            normalize(1, 1)
            with nc.scalar.Fori(0, (TILES - 3) // 2) as i:
                for u in range(2):
                    normalize(2 * i + 2 + u, u)
            normalize(TILES - 1, 0)

        @block.vector
        def _(dve):
            nc.vector.tensor_scalar(denom[:, :, :], keep["acc"][:, :, :].rearrange("p t (h d) -> p t h d", h=H)[:, :, :, HD], 1e-10, None, ALU.max).then_inc(s["denom"], 1)
            dve.wait_ge(s["denom"], 1)
            nc.vector.reciprocal(inverse[:, :, :], denom[:, :, :]).then_inc(s["inverse"], 1)
            dve.wait_ge(s["inverse"], 1)

            def attend(t, b, first=False):
                if not first:
                    dve.wait_ge(s["x1"], t - 1)
                nc.vector.tensor_tensor(heads(fresh[:, b, :]), heads(at(keep["acc"], t))[:, :, 0:HD], spread(at(inverse, t), HD), ALU.mult).then_inc(s["gnn"], 1)

            def add_x(t, b):
                dve.wait_ge(s["gnn"], t + 1)
                dve.wait_ge(s["x_biased"], t + 1)
                nc.vector.tensor_tensor(at(x1, t), at(x1, t), fresh[:, b, :], ALU.add).then_inc(s["x1"], 1)

            def measure(t):
                dve.wait_ge(s["x1"], t + 1)
                nc.vector.bn_stats(at(stats, t), at(x1, t)).then_inc(s["stats"], 1)

            attend(0, 0, True)
            attend(1, 1, True)
            add_x(0, 0)
            with nc.vector.Fori(0, (NT - 2) // 2) as i:
                for u in range(2):
                    add_x(2 * i + 1 + u, 1 - u)
                    attend(2 * i + 2 + u, u)
                    measure(2 * i + u)
            add_x(NT - 1, 1)
            measure(NT - 2)
            measure(NT - 1)
            dve.wait_ge(s["stats"], NT)
            merge_moments(nc, dve, stats, halves, moments, s["moments"])
            dve.wait_ge(s["std"], 1)
            nc.vector.reciprocal(rstd[:, :, 0], std[:, :]).then_inc(s["rstd"], 1)
            dve.wait_ge(s["rstd"], 1)

            def normalize(t, b):
                if not (isinstance(t, int) and t < 2):
                    dve.wait_ge(s["x2T"], t - 1)
                    dve.wait_ge(s["x2_kept"], t - 1)
                mean_t = moments[:, t, 0:1] if isinstance(t, int) else moments[:, bass.ds(t, 1), 0]
                nc.vector.tensor_scalar(fresh[:, b, :], at(x1, t), mean_t, at(rstd, t), ALU.subtract, ALU.mult).then_inc(s["fresh"], 1)

            normalize(0, 0)
            normalize(1, 1)
            with nc.vector.Fori(0, (NT - 4) // 2) as i:
                for u in range(2):
                    normalize(2 * i + 2 + u, u)
            normalize(NT - 2, 0)
            dve.wait_ge(s["x2_kept"], NT - 2)
            dve.wait_ge(s["x2T"], NT - 2)
            nc.vector.tensor_scalar(fresh[:, 1, :], x1[:, NT - 1, :], moments[:, NT - 1, 0:1], rstd[:, NT - 1, :], ALU.subtract, ALU.mult).then_inc(s["fresh"], 1)

            dve.wait_ge(s["x2T_moved"], 2 * TILES)
            nc.vector.tensor_reduce(total[:, :], col_sums[:, :, :], AX.X, ALU.add).then_inc(s["total"], 1)
            dve.wait_ge(s["total"], 1)
            nc.vector.tensor_scalar(mean[:, :], total[:, :], 1.0 / N, None, ALU.mult).then_inc(s["mean"], 1)
            dve.wait_ge(s["logits"], 1)
            dve.wait_ge(s["wr"], 32)
            count = [0]

            def link(ins):
                count[0] += 1
                ins.then_inc(s["small"], 1)
                dve.wait_ge(s["small"], count[0])

            def softmax(to, of, w, n):
                link(nc.vector.tensor_reduce(r_["top"][:, :], of, AX.X, ALU.max))
                link(nc.vector.tensor_scalar(r_["d"][:, 0:w], of, r_["top"][:, 0:1], None, ALU.subtract))
                assert count[0] == EXP_AT[n]
                dve.wait_ge(s["expo"], n + 1)
                link(nc.vector.tensor_reduce(r_["sum"][:, :], r_["e"][:, 0:w], AX.X, ALU.add))
                link(nc.vector.reciprocal(r_["sum"][:, :], r_["sum"][:, :]))
                link(nc.vector.tensor_scalar(to, r_["e"][:, 0:w], r_["sum"][:, 0:1], None, ALU.mult))

            link(nc.vector.tensor_tensor(r_["logits"][:, :], p_r[0:1, 0:NX], r_["br"][:, :], ALU.add))
            softmax(r_["p"][:, :], r_["logits"][:, :], NX, 0)
            link(nc.vector.tensor_scalar(r_["load"][:, :], r_["p"][:, :], float(N), None, ALU.mult))
            link(nc.vector.reciprocal(r_["q"][:, :], r_["load"][:, :]))
            link(nc.vector.tensor_scalar(r_["q"][:, :], r_["q"][:, :], CAPACITY, None, ALU.mult))
            link(nc.vector.tensor_scalar(r_["over"][:, :], r_["load"][:, :], CAPACITY, None, ALU.is_gt))
            link(nc.vector.tensor_scalar(r_["under"][:, :], r_["load"][:, :], CAPACITY, None, ALU.is_le))
            link(nc.vector.tensor_scalar(r_["q"][:, :], r_["q"][:, :], 1.0, None, ALU.min))
            link(nc.vector.tensor_tensor(r_["q"][:, :], r_["q"][:, :], r_["over"][:, :], ALU.mult))
            link(nc.vector.tensor_tensor(r_["scale"][:, :], r_["q"][:, :], r_["under"][:, :], ALU.add))
            link(nc.vector.tensor_tensor(r_["t"][:, :], r_["p"][:, :], r_["scale"][:, :], ALU.mult))
            softmax(r_["p"][:, :], r_["t"][:, :], NX, 1)
            link(nc.vector.max(r_["best"][:, :], r_["p"][:, :]))
            link(nc.vector.max_index(r_["index"][:, :], r_["best"][:, :], r_["p"][:, :]))
            assert count[0] == INDEX_AT
            softmax(r_["w2"][:, :], r_["best"][:, 0:TOPK], TOPK, 2)
            dve.wait_ge(s["share"], 1)
            nc.vector.tensor_copy(share[:, :], p_r[:, 64:64 + TOPK]).then_inc(s["shared"], 1)
            dve.wait_ge(s["shared"], 1)
            dve.wait_ge(s["expert"], 64 * TOPK)
            for k in range(TOPK):
                nc.vector.tensor_scalar(w2[:, k, :, :], w2[:, k, :, :], share[:, k:k + 1], None, ALU.mult).then_inc(s["w2_scaled"], 1)
            nc.vector.tensor_scalar(b2_mix[:, :], b2[:, 0, :], share[:, 0:1], None, ALU.mult).then_inc(s["b2a"], 1)
            dve.wait_ge(s["b2a"], 1)
            nc.vector.scalar_tensor_tensor(b2_mix[:, :], b2[:, 1, :], share[:, 1:2], b2_mix[:, :], ALU.mult, ALU.add).then_inc(s["b2_mix"], 1)

            def gather_down(t, u):
                dve.wait_ge(s["down"], t + 1)
                dve.wait_ge(s["b2_added"], t + 1)
                nc.vector.tensor_tensor(at(moe, t), at(moe, t), p_y[u][:, :], ALU.add).then_inc(s["moe"], 1)
                dve.wait_ge(s["moe"], t + 1)
                nc.vector.bn_stats(at(stats, t), at(moe, t)).then_inc(s["stats2"], 1)

            with nc.vector.Fori(0, (TILES - 1) // 2) as i:
                for u in range(2):
                    gather_down(2 * i + u, u)
            gather_down(TILES - 1, 0)
            dve.wait_ge(s["stats2"], TILES)
            merge_moments(nc, dve, stats, halves, moments, s["moments2"])
            dve.wait_ge(s["std2"], 1)
            nc.vector.reciprocal(rstd[:, 0:TILES, 0], std[:, 0:TILES]).then_inc(s["rstd2"], 1)
            dve.wait_ge(s["rstd2"], 1)
            nc.vector.scalar_tensor_tensor(shift[:, 0:TILES, 0], moments[:, 0:TILES, 0], -1.0, rstd[:, 0:TILES, 0], ALU.mult, ALU.mult).then_inc(s["shift"], 1)
            dve.wait_ge(s["x1_beta"], NT)
            dve.wait_ge(s["x2_kept"], NT)

            def finish(t, b):
                dve.wait_ge(s["normed"], t + 1)
                if not (isinstance(t, int) and t < 2):
                    dve.wait_ge(s["result"], t - 1)
                nc.vector.tensor_tensor(fresh[:, b, :], normed[:, b, :], gamma[:, :], ALU.mult).then_inc(s["scaled"], 1)
                dve.wait_ge(s["scaled"], t + 1)
                nc.vector.tensor_tensor(at(x1, t), fresh[:, b, :], at(x1, t), ALU.add).then_inc(s["result"], 1)

            finish(0, 0)
            finish(1, 1)
            with nc.vector.Fori(0, (TILES - 3) // 2) as i:
                for u in range(2):
                    finish(2 * i + 2 + u, u)
            finish(TILES - 1, 0)


_INS = {"x": "x", "src": "src", "dst": "dst", "attr": "edge_attr_3", "W": "L0_gnn_W", "a_src": "L0_gnn_a_src",
        "a_dst": "L0_gnn_a_dst", "edge_W": "L0_gnn_edge_W", "edge_b": "L0_gnn_edge_b", "gnn_bias": "L0_gnn_bias",
        "Wr": "L0_ffn_Wr", "br": "L0_ffn_br", "W1": "L0_ffn_W1", "b1": "L0_ffn_b1", "W2": "L0_ffn_W2",
        "b2": "L0_ffn_b2", "gamma": "L0_ffn_gamma", "beta": "L0_ffn_beta"}


def build(nc, a, out):
    def dram(name, shape, dt):
        return nc.dram_tensor(name, shape, dt, kind="Internal").ap()

    scr = dict(rows=dram("node_rows", (NT * P, ROW), F32), parts=dram("node_parts", (NT, P, 3 * PART), BF16),
               edges=dram("edge_records", (NC, P, REC), F32), starts=dram("segment_starts", (NC, C * H, P), F32))
    with Scope(nc) as m:
        keep = dict(
            ident=m.sb("ident", [P, P]), identb=m.sb("identb", [P, P], BF16), node_at=m.sb("node_at", [P, P]),
            expander=m.sb("expander", [3 * KA, D], BF16), step_chunk=m.sb("step_chunk", [1, STEPS], I32),
            step_tile=m.sb("step_tile", [1, STEPS], I32), tile_base=m.sb("tile_base", [P, STEPS]),
            acc=m.sb("acc", [P, NT, ROW]), top=m.sb("top", [P, NT, H]),
        )
        prologue(nc, a, scr, keep)
        edge_loop(nc, scr, keep)
        epilogue(nc, a, keep, out)


def kernel(**inputs):
    import numpy as np
    import concourse.bacc as bacc
    from concourse.bass_utils import run_bass_kernel_spmd

    nc = bacc.Bacc("TRN2", target_bir_lowering=False, num_devices=1)
    arrays, args = {}, {}
    for short, name in _INS.items():
        v = np.ascontiguousarray(inputs[name])
        arrays["in_" + name] = v
        args[short] = nc.dram_tensor("in_" + name, v.shape, mybir.dt.from_np(v.dtype), kind="ExternalInput").ap()
    out = nc.dram_tensor("out_x", (N, D), F32, kind="ExternalOutput").ap()
    build(nc, args, out)
    r = run_bass_kernel_spmd(nc, [arrays], core_ids=[0])
    return r.results[0]["out_x"]
```

```python
from contextlib import ExitStack

import concourse.bass as bass
from concourse import mybir

F32, BF16, I32, U32 = mybir.dt.float32, mybir.dt.bfloat16, mybir.dt.int32, mybir.dt.uint32
ALU, ACT, AX = mybir.AluOpType, mybir.ActivationFunctionType, mybir.AxisListType

P = 128
N, E = 6250, 200000
D, H, HD = 256, 8, 32
EF = 3
FF, NX, TOPK = 512, 8, 2
LN_EPS = 1e-5
CAPACITY = float(-(-N * 5 // (4 * NX)))

C = 8
CHUNK = P * C
NC = -(-E // CHUNK)
FULL = E // CHUNK
REST = E - FULL * CHUNK
TILES = -(-N // P)
STEPS = NC + TILES - 1
NT = TILES + TILES % 2
LASTROWS = N - (TILES - 1) * P
GROUPS = [(g, min(P, NC - g)) for g in range(0, NC, P)]

ROW = H * (HD + 1)
PART = D + H
KA = 12
KE = 3 * KA
REC = C * (3 + KE // 2)
DST, LAST, SRC, ATTR = 0, C, 2 * C, 3 * C
BIG = 1e30
PAD_DST = 1 << 20
assert C == 8 and NC <= 2 * P


def at(ap, t):
    return ap[:, t, :] if isinstance(t, int) else ap[:, bass.ds(t, 1), :].rearrange("p o n -> p (o n)")


def block_of(ap, t):
    return ap[t, :, :] if isinstance(t, int) else ap[bass.ds(t, 1), :, :].rearrange("o p n -> p (o n)")


def merge_moments(nc, dve, stats, halves, moments, made):
    m0, v0, m1, v1 = (stats[:, :, i] for i in (1, 2, 4, 5))
    nc.vector.tensor_tensor(halves[:, 0, :], m0, m1, ALU.add).then_inc(made, 1)
    nc.vector.tensor_tensor(halves[:, 1, :], m0, m1, ALU.subtract).then_inc(made, 1)
    nc.vector.tensor_tensor(halves[:, 2, :], v0, v1, ALU.add).then_inc(made, 1)
    dve.wait_ge(made, 3)
    nc.vector.tensor_scalar(moments[:, :, 0], halves[:, 0, :], 0.5, None, ALU.mult)
    nc.vector.scalar_tensor_tensor(halves[:, 3, :], halves[:, 1, :], 0.25, halves[:, 1, :], ALU.mult, ALU.mult).then_inc(made, 1)
    dve.wait_ge(made, 4)
    nc.vector.scalar_tensor_tensor(moments[:, :, 1], halves[:, 2, :], 1.0 / D, halves[:, 3, :], ALU.mult, ALU.add).then_inc(made, 2)


def spread(ap, n):
    return ap.unsqueeze(ap.ndim).broadcast_to([*ap.shape, n])


class Scope(ExitStack):

    def __init__(self, nc):
        super().__init__()
        self.nc = nc

    def sb(self, name, shape, dt=F32):
        return self.enter_context(self.nc.sbuf_tensor(name, shape, dt))

    def ps(self, name, shape, dt=F32):
        return self.enter_context(self.nc.psum_tensor(name, shape, dt))

    def sem(self, name):
        return self.enter_context(self.nc.semaphore(name))


def prologue(nc, a, scr, keep):
    with Scope(nc) as m:
        x_all = keep["acc"][:, :, 0:D]
        dst_rows = m.sb("dst_rows", [P, CHUNK], I32)
        src_rows = m.sb("src_rows", [P, CHUNK], I32)
        attr_rows = m.sb("attr_rows", [P, CHUNK * EF])
        rec = m.sb("rec", [P, P, REC])
        start_rows = m.sb("start_rows", [P, C, P])
        changed = m.sb("changed", [P, P, C])
        steps_at = m.sb("steps_at", [P, STEPS])
        started = m.sb("started", [P, 2, STEPS])
        tile_edges = m.sb("tile_edges", [P, TILES - 1])
        reached = m.sb("reached", [P, TILES - 1])
        chunk_tile = m.sb("chunk_tile", [P, 2])
        chunk_start = m.sb("chunk_start", [P, 2])
        chunk_no = m.sb("chunk_no", [P, 2])
        step_c = m.sb("step_c", [P, STEPS])
        step_t = m.sb("step_t", [P, STEPS])
        ones = m.sb("ones", [P, P])
        stats = m.sb("stats", [P, NT, 6])
        moments = m.sb("moments", [P, NT, 2])
        halves = m.sb("halves", [P, 4, NT])
        std = m.sb("std", [P, NT])
        rstd = m.sb("rstd", [P, NT, 1])
        eps = m.sb("eps", [P, 1])
        xn = m.sb("xn", [P, 2, D])
        xnT = m.sb("xnT", [P, 2, 2, P])
        w_nat = m.sb("w_nat", [P, 2, D])
        w_ext = m.sb("w_ext", [P, 2, D + 2 * H])
        a_diag = m.sb("a_diag", [P, 2, 2, H])
        a_col = m.sb("a_col", [P, 2, 2])
        out_rows = m.sb("out_rows", [P, 2, ROW])
        dst_score = m.sb("dst_score", [P, 2, H])
        out_parts = m.sb("out_parts", [P, 2, 3 * PART], BF16)
        part_left = m.sb("part_left", [P, PART])
        enc_f = m.sb("enc_f", [KA, D])
        enc_left = m.sb("enc_left", [KA, D])
        enc_p = m.sb("enc_p", [KA, 3, D], BF16)
        p_xT = [m.ps(f"p_xT{i}", [P, 2, P]) for i in range(2)]
        p_h = [m.ps(f"p_h{i}", [P, D + 2 * H]) for i in range(2)]
        p_w = m.ps("p_w", [P, 512])
        p_v = m.ps("p_v", [P, 4 * H])
        p_s = m.ps("p_s", [P, STEPS])

        names = """w_loaded x_loaded enc_loaded zeros_made ones_made consts_made ident_made ident_filled row_pad enc_hi enc_l enc_mid
            enc_parts enc_moved rec_made rec_stored started_at counted starts_made rec_copied diag_zero diag_made wT_made v_made
            wext_made stats_made moments_made std_made rstd_made xn_made xT_made xT_moved h_made rows_made
            hi_made left_made mid_made parts_made dst_made chg_made a_hi a_left a_mid reached_s ctile_s cfix_s cstart_s
            stepc_s stept_s tables_s rec_const zero_acc""".split()
        s = {n: m.sem("s_" + n) for n in names}
        s_edges = [m.sem(f"s_edges_loaded{g}") for g in range(len(GROUPS))]
        s_stored = [m.sem(f"s_tables_stored{i}") for i in range(2)]
        rec_i = rec[:, :, :].bitcast(I32)
        attr_w = rec[:, :, :].bitcast(BF16)[:, :, 2 * ATTR:].rearrange("c p (k j w) -> c p k j w", k=C, j=3)
        attr_p = rec[:, :, :].bitcast(BF16)[:, :, 2 * ATTR:].rearrange("c p (k j i f) -> c p k j i f", k=C, j=3, i=3)[:, :, :, 0, :, :]

        block = m.enter_context(nc.Block())

        def store_records(sp, g):
            c0, n = GROUPS[g]
            sp.wait_ge(s["rec_copied"], 2 * g + 2)
            sp.dma_start(scr["edges"][c0:c0 + n, :, :], rec[0:n, :, :]).then_inc(s["rec_stored"], 16)
            for h in range(H):
                sp.dma_start(scr["starts"][c0:c0 + n, :, :].rearrange("c (k h) p -> c k h p", h=H)[:, :, h, :],
                             start_rows[0:n, :, :]).then_inc(s["rec_stored"], 16)

        @block.sync
        def _(sp):
            sp.dma_start(w_nat[:, :, :], a["W"].rearrange("(c p) n -> p c n", p=P)).then_inc(s["w_loaded"], 16)
            for half in range(2):
                for i, name in enumerate(("a_src", "a_dst")):
                    v = a[name].rearrange("h (d o) -> (h d) o", o=1)[half * P:(half + 1) * P, :]
                    sp.dma_start(a_col[:, half, i:i + 1], v).then_inc(s["w_loaded"], 16)
            sp.wait_ge(s["zeros_made"], 1)
            full = (TILES - 1) * P
            sp.dma_start(x_all[:, 0:TILES - 1, :], a["x"][0:full, :].rearrange("(t p) n -> p t n", p=P)).then_inc(s["x_loaded"], 16)
            sp.dma_start(x_all[0:LASTROWS, TILES - 1, :], a["x"][full:N, :]).then_inc(s["x_loaded"], 16)
            for g, (c0, n) in enumerate(GROUPS):
                if g:
                    sp.wait_ge(s["row_pad"], 1)
                whole = min(n, FULL - c0)
                for rows, name, w in ((dst_rows, "dst", 1), (src_rows, "src", 1), (attr_rows, "attr", EF)):
                    flat = a[name] if w == 1 else a[name].rearrange("e f -> (e f)")
                    sp.dma_start(rows[0:whole, :], flat[c0 * CHUNK * w:(c0 + whole) * CHUNK * w]
                                 .rearrange("(c e) -> c e", c=whole)).then_inc(s_edges[g], 16)
                    if c0 + n > FULL:
                        sp.dma_start(rows[whole:whole + 1, 0:REST * w], flat[FULL * CHUNK * w:E * w]
                                     .rearrange("(c e) -> c e", c=1)).then_inc(s_edges[g], 16)
                if g == 0:
                    continue
                store_records(sp, g - 1)
            store_records(sp, len(GROUPS) - 1)
            sp.wait_ge(s["rec_stored"], 16 * (1 + H) * len(GROUPS))

        @block.gpsimd
        def _(pool):
            nc.gpsimd.memset(x_all[:, TILES - 1:NT, :], 0.0).then_inc(s["zeros_made"], 1)
            nc.gpsimd.memset(keep["ident"][:, :], 0.0).then_inc(s["ident_made"], 1)
            nc.gpsimd.memset(keep["identb"][:, :], 0.0).then_inc(s["ident_made"], 1)
            pool.wait_ge(s["ident_made"], 2)
            for one in (keep["ident"], keep["identb"]):
                nc.gpsimd.affine_select(out=one[:, :], in_=one[:, :], compare_op=ALU.not_equal, fill=1.0, base=0,
                                        pattern=[[-1, P]], channel_multiplier=1).then_inc(s["ident_filled"], 1)
            nc.gpsimd.memset(ones[:, :], 1.0).then_inc(s["ones_made"], 1)
            nc.gpsimd.memset(eps[:, :], LN_EPS).then_inc(s["consts_made"], 1)
            for i in range(3):
                for f in range(EF):
                    pool.dma_start(enc_f[4 * i + f:4 * i + f + 1, :], a["edge_W"].rearrange("n f -> f n")[f:f + 1, :],
                                   allow_slow_non_contiguous=True).then_inc(s["enc_loaded"], 16)
                pool.dma_start(enc_f[4 * i + EF:4 * i + 4, :], a["edge_b"].rearrange("(o n) -> o n", o=1)).then_inc(s["enc_loaded"], 16)
            nc.gpsimd.iota(steps_at[:, :], pattern=[[1, STEPS]], base=0, channel_multiplier=0,
                           allow_small_or_imprecise_dtypes=True).then_inc(s["consts_made"], 1)
            nc.gpsimd.iota(tile_edges[:, :], pattern=[[P, TILES - 1]], base=P, channel_multiplier=0,
                           allow_small_or_imprecise_dtypes=True).then_inc(s["consts_made"], 1)
            nc.gpsimd.iota(keep["node_at"][:, :], pattern=[[1, P]], base=0, channel_multiplier=0,
                           allow_small_or_imprecise_dtypes=True).then_inc(s["consts_made"], 1)
            for g, (c0, n) in enumerate(GROUPS):
                nc.gpsimd.iota(chunk_no[:, g:g + 1], pattern=[[0, 1]], base=c0, channel_multiplier=1,
                               allow_small_or_imprecise_dtypes=True).then_inc(s["consts_made"], 1)
            pool.wait_ge(s["enc_parts"], 1)
            for j in range(3):
                pool.dma_start(keep["expander"][KA * j:KA * (j + 1), :], enc_p[:, j, :]).then_inc(s["enc_moved"], 16)
            pool.wait_ge(s["enc_moved"], 48)
            for g, (c0, n) in enumerate(GROUPS):
                pool.wait_ge(s["rec_made"], g + 1)
                nc.gpsimd.tensor_copy(attr_w[0:n, :, :, 2, :], attr_w[0:n, :, :, 0, :]).then_inc(s["rec_copied"], 1)
            pool.wait_ge(s["xn_made"], NT)
            nc.gpsimd.memset(keep["acc"][:, :, :], 0.0).then_inc(s["zero_acc"], 1)
            pool.wait_ge(s["zero_acc"], 2)

        @block.tensor
        def _(pe):
            pe.wait_ge(s["w_loaded"], 80)
            pe.wait_ge(s["ident_filled"], 2)
            for i in range(2):
                for o in range(2):
                    last = nc.tensor.transpose(p_w[:, (2 * i + o) * P:(2 * i + o + 1) * P],
                                               w_nat[:, o, i * P:(i + 1) * P], keep["ident"][:, :])
            last.then_inc(s["wT_made"], 1)
            pe.wait_ge(s["diag_made"], 1)
            for i in range(2):
                for o in range(2):
                    last = nc.tensor.matmul(p_v[:, i * 2 * H:(i + 1) * 2 * H], w_nat[:, o, i * P:(i + 1) * P],
                                            a_diag[:, o, :, :].rearrange("p i h -> p (i h)"), start=(o == 0), stop=(o == 1))
            last.then_inc(s["v_made"], 1)

            def transpose_tile(t, b):
                pe.wait_ge(s["xn_made"], t + 1)
                if not (isinstance(t, int) and t < 2):
                    pe.wait_ge(s["xT_moved"], t - 1)
                for i in range(2):
                    last = nc.tensor.transpose(p_xT[b][:, i, :], xn[:, b, i * P:(i + 1) * P], keep["ident"][:, :])
                last.then_inc(s["xT_made"], 1)

            def project_tile(t, b):
                pe.wait_ge(s["xT_moved"], t + 1)
                if not (isinstance(t, int) and t < 2):
                    pe.wait_ge(s["rows_made"], t - 1)
                for i in range(2):
                    last = nc.tensor.matmul(p_h[b][:, :], xnT[:, b, i, :], w_ext[:, i, :], start=(i == 0), stop=(i == 1))
                last.then_inc(s["h_made"], 1)

            pe.wait_ge(s["wext_made"], 2)
            transpose_tile(0, 0)
            transpose_tile(1, 1)
            project_tile(0, 0)
            with nc.tensor.Fori(0, (NT - 2) // 2) as i:
                for u in range(2):
                    transpose_tile(2 * i + 2 + u, u)
                    project_tile(2 * i + 1 + u, 1 - u)
            project_tile(NT - 1, 1)
            pe.wait_ge(s["ones_made"], 1)
            for g, (c0, n) in enumerate(GROUPS):
                pe.wait_ge(s["started_at"], g + 1)
                nc.tensor.matmul(p_s[:, :], ones[0:n, :], started[0:n, g, :], start=(g == 0),
                                 stop=(g == len(GROUPS) - 1)).then_inc(s["counted"], 1)

        @block.scalar
        def _(act):
            act.wait_ge(s["moments_made"], 6)
            act.wait_ge(s["consts_made"], 1)
            nc.scalar.activation(std[:, :], moments[:, :, 1], ACT.Sqrt, bias=eps[:, 0:1]).then_inc(s["std_made"], 1)

            def move_transposed(t, b):
                act.wait_ge(s["xT_made"], t + 1)
                if not (isinstance(t, int) and t < 2):
                    act.wait_ge(s["h_made"], t - 1)
                nc.scalar.copy(xnT[:, b, :, :], p_xT[b][:, :, :]).then_inc(s["xT_moved"], 1)

            def make_rows(t, b, stored):
                act.wait_ge(s["h_made"], t + 1)
                if not (isinstance(stored, int) and stored == 0):
                    act.wait_ge(s_stored[b], stored * 32)
                    act.wait_ge(s["left_made"], 2 * t - 2)
                v = out_rows[:, b, :].rearrange("p (h d) -> p h d", h=H)
                nc.scalar.copy(v[:, :, 0:HD], p_h[b][:, 0:D].rearrange("p (h d) -> p h d", h=H))
                nc.scalar.copy(v[:, :, HD], p_h[b][:, D:D + H])
                nc.scalar.copy(dst_score[:, b, :], p_h[b][:, D + H:D + 2 * H]).then_inc(s["rows_made"], 1)

            def store(t, b):
                act.wait_ge(s["rows_made"], t + 1)
                act.wait_ge(s["parts_made"], t + 1)
                act.dma_start(block_of(scr["rows"].rearrange("(t p) n -> t p n", p=P), t), out_rows[:, b, :]).then_inc(s_stored[b], 16)
                act.dma_start(block_of(scr["parts"], t), out_parts[:, b, :]).then_inc(s_stored[b], 16)

            move_transposed(0, 0)
            move_transposed(1, 1)
            make_rows(0, 0, 0)
            store(0, 0)
            make_rows(1, 1, 0)
            with nc.scalar.Fori(0, (NT - 2) // 2) as i:
                move_transposed(2 * i + 2, 0)
                store(2 * i + 1, 1)
                make_rows(2 * i + 2, 0, i + 1)
                move_transposed(2 * i + 3, 1)
                store(2 * i + 2, 0)
                make_rows(2 * i + 3, 1, i + 1)
            store(NT - 1, 1)
            for b in range(2):
                act.wait_ge(s_stored[b], 32 * (NT // 2))
            for g, (c0, n) in enumerate(GROUPS):
                act.wait_ge(s["rec_made"], g + 1)
                nc.scalar.copy(attr_w[0:n, :, :, 1, :], attr_w[0:n, :, :, 0, :]).then_inc(s["rec_copied"], 1)

        @block.vector
        def _(dve):
            nc.vector.memset(keep["top"][:, :, :], -BIG).then_inc(s["zero_acc"], 1)
            nc.vector.memset(a_diag[:, :, :, :], 0.0).then_inc(s["diag_zero"], 1)
            dve.wait_ge(s["w_loaded"], 80)
            dve.wait_ge(s["diag_zero"], 1)
            for half in range(2):
                for q in range(P // HD):
                    last = nc.vector.tensor_copy(a_diag[q * HD:(q + 1) * HD, half, :, half * (P // HD) + q],
                                                 a_col[q * HD:(q + 1) * HD, half, :])
            last.then_inc(s["diag_made"], 1)
            dve.wait_ge(s["enc_loaded"], 16 * 3 * (EF + 1))
            nc.vector.tensor_copy(enc_p[:, 0, :], enc_f[:, :]).then_inc(s["enc_hi"], 1)
            dve.wait_ge(s["enc_hi"], 1)
            nc.vector.tensor_tensor(enc_left[:, :], enc_f[:, :], enc_p[:, 0, :], ALU.subtract).then_inc(s["enc_l"], 1)
            dve.wait_ge(s["enc_l"], 1)
            nc.vector.tensor_copy(enc_p[:, 1, :], enc_left[:, :]).then_inc(s["enc_mid"], 1)
            dve.wait_ge(s["enc_mid"], 1)
            nc.vector.tensor_tensor(enc_p[:, 2, :], enc_left[:, :], enc_p[:, 1, :], ALU.subtract).then_inc(s["enc_parts"], 1)
            dve.wait_ge(s["wT_made"], 1)
            nc.vector.tensor_copy(w_ext[:, :, 0:D], p_w[:, :].rearrange("p (i n) -> p i n", i=2)).then_inc(s["wext_made"], 1)
            dve.wait_ge(s["v_made"], 1)
            nc.vector.tensor_copy(w_ext[:, :, D:D + 2 * H], p_v[:, :].rearrange("p (i n) -> p i n", i=2)).then_inc(s["wext_made"], 1)

            dve.wait_ge(s["x_loaded"], 32)
            with nc.vector.Fori(0, NT) as t:
                nc.vector.bn_stats(at(stats, t), at(x_all, t)).then_inc(s["stats_made"], 1)
            dve.wait_ge(s["stats_made"], NT)
            merge_moments(nc, dve, stats, halves, moments, s["moments_made"])
            dve.wait_ge(s["std_made"], 1)
            nc.vector.reciprocal(rstd[:, :, 0], std[:, :]).then_inc(s["rstd_made"], 1)
            dve.wait_ge(s["rstd_made"], 1)

            def normalize(t, b):
                if not (isinstance(t, int) and t < 2):
                    dve.wait_ge(s["xT_made"], t - 1)
                mean = moments[:, t, 0:1] if isinstance(t, int) else moments[:, bass.ds(t, 1), 0]
                nc.vector.tensor_scalar(xn[:, b, :], at(x_all, t), mean, at(rstd, t), ALU.subtract, ALU.mult).then_inc(s["xn_made"], 1)

            def make_parts(t, b, stored):
                dve.wait_ge(s["rows_made"], t + 1)
                if not (isinstance(stored, int) and stored == 0):
                    dve.wait_ge(s_stored[b], stored * 32)
                o = out_parts[:, b, :].rearrange("p (i n) -> p i n", i=3)
                h_v = out_rows[:, b, :].rearrange("p (h d) -> p h d", h=H)[:, :, 0:HD]
                hi_v = o[:, 0, 0:D].rearrange("p (h d) -> p h d", h=H)
                nc.vector.tensor_copy(hi_v, h_v).then_inc(s["hi_made"], 1)
                nc.vector.tensor_copy(o[:, 0, D:PART], dst_score[:, b, :]).then_inc(s["hi_made"], 1)
                dve.wait_ge(s["hi_made"], 2 * t + 2)
                if not (isinstance(t, int) and t == 0):
                    dve.wait_ge(s["parts_made"], t)
                nc.vector.tensor_tensor(part_left[:, 0:D].rearrange("p (h d) -> p h d", h=H), h_v, hi_v, ALU.subtract).then_inc(s["left_made"], 1)
                nc.vector.tensor_tensor(part_left[:, D:PART], dst_score[:, b, :], o[:, 0, D:PART], ALU.subtract).then_inc(s["left_made"], 1)
                dve.wait_ge(s["left_made"], 2 * t + 2)
                nc.vector.tensor_copy(o[:, 1, :], part_left[:, :]).then_inc(s["mid_made"], 1)
                dve.wait_ge(s["mid_made"], t + 1)
                nc.vector.tensor_tensor(o[:, 2, :], part_left[:, :], o[:, 1, :], ALU.subtract).then_inc(s["parts_made"], 1)

            normalize(0, 0)
            normalize(1, 1)
            make_parts(0, 0, 0)
            normalize(2, 0)
            make_parts(1, 1, 0)
            normalize(3, 1)
            make_parts(2, 0, 1)
            with nc.vector.Fori(0, (NT - 4) // 2) as i:
                normalize(2 * i + 4, 0)
                make_parts(2 * i + 3, 1, i + 1)
                normalize(2 * i + 5, 1)
                make_parts(2 * i + 4, 0, i + 2)
            make_parts(NT - 1, 1, NT // 2 - 1)

            nc.vector.memset(attr_p[:, :, :, 1, EF], 0.0).then_inc(s["rec_const"], 1)
            nc.vector.memset(attr_p[:, :, :, 2, EF], 0.0).then_inc(s["rec_const"], 1)
            nc.vector.memset(attr_p[:, :, :, 0, EF], 1.0).then_inc(s["rec_const"], 1)
            dve.wait_ge(s["consts_made"], 4 + len(GROUPS))
            for g, (c0, n) in enumerate(GROUPS):
                dve.wait_ge(s_edges[g], 96 if c0 + n > FULL else 48)
                if g:
                    dve.wait_ge(s["rec_stored"], 16 * (1 + H) * g)
                dst = rec[0:n, :, DST:DST + C]
                nc.vector.tensor_copy(dst, dst_rows[0:n, :].rearrange("c (p k) -> c p k", k=C)).then_inc(s["dst_made"], 1)
                nc.vector.tensor_copy(rec_i[0:n, :, SRC:SRC + C], src_rows[0:n, :].rearrange("c (p k) -> c p k", k=C))
                dve.wait_ge(s["dst_made"], g + 1)
                ch = changed[0:n, 0:P - 1, :]
                nc.vector.tensor_tensor(ch, dst[:, 1:P, :], dst[:, 0:P - 1, :], ALU.not_equal).then_inc(s["chg_made"], 1)
                nc.vector.tensor_scalar(reached[0:n, :], tile_edges[0:n, :], rec[0:n, 0, 0:1], None, ALU.is_le).then_inc(s["reached_s"], 1)
                av = attr_rows[0:n, :].rearrange("c (p k f) -> c p k f", k=C, f=EF)
                nc.vector.tensor_copy(attr_p[0:n, :, :, 0, 0:EF], av).then_inc(s["a_hi"], 1)
                dve.wait_ge(s["chg_made"], g + 1)
                nc.vector.tensor_copy(rec[0:n, 0:P - 1, LAST:LAST + C], ch)
                nc.vector.memset(rec[0:n, P - 1, LAST:LAST + C], 1.0)
                nc.vector.memset(start_rows[0:n, :, 0:1], -BIG)
                nc.vector.tensor_scalar(start_rows[0:n, :, 1:P].rearrange("c k p -> c p k"), ch, -BIG, None, ALU.mult).then_inc(s["starts_made"], 1)
                dve.wait_ge(s["reached_s"], g + 1)
                nc.vector.tensor_reduce(chunk_tile[0:n, g:g + 1], reached[0:n, :], AX.X, ALU.add).then_inc(s["ctile_s"], 1)
                dve.wait_ge(s["ctile_s"], g + 1)
                if g == 0:
                    nc.vector.memset(chunk_tile[0:1, 0:1], 0.0).then_inc(s["cfix_s"], 1)
                    dve.wait_ge(s["cfix_s"], 1)
                nc.vector.tensor_tensor(chunk_start[0:n, g:g + 1], chunk_tile[0:n, g:g + 1], chunk_no[0:n, g:g + 1], ALU.add).then_inc(s["cstart_s"], 1)
                dve.wait_ge(s["a_hi"], g + 1)
                nc.vector.tensor_tensor(av, av, attr_p[0:n, :, :, 0, 0:EF], ALU.subtract).then_inc(s["a_left"], 1)
                dve.wait_ge(s["cstart_s"], g + 1)
                nc.vector.tensor_scalar(started[0:n, g, :], steps_at[0:n, :], chunk_start[0:n, g:g + 1], None, ALU.is_ge).then_inc(s["started_at"], 1)
                dve.wait_ge(s["a_left"], g + 1)
                nc.vector.tensor_copy(attr_p[0:n, :, :, 1, 0:EF], av).then_inc(s["a_mid"], 1)
                dve.wait_ge(s["a_mid"], g + 1)
                dve.wait_ge(s["rec_const"], 3)
                nc.vector.tensor_tensor(attr_p[0:n, :, :, 2, 0:EF], av, attr_p[0:n, :, :, 1, 0:EF], ALU.subtract).then_inc(s["rec_made"], 1)
                if g == 0:
                    dve.wait_ge(s["rec_made"], 1)
                    nc.vector.memset(dst_rows[:, :], PAD_DST)
                    nc.vector.memset(src_rows[:, :], 0)
                    nc.vector.memset(attr_rows[:, :], 0.0).then_inc(s["row_pad"], 1)
            dve.wait_ge(s["counted"], len(GROUPS))
            nc.vector.tensor_scalar(step_c[:, :], p_s[:, :], -1.0, None, ALU.add).then_inc(s["stepc_s"], 1)
            dve.wait_ge(s["stepc_s"], 1)
            nc.vector.tensor_tensor(step_t[:, :], steps_at[:, :], step_c[:, :], ALU.subtract).then_inc(s["stept_s"], 1)
            nc.vector.tensor_copy(keep["step_chunk"][:, :], step_c[0:1, :]).then_inc(s["tables_s"], 1)
            dve.wait_ge(s["stept_s"], 1)
            nc.vector.tensor_copy(keep["step_tile"][:, :], step_t[0:1, :]).then_inc(s["tables_s"], 1)
            nc.vector.tensor_scalar(keep["tile_base"][:, :], step_t[:, :], float(P), None, ALU.mult).then_inc(s["tables_s"], 1)
            dve.wait_ge(s["tables_s"], 3)
            dve.wait_ge(s["zero_acc"], 2)


RING = 4
PAIRS = C // 2


class Step:

    def __init__(self, s, slot, turn):
        self.s, self.slot, self.turn = s, slot, turn
        self.parity = slot % 2

    def next(self):
        wraps = self.slot == RING - 1
        return Step(self.s + 1, (self.slot + 1) % RING, self.turn + 1 if wraps else self.turn)

    def prev(self):
        wraps = self.slot == 0
        return Step(self.s - 1, (self.slot - 1) % RING, self.turn - 1 if wraps else self.turn)

    def column(self, ap):
        return ap[:, self.s:self.s + 1] if isinstance(self.s, int) else ap[:, bass.ds(self.s, 1)]

    def since(self, n):
        return not isinstance(self.s, int) or self.s >= n


def edge_loop(nc, scr, keep):
    with Scope(nc) as m:
        rec = m.sb("rec_in", [P, RING, REC])
        rec_i = rec[:, :, :].bitcast(I32)
        rec_b = rec[:, :, :].bitcast(BF16)
        starts = m.sb("starts_in", [C * H, RING, P])
        node = m.sb("node_in", [P, RING, 3 * PART], BF16)
        src = m.sb("src_in", [P, RING, C, ROW])
        local = m.sb("local", [P, 2, C])
        away = m.sb("away", [P, 2, 4 * P])
        hot = m.sb("hot", [P, RING, C, P])
        hotT = m.sb("hotT", [P, RING, C * P], BF16)
        attrT = m.sb("attrT", [KE, RING, C * P], BF16)
        enc = m.sb("enc", [P, 2, 2 * D])
        prod = m.sb("prod", [P, C, H, HD + 2])
        dots = m.sb("dots", [P, 2, C * H])
        score = m.sb("score", [P, 2, P])
        running = m.sb("running", [P, P])
        lasts = m.sb("lasts", [P, C, H + 1])
        absent = m.sb("absent", [P, C])
        masked = m.sb("masked", [P, C, H])
        chunk_top = m.sb("chunk_top", [P, H])
        new_top = m.sb("new_top", [P, H])
        drop = m.sb("drop", [P, H])
        keep_by = m.sb("keep_by", [P, 2, H])
        top_left = m.sb("top_left", [P, H])
        top_p = m.sb("top_p", [P, 3, H], BF16)
        below = m.sb("below", [P, C * H])
        capped = m.sb("capped", [P, C * H])
        weight = m.sb("weight", [P, C * H])
        weighted = m.sb("weighted", [P, C, ROW])
        scaled = m.sb("scaled", [P, ROW])

        p_enc = [m.ps(f"p_enc{i}", [P, 2 * D]) for i in range(2)]
        p_dst = [m.ps(f"p_dst{i}", [P, 2 * D]) for i in range(2)]
        p_turn = m.ps("p_turn", [P, 4, P])
        p_chain = m.ps("p_chain", [P, 512])
        p_misc = m.ps("p_misc", [P, 512])
        p_sums = m.ps("p_sums", [P, 512])
        p_score = p_misc[:, 0:C * H]
        p_attrT = p_misc[0:KE, 2 * P:4 * P].bitcast(BF16)
        p_scoreT, p_back = p_chain[:, 0:P], p_chain[:, P:2 * P]
        p_lasts = p_back[:, 0:C * H]
        p_top = p_chain[:, 256:256 + C * (H + 1)].rearrange("p (k h) -> p k h", k=C)
        p_sum, p_ref = p_sums[:, 0:ROW], p_sums[:, 384:384 + C * H]

        s_loaded = [m.sem(f"s_loaded{i}") for i in range(RING)]
        s_gathered = [m.sem(f"s_gathered{i}") for i in range(RING)]
        names = """turning gathering zeros local away hot attr_turned attr_moved hot_turned hot_moved enc dst_picked relu prod dst_score src_score dots score
            scoreT running lasts_back lasts chunk_tops absent masked chunk_top new_top drop top_hi top_left top_mid
            top_parts top_kept kept refs below capped weight weight_row weighted sums scaled merged""".split()
        s = {n: m.sem("s_" + n) for n in names}

        block = m.enter_context(nc.Block())

        def loop(engine, body, first, last, last_steps=2):
            def straight(k):
                return Step(k, k % RING, k // RING)

            first()
            for k in range(1, RING):
                body(straight(k))
            turns = (STEPS - last_steps - RING) // RING
            with engine.Fori(0, turns) as i:
                for u in range(RING):
                    body(Step(i * RING + RING + u, u, i + 1))
            for k in range((turns + 1) * RING, STEPS - last_steps):
                body(straight(k))
            last(straight(STEPS - 1))

        first_step = Step(0, 0, 0)

        @block.sync
        def _(sp):
            def load(q):
                chunk = nc.sync.value_load(q.column(keep["step_chunk"]), min_val=0, max_val=NC - 1)
                tile = nc.sync.value_load(q.column(keep["step_tile"]), min_val=0, max_val=TILES - 1)
                if q.since(RING):
                    sp.wait_ge(s["refs"], q.s - RING + 1)
                sp.dma_start(rec[:, q.slot, :], block_of(scr["edges"], chunk)).then_inc(s_loaded[q.slot], 16)
                sp.dma_start(node[:, q.slot, :], block_of(scr["parts"], tile)).then_inc(s_loaded[q.slot], 16)
                sp.dma_start(starts[:, q.slot, :], block_of(scr["starts"], chunk)).then_inc(s_loaded[q.slot], 16)

            loop(nc.sync, load, lambda: load(first_step), load, 1)

        @block.gpsimd
        def _(pool):
            def gather(q):
                if q.since(RING):
                    pool.wait_ge(s["weighted"], 2 * (q.s - RING + 1))
                pool.wait_ge(s_loaded[q.slot], 48 * (q.turn + 1))
                nc.gpsimd.sem_inc(s["gathering"], 1)
                for k in range(C):
                    pool.indirect_dma_start(src[:, q.slot, k, :], None, scr["rows"],
                                            bass.IndirectOffsetOnAxis(ap=rec_i[:, q.slot, SRC + k:SRC + k + 1], axis=0)
                                            ).then_inc(s_gathered[q.slot], 16)

            loop(nc.gpsimd, gather, lambda: gather(first_step), gather, 1)

        @block.tensor
        def _(pe):
            def turn_edges(q, half):
                n = 2 * q.s + half
                ks = range(4 * half, 4 * half + 4)
                if half == 0:
                    pe.wait_ge(s_loaded[q.slot], 48 * (q.turn + 1))
                if q.since(1) or half:
                    pe.wait_ge(s["hot_moved"], n)
                if half == 0 and q.since(1):
                    pe.wait_ge(s["dst_score"], q.s)
                nc.tensor.sem_inc(s["turning"], 1)
                for j, k in enumerate(ks):
                    last = nc.tensor.transpose(p_attrT[:, j * P:(j + 1) * P], rec_b[:, q.slot, 2 * ATTR + KE * k:2 * ATTR + KE * (k + 1)], keep["identb"][:, :])
                last.then_inc(s["attr_turned"], 1)
                pe.wait_ge(s["hot"], n + 1)
                for j, k in enumerate(ks):
                    last = nc.tensor.transpose(p_turn[:, j, :], hot[:, q.slot, k, :], keep["ident"][:, :])
                last.then_inc(s["hot_turned"], 1)

            def pair(q, r, turned):
                b, n = q.slot, PAIRS * q.s + r
                pe.wait_ge(s["attr_moved"], 2 * q.s + (2 * r) // 4 + 1)
                if q.since(1) or r >= 2:
                    pe.wait_ge(s["relu"], n - 1)
                for j in range(2):
                    k = 2 * r + j
                    last = nc.tensor.matmul(p_enc[r % 2][:, j * D:(j + 1) * D], attrT[:, b, k * P:(k + 1) * P],
                                            keep["expander"][:, :], start=True, stop=True)
                last.then_inc(s["enc"], 1)
                pe.wait_ge(s["hot_moved"], 2 * q.s + (2 * r) // 4 + 1)
                if q.since(1) or r >= 2:
                    pe.wait_ge(s["prod"], n - 1)
                if r == 0 and q.since(1):
                    pe.wait_ge(s["dst_score"], q.s)
                pe.wait_ge(s["attr_moved"], turned)
                for j in range(2):
                    k = 2 * r + j
                    for i in range(3):
                        nc.tensor.matmul(p_dst[r % 2][:, j * D:(j + 1) * D], hotT[:, b, k * P:(k + 1) * P],
                                         node[:, q.slot, i * PART:i * PART + D], start=(i == 0), stop=(i == 2))
                    for i in range(3):
                        last = nc.tensor.matmul(p_score[:, k * H:(k + 1) * H], hotT[:, b, k * P:(k + 1) * P],
                                                node[:, q.slot, i * PART + D:(i + 1) * PART], start=(i == 0), stop=(i == 2))
                last.then_inc(s["dst_picked"], 1)

            def turn_scores(q):
                pe.wait_ge(s["score"], q.s + 1)
                if q.since(1):
                    pe.wait_ge(s["masked"], q.s)
                nc.tensor.transpose(p_scoreT, score[:, q.parity, :], keep["ident"][:, :]).then_inc(s["scoreT"], 1)

            def turn_back(q):
                pe.wait_ge(s["running"], q.s + 1)
                nc.tensor.transpose(p_back, running[:, :], keep["ident"][:, :]).then_inc(s["lasts_back"], 1)

            def tops(q):
                pe.wait_ge(s["lasts"], q.s + 1)
                for k in range(C):
                    last = nc.tensor.matmul(p_top[:, k, :], hot[:, q.slot, k, :], lasts[:, k, :], start=True, stop=True)
                last.then_inc(s["chunk_tops"], 1)

            def refs(q):
                b = q.slot
                pe.wait_ge(s["top_parts"], q.s + 1)
                if q.since(1):
                    pe.wait_ge(s["merged"], q.s)
                for k in range(C):
                    for i in range(3):
                        last = nc.tensor.matmul(p_ref[:, k * H:(k + 1) * H], hotT[:, b, k * P:(k + 1) * P], top_p[:, i, :],
                                                start=(i == 0), stop=(i == 2))
                last.then_inc(s["refs"], 1)

            def sums(q, half):
                pe.wait_ge(s["weight_row"], q.s + 1)
                pe.wait_ge(s["weighted"], 2 * q.s + half + 1)
                if half == 0:
                    pe.wait_ge(s["below"], q.s + 1)
                for k in range(4 * half, 4 * half + 4):
                    last = nc.tensor.matmul(p_sum, hot[:, q.slot, k, :], weighted[:, k, :], start=(k == 0), stop=(k == C - 1))
                if half:
                    last.then_inc(s["sums"], 1)

            def first():
                for half in range(2):
                    turn_edges(first_step, half)
                for r in range(PAIRS):
                    pair(first_step, r, 2)
                second = first_step.next()
                for half in range(2):
                    turn_edges(second, half)
                pair(second, 0, 4)
                pair(second, 1, 4)
                body(first_step)

            def body(q, ahead=True):
                n = q.next()
                turn_scores(q)
                pair(n, 2, 2 * n.s + 2)
                if q.since(1):
                    refs(q.prev())
                turn_back(q)
                pair(n, 3, 2 * n.s + 2)
                tops(q)
                if ahead:
                    turn_edges(n.next(), 0)
                if q.since(1):
                    sums(q.prev(), 0)
                if ahead:
                    turn_edges(n.next(), 1)
                if q.since(1):
                    sums(q.prev(), 1)
                if ahead:
                    pair(n.next(), 0, 2 * n.s + 4)
                    pair(n.next(), 1, 2 * n.s + 4)

            def last(q):
                body(q.prev(), ahead=False)
                turn_scores(q)
                refs(q.prev())
                turn_back(q)
                tops(q)
                for p in (q.prev(), q):
                    if p is q:
                        refs(q)
                    sums(p, 0)
                    sums(p, 1)

            loop(nc.tensor, body, first, last)

        @block.scalar
        def _(act):
            def measure(q, half):
                if half == 0:
                    act.wait_ge(s_loaded[q.slot], 48 * (q.turn + 1))
                    nc.scalar.activation(local[:, q.parity, :], rec[:, q.slot, DST:DST + C], ACT.Identity,
                                         bias=q.column(keep["tile_base"]), scale=-1.0).then_inc(s["local"], 1)
                    act.wait_ge(s["local"], q.s + 1)
                if q.since(1):
                    act.wait_ge(s["hot"], 2 * q.s + half - 1)
                for j in range(4):
                    k = 4 * half + j
                    last = nc.scalar.activation(away[:, half, j * P:(j + 1) * P], keep["node_at"][:, :], ACT.Abs, bias=local[:, q.parity, k:k + 1])
                last.then_inc(s["away"], 1)

            def make_hot(q, half):
                if q.since(RING):
                    act.wait_ge(s["sums"], q.s - RING + 1)
                act.wait_ge(s["away"], 2 * q.s + half + 1)
                nc.scalar.activation(hot[:, q.slot, 4 * half:4 * half + 4, :].rearrange("p k n -> p (k n)"), away[:, half, :], ACT.Relu,
                                     scale=-1.0, bias=1.0).then_inc(s["hot"], 1)

            def move_turned(q, half):
                b, n = q.slot, 2 * q.s + half
                cols = slice(half * 4 * P, (half + 1) * 4 * P)
                act.wait_ge(s["attr_turned"], n + 1)
                if q.since(RING):
                    act.wait_ge(s["refs"], q.s - RING + 1)
                nc.scalar.copy(attrT[:, b, cols], p_attrT).then_inc(s["attr_moved"], 1)
                act.wait_ge(s["hot_turned"], n + 1)
                nc.scalar.copy(hotT[:, b, cols], p_turn[:, :, :].rearrange("p j n -> p (j n)")).then_inc(s["hot_moved"], 1)

            def move_scores(q):
                if q.since(1):
                    act.wait_ge(s["dots"], 2 * q.s)
                act.wait_ge(s["dst_picked"], PAIRS * (q.s + 1))
                nc.scalar.copy(prod[:, :, :, HD], p_score.rearrange("p (k h) -> p k h", k=C)).then_inc(s["dst_score"], 1)
                act.wait_ge(s_gathered[q.slot], 16 * C * (q.turn + 1))
                nc.scalar.copy(prod[:, :, :, HD + 1], src[:, q.slot, :, :].rearrange("p k (h d) -> p k h d", h=H)[:, :, :, HD]).then_inc(s["src_score"], 1)

            def relu(q, r):
                n = PAIRS * q.s + r
                act.wait_ge(s["enc"], n + 1)
                if q.since(1) or r >= 2:
                    act.wait_ge(s["prod"], n - 1)
                nc.scalar.activation(enc[:, r % 2, :], p_enc[r % 2][:, :], ACT.Relu).then_inc(s["relu"], 1)

            def rescale(q):
                act.wait_ge(s["drop"], q.s + 1)
                nc.scalar.activation(keep_by[:, q.parity, :], drop[:, :], ACT.Exp).then_inc(s["kept"], 1)

            def weights(q):
                act.wait_ge(s["capped"], q.s + 1)
                if q.since(1):
                    act.wait_ge(s["weighted"], 2 * q.s)
                nc.scalar.activation(weight[:, :], capped[:, :], ACT.Exp).then_inc(s["weight"], 1)
                if q.since(1):
                    act.wait_ge(s["sums"], q.s)
                nc.scalar.activation(weighted[:, :, :].rearrange("p k (h d) -> p k h d", h=H)[:, :, :, HD],
                                     capped[:, :].rearrange("p (k h) -> p k h", k=C), ACT.Exp).then_inc(s["weight_row"], 1)

            def first():
                second = first_step.next()
                for q in (first_step, second, second.next()):
                    for half in range(2 if q.s < 2 else 1):
                        measure(q, half)
                        make_hot(q, half)
                for half in range(2):
                    move_turned(first_step, half)
                for r in range(PAIRS):
                    relu(first_step, r)
                move_scores(first_step)
                for half in range(2):
                    move_turned(second, half)
                relu(second, 0)
                relu(second, 1)
                body(first_step)

            def body(q, ahead=2):
                n = q.next()
                m2 = n.next()
                relu(n, 2)
                if q.since(1):
                    weights(q.prev())
                relu(n, 3)
                move_scores(n)
                if ahead:
                    measure(m2, 1)
                    make_hot(m2, 1)
                    move_turned(m2, 0)
                if ahead > 1:
                    measure(m2.next(), 0)
                if ahead:
                    move_turned(m2, 1)
                rescale(q)
                if ahead > 1:
                    make_hot(m2.next(), 0)
                if ahead:
                    relu(m2, 0)
                    relu(m2, 1)

            def last(q):
                body(q.prev().prev(), 1)
                body(q.prev(), 0)
                weights(q.prev())
                rescale(q)
                weights(q)

            loop(nc.scalar, body, first, last, 3)

        @block.vector
        def _(dve):
            def product(q, r):
                n = PAIRS * q.s + r
                dve.wait_ge(s["relu"], n + 1)
                dve.wait_ge(s["dst_picked"], n + 1)
                if q.since(1):
                    dve.wait_ge(s["dots"], 2 * q.s - 1 + r // 2)
                by_head = lambda v: v.rearrange("p (k h d) -> p k h d", k=2, h=H)
                nc.vector.tensor_tensor(prod[:, 2 * r:2 * r + 2, :, 0:HD], by_head(enc[:, r % 2, :]), by_head(p_dst[r % 2][:, :]),
                                        ALU.mult).then_inc(s["prod"], 1)

            def sum_heads(q, half):
                dve.wait_ge(s["prod"], PAIRS * q.s + 2 * half + 2)
                dve.wait_ge(s["src_score"], q.s + 1)
                n, ks = C * H // 2, slice(4 * half, 4 * half + 4)
                nc.vector.tensor_reduce(dots[:, q.parity, half * n:(half + 1) * n], prod[:, ks, :, :].rearrange("p k h d -> p (k h) d"),
                                        AX.X, ALU.add).then_inc(s["dots"], 1)

            def scores(q):
                dve.wait_ge(s["dots"], 2 * q.s + 2)
                if q.since(2):
                    dve.wait_ge(s["below"], q.s - 1)
                d = dots[:, q.parity, :]
                nc.vector.scalar_tensor_tensor(score[:, q.parity, 0:C * H], d, 0.2, d, ALU.mult, ALU.max).then_inc(s["score"], 1)

            def scan(q):
                dve.wait_ge(s["scoreT"], q.s + 1)
                nc.vector.tensor_tensor_scan(running[0:C * H, :], starts[:, q.slot, :], p_scoreT[0:C * H, :], -BIG, ALU.add, ALU.max).then_inc(s["running"], 1)

            def mask_lasts(q):
                last_v = rec[:, q.slot, LAST:LAST + C]
                nc.vector.tensor_copy(lasts[:, :, H], last_v)
                dve.wait_ge(s["lasts_back"], q.s + 1)
                nc.vector.tensor_tensor(lasts[:, :, 0:H], p_lasts.rearrange("p (k h) -> p k h", k=C),
                                        spread(last_v, H), ALU.mult).then_inc(s["lasts"], 1)

            def top_of_chunk(q, stage):
                if stage == 0:
                    dve.wait_ge(s["chunk_tops"], q.s + 1)
                    nc.vector.tensor_scalar(absent[:, :], p_top[:, :, H], BIG, -BIG, ALU.mult, ALU.add).then_inc(s["absent"], 1)
                elif stage == 1:
                    dve.wait_ge(s["absent"], q.s + 1)
                    nc.vector.tensor_tensor(masked[:, :, :], p_top[:, :, 0:H], spread(absent[:, :], H), ALU.add).then_inc(s["masked"], 1)
                else:
                    dve.wait_ge(s["masked"], q.s + 1)
                    nc.vector.tensor_reduce(chunk_top[:, :], masked[:, :, :].rearrange("p k h -> p h k"), AX.X, ALU.max).then_inc(s["chunk_top"], 1)

            def update_top(q):
                top = at(keep["top"], load_tile(q))
                dve.wait_ge(s["chunk_top"], q.s + 1)
                nc.vector.tensor_tensor(new_top[:, :], chunk_top[:, :], top, ALU.max).then_inc(s["new_top"], 1)
                dve.wait_ge(s["new_top"], q.s + 1)
                nc.vector.tensor_copy(top_p[:, 0, :], new_top[:, :]).then_inc(s["top_hi"], 1)
                if q.since(1):
                    dve.wait_ge(s["kept"], q.s)
                nc.vector.tensor_tensor(drop[:, :], top, new_top[:, :], ALU.subtract).then_inc(s["drop"], 1)
                dve.wait_ge(s["top_hi"], q.s + 1)
                nc.vector.tensor_tensor(top_left[:, :], new_top[:, :], top_p[:, 0, :], ALU.subtract).then_inc(s["top_left"], 1)
                dve.wait_ge(s["drop"], q.s + 1)
                nc.vector.tensor_scalar(top, new_top[:, :], 1.0, None, ALU.mult).then_inc(s["top_kept"], 1)

            def split_top(q):
                dve.wait_ge(s["top_left"], q.s + 1)
                nc.vector.tensor_copy(top_p[:, 1, :], top_left[:, :]).then_inc(s["top_mid"], 1)
                dve.wait_ge(s["top_mid"], q.s + 1)
                nc.vector.tensor_tensor(top_p[:, 2, :], top_left[:, :], top_p[:, 1, :], ALU.subtract).then_inc(s["top_parts"], 1)

            def exponents(q):
                dve.wait_ge(s["refs"], q.s + 1)
                nc.vector.tensor_tensor(below[:, :], score[:, q.parity, 0:C * H], p_ref, ALU.subtract).then_inc(s["below"], 1)
                dve.wait_ge(s["below"], q.s + 1)
                if q.since(1):
                    dve.wait_ge(s["weight_row"], q.s)
                nc.vector.tensor_scalar(capped[:, :], below[:, :], 0.0, None, ALU.min).then_inc(s["capped"], 1)

            def apply_weights(q, half):
                if half == 0:
                    dve.wait_ge(s["weight"], q.s + 1)
                    if q.since(1):
                        dve.wait_ge(s["sums"], q.s)
                ks = slice(4 * half, 4 * half + 4)
                w = weight[:, :].rearrange("p (k h) -> p k h", k=C)[:, ks, :].rearrange("p k h -> p (k h)")
                nc.vector.tensor_tensor(weighted[:, ks, :].rearrange("p k (h d) -> p (k h) d", h=H)[:, :, 0:HD],
                                        src[:, q.slot, ks, :].rearrange("p k (h d) -> p (k h) d", h=H)[:, :, 0:HD],
                                        spread(w, HD), ALU.mult).then_inc(s["weighted"], 1)

            def merge(q):
                acc = at(keep["acc"], load_tile(q))
                dve.wait_ge(s["kept"], q.s + 1)
                if q.since(1):
                    dve.wait_ge(s["merged"], q.s)
                heads = lambda v: v.rearrange("p (h d) -> p h d", h=H)
                nc.vector.tensor_tensor(heads(scaled[:, :]), heads(acc), spread(keep_by[:, q.parity, :], HD + 1),
                                        ALU.mult).then_inc(s["scaled"], 1)
                dve.wait_ge(s["scaled"], q.s + 1)
                dve.wait_ge(s["sums"], q.s + 1)
                nc.vector.tensor_tensor(acc, scaled[:, :], p_sum, ALU.add).then_inc(s["merged"], 1)

            def load_tile(q):
                return nc.vector.value_load(q.column(keep["step_tile"]), min_val=0, max_val=TILES - 1)

            def first():
                nc.vector.memset(score[:, :, :], 0.0).then_inc(s["zeros"], 1)
                nc.vector.memset(running[:, :], 0.0).then_inc(s["zeros"], 1)
                dve.wait_ge(s["zeros"], 2)
                for r in range(PAIRS):
                    product(first_step, r)
                sum_heads(first_step, 0)
                sum_heads(first_step, 1)
                scores(first_step)
                body(first_step)

            def body(q):
                n = q.next()
                product(n, 0)
                scan(q)
                product(n, 1)
                if q.since(1):
                    exponents(q.prev())
                mask_lasts(q)
                product(n, 2)
                if q.since(1):
                    apply_weights(q.prev(), 0)
                    apply_weights(q.prev(), 1)
                product(n, 3)
                top_of_chunk(q, 0)
                top_of_chunk(q, 1)
                sum_heads(n, 0)
                top_of_chunk(q, 2)
                update_top(q)
                split_top(q)
                sum_heads(n, 1)
                scores(n)
                if q.since(1):
                    merge(q.prev())

            def last(q):
                body(q.prev())
                scan(q)
                exponents(q.prev())
                mask_lasts(q)
                for half in range(2):
                    apply_weights(q.prev(), half)
                for stage in range(3):
                    top_of_chunk(q, stage)
                update_top(q)
                split_top(q)
                merge(q.prev())
                exponents(q)
                for half in range(2):
                    apply_weights(q, half)
                merge(q)
                dve.wait_ge(s["merged"], STEPS)

            loop(nc.vector, body, first, last)


EXP_AT = (3, 17, 24)
INDEX_AT = 22


def epilogue(nc, a, keep, out):
    hidden = FF // P
    blocks = -(-N // (2 * P))
    last_cols = N - (blocks - 1) * 2 * P
    assert last_cols <= P and NT == 2 * blocks and TOPK == 2
    with Scope(nc) as m:
        x1 = m.sb("x1", [P, NT, D])
        moe = keep["acc"][:, :, 0:D]
        x2T = m.sb("x2T", [P, 2, NT * P])
        fresh = m.sb("fresh", [P, 2, D])
        denom = m.sb("denom", [P, NT, H])
        inverse = m.sb("inverse", [P, NT, H])
        bias = m.sb("bias", [P, D])
        gamma = m.sb("gamma", [P, D])
        beta = m.sb("beta", [P, D])
        stats = m.sb("e_stats", [P, NT, 6])
        halves = m.sb("e_halves", [P, 4, NT])
        moments = m.sb("e_moments", [P, NT, 2])
        std = m.sb("e_std", [P, NT])
        rstd = m.sb("e_rstd", [P, NT, 1])
        shift = m.sb("e_shift", [P, NT, 1])
        eps = m.sb("e_eps", [P, 1])
        col_sums = m.sb("col_sums", [P, 2, TILES])
        mean = m.sb("mean", [P, 2])
        total = m.sb("total", [P, 2])
        wr = m.sb("wr", [P, 2, NX])
        r_ = {n: m.sb("r_" + n, [1, w], dt) for n, w, dt in (
            ("br", NX, F32), ("logits", NX, F32), ("top", 1, F32), ("d", NX, F32), ("e", NX, F32), ("sum", 1, F32),
            ("p", NX, F32), ("load", NX, F32), ("q", NX, F32), ("over", NX, F32), ("under", NX, F32),
            ("scale", NX, F32), ("t", NX, F32), ("best", NX, F32), ("index", NX, U32), ("w2", TOPK, F32), ("ones", P, F32))}
        share = m.sb("share", [P, TOPK])
        w1 = m.sb("w1", [P, TOPK, 2, FF])
        w2 = m.sb("w2", [P, TOPK, hidden, D])
        b1 = m.sb("b1", [P, TOPK, hidden])
        b2 = m.sb("b2", [P, TOPK, D])
        b2_mix = m.sb("b2_mix", [P, D])
        act_h = m.sb("act_h", [P, 2, TOPK * hidden, 2 * P])
        normed = m.sb("normed", [P, 2, D])

        p_T = [m.ps(f"p_T{i}", [P, 2, P]) for i in range(2)]
        p_up = [m.ps(f"p_up{i}", [P, 2 * P]) for i in range(4)]
        p_y = [m.ps(f"p_y{i}", [P, D]) for i in range(2)]
        p_r = p_y[0]

        names = """eps cap ones x bias vec x_biased denom inverse gnn x1 stats moments std rstd fresh x2T x2T_moved x2_kept pad
            wr total mean logits  share expert b2a b2_mix w2_scaled x1_beta b2_added up act_h down moe stats2
            moments2 std2 rstd2 mean_r shift normed scaled result small stored expo shared""".split()
        s = {n: m.sem("e_" + n) for n in names}
        heads = lambda v: v.rearrange("p (h d) -> p h d", h=H)
        block = m.enter_context(nc.Block())

        @block.sync
        def _(sp):
            full = (TILES - 1) * P
            sp.dma_start(x1[:, 0:TILES - 1, :], a["x"][0:full, :].rearrange("(t p) n -> p t n", p=P)).then_inc(s["x"], 16)
            sp.wait_ge(s["pad"], 1)
            sp.dma_start(x1[0:LASTROWS, TILES - 1, :], a["x"][full:N, :]).then_inc(s["x"], 16)
            sp.dma_start(bias[:, :], a["gnn_bias"].partition_broadcast(P)).then_inc(s["bias"], 16)
            sp.dma_start(gamma[:, :], a["gamma"].partition_broadcast(P)).then_inc(s["vec"], 16)
            sp.dma_start(beta[:, :], a["beta"].partition_broadcast(P)).then_inc(s["vec"], 16)
            sp.dma_start(wr[:, :, :], a["Wr"].rearrange("(c p) n -> p c n", p=P)).then_inc(s["wr"], 16)
            sp.dma_start(r_["br"][:, :], a["br"].rearrange("(o n) -> o n", o=1)).then_inc(s["wr"], 16)
            sp.wait_ge(s["small"], INDEX_AT)
            for k in range(TOPK):
                e = nc.sync.value_load(r_["index"][0:1, k:k + 1], min_val=0, max_val=NX - 1)
                one = lambda v: v[bass.ds(e, 1)]
                sp.dma_start(w1[:, k, :, :], one(a["W1"]).rearrange("o (c p) f -> p (o c) f", p=P)).then_inc(s["expert"], 16)
                sp.dma_start(w2[:, k, :, :], one(a["W2"]).rearrange("o (c p) f -> p (o c) f", p=P)).then_inc(s["expert"], 16)
                sp.dma_start(b1[:, k, :], one(a["b1"]).rearrange("o (c p) -> p (o c)", p=P), allow_slow_non_contiguous=True).then_inc(s["expert"], 16)
                sp.dma_start(b2[:, k, :], one(a["b2"]).rearrange("o n -> (o n)").partition_broadcast(P)).then_inc(s["expert"], 16)
            def store(t, rows=P):
                dst = out[t * P:t * P + rows, :] if isinstance(t, int) else out[bass.ds(t * P, P), :]
                sp.wait_ge(s["result"], t + 1)
                sp.dma_start(dst, at(x1, t)[0:rows, :]).then_inc(s["stored"], 16)

            with nc.sync.Fori(0, TILES - 1) as t:
                store(t)
            store(TILES - 1, LASTROWS)
            sp.wait_ge(s["stored"], 16 * TILES)

        @block.gpsimd
        def _(pool):
            nc.gpsimd.memset(x1[:, TILES - 1:NT, :], 0.0).then_inc(s["pad"], 1)
            nc.gpsimd.memset(x2T[:, :, (TILES - 1) * P:], 0.0).then_inc(s["pad"], 1)
            nc.gpsimd.memset(eps[:, :], LN_EPS).then_inc(s["eps"], 1)
            nc.gpsimd.memset(r_["ones"][:, :], 1.0).then_inc(s["ones"], 1)
            pool.wait_ge(s["x"], 32)
            pool.wait_ge(s["bias"], 16)
            with nc.gpsimd.Fori(0, NT) as t:
                nc.gpsimd.tensor_tensor(at(x1, t), at(x1, t), bias[:, :], ALU.add).then_inc(s["x_biased"], 1)
            pool.wait_ge(s["b2_mix"], 1)
            pool.wait_ge(s["x2_kept"], NT)
            pool.wait_ge(s["fresh"], NT)
            pool.wait_ge(s["vec"], 32)
            with nc.gpsimd.Fori(0, NT) as t:
                nc.gpsimd.tensor_tensor(at(moe, t), at(moe, t), b2_mix[:, :], ALU.add).then_inc(s["b2_added"], 1)
                nc.gpsimd.tensor_tensor(at(x1, t), at(x1, t), beta[:, :], ALU.add).then_inc(s["x1_beta"], 1)

        @block.tensor
        def _(pe):
            def turn(t, b):
                pe.wait_ge(s["fresh"], t + 1)
                if not (isinstance(t, int) and t < 2):
                    pe.wait_ge(s["x2T_moved"], 2 * (t - 1))
                for i in range(2):
                    last = nc.tensor.transpose(p_T[b][:, i, :], fresh[:, b, i * P:(i + 1) * P], keep["ident"][:, :])
                last.then_inc(s["x2T"], 1)

            turn(0, 0)
            turn(1, 1)
            with nc.tensor.Fori(0, (TILES - 3) // 2) as i:
                for u in range(2):
                    turn(2 * i + 2 + u, u)
            turn(TILES - 1, 0)
            pe.wait_ge(s["mean"], 1)
            pe.wait_ge(s["wr"], 32)
            for i in range(2):
                last = nc.tensor.matmul(p_r[0:1, 0:NX], mean[:, i:i + 1], wr[:, i, :], start=(i == 0), stop=(i == 1))
            last.then_inc(s["logits"], 1)
            pe.wait_ge(s["ones"], 1)
            pe.wait_ge(s["small"], EXP_AT[2] + 3)
            nc.tensor.matmul(p_r[:, 64:64 + TOPK], r_["ones"][:, :], r_["w2"][:, :], start=True, stop=True).then_inc(s["share"], 1)

            def up(j, cols=2 * P):
                for n in range(TOPK * hidden):
                    k, f = n // hidden, n % hidden
                    if not (isinstance(j, int) and j == 0 and n < 4):
                        pe.wait_ge(s["act_h"], TOPK * hidden * j + n - 3)
                    for i in range(2):
                        x = x2T[:, i, j * 2 * P:j * 2 * P + cols] if isinstance(j, int) else x2T[:, i, bass.ds(j * 2 * P, cols)]
                        last = nc.tensor.matmul(p_up[n % 4][:, 0:cols], w1[:, k, i, f * P:(f + 1) * P], x, start=(i == 0), stop=(i == 1))
                    last.then_inc(s["up"], 1)

            def down(j, b, tiles=2):
                for u in range(tiles):
                    pe.wait_ge(s["act_h"], TOPK * hidden * (j + 1))
                    if not (isinstance(j, int) and j == 0):
                        pe.wait_ge(s["moe"], 2 * j + u - 1)
                    for n in range(TOPK * hidden):
                        k, f = n // hidden, n % hidden
                        last = nc.tensor.matmul(p_y[u][:, :], act_h[:, b, n, u * P:(u + 1) * P], w2[:, k, f, :], start=(n == 0), stop=(n == TOPK * hidden - 1))
                    last.then_inc(s["down"], 1)

            pe.wait_ge(s["expert"], 64 * TOPK)
            up(0)
            up(1)
            pe.wait_ge(s["w2_scaled"], TOPK)
            down(0, 0)
            with nc.tensor.Fori(0, (blocks - 3) // 2) as i:
                for u in range(2):
                    up(2 * i + 2 + u)
                    down(2 * i + 1 + u, 1 - u)
            up(blocks - 1, last_cols)
            down(blocks - 2, 1)
            down(blocks - 1, 0, 1)

        @block.scalar
        def _(act):
            act.wait_ge(s["eps"], 1)
            act.wait_ge(s["moments"], 6)
            nc.scalar.activation(std[:, :], moments[:, :, 1], ACT.Sqrt, bias=eps[:, 0:1]).then_inc(s["std"], 1)

            def move(t, b, cols=P):
                act.wait_ge(s["x2T"], t + 1)
                for i in range(2):
                    to = x2T[:, i, t * P:t * P + cols] if isinstance(t, int) else x2T[:, i, bass.ds(t * P, P)]
                    total_at = col_sums[:, i, t:t + 1] if isinstance(t, int) else col_sums[:, i, bass.ds(t, 1)]
                    nc.scalar.activation(to, p_T[b][:, i, 0:cols], ACT.Copy, accum_out=total_at).then_inc(s["x2T_moved"], 1)
                nc.scalar.copy(at(moe, t), fresh[:, b, :]).then_inc(s["x2_kept"], 1)

            act.wait_ge(s["pad"], 2)
            with nc.scalar.Fori(0, (TILES - 1) // 2) as i:
                for u in range(2):
                    move(2 * i + u, u)
            move(TILES - 1, 0, LASTROWS)
            act.wait_ge(s["fresh"], NT)
            nc.scalar.copy(moe[:, NT - 1, :], fresh[:, 1, :]).then_inc(s["x2_kept"], 1)
            for n in range(3):
                act.wait_ge(s["small"], EXP_AT[n])
                w = NX if n < 2 else TOPK
                nc.scalar.activation(r_["e"][:, 0:w], r_["d"][:, 0:w], ACT.Exp).then_inc(s["expo"], 1)

            def gelu(j, b, cols=2 * P):
                for n in range(TOPK * hidden):
                    act.wait_ge(s["up"], TOPK * hidden * j + n + 1)
                    if n == 0 and not (isinstance(j, int) and j < 2):
                        act.wait_ge(s["down"], 2 * (j - 1))
                    k, f = n // hidden, n % hidden
                    nc.scalar.activation(act_h[:, b, n, 0:cols], p_up[n % 4][:, 0:cols], ACT.Gelu,
                                         bias=b1[:, k, f:f + 1]).then_inc(s["act_h"], 1)

            act.wait_ge(s["expert"], 64 * TOPK)
            gelu(0, 0)
            gelu(1, 1)
            with nc.scalar.Fori(0, (blocks - 3) // 2) as i:
                for u in range(2):
                    gelu(2 * i + 2 + u, u)
            gelu(blocks - 1, 0, last_cols)

            act.wait_ge(s["moments2"], 6)
            nc.scalar.activation(std[:, 0:TILES], moments[:, 0:TILES, 1], ACT.Sqrt, bias=eps[:, 0:1]).then_inc(s["std2"], 1)
            act.wait_ge(s["shift"], 1)

            def normalize(t, b):
                if not (isinstance(t, int) and t < 2):
                    act.wait_ge(s["scaled"], t - 1)
                nc.scalar.activation(normed[:, b, :], at(moe, t), ACT.Identity, bias=at(shift, t), scale=at(rstd, t)).then_inc(s["normed"], 1)

            normalize(0, 0)
            normalize(1, 1)
            with nc.scalar.Fori(0, (TILES - 3) // 2) as i:
                for u in range(2):
                    normalize(2 * i + 2 + u, u)
            normalize(TILES - 1, 0)

        @block.vector
        def _(dve):
            nc.vector.tensor_scalar(denom[:, :, :], keep["acc"][:, :, :].rearrange("p t (h d) -> p t h d", h=H)[:, :, :, HD], 1e-10, None, ALU.max).then_inc(s["denom"], 1)
            dve.wait_ge(s["denom"], 1)
            nc.vector.reciprocal(inverse[:, :, :], denom[:, :, :]).then_inc(s["inverse"], 1)
            dve.wait_ge(s["inverse"], 1)

            def attend(t, b, first=False):
                if not first:
                    dve.wait_ge(s["x1"], t - 1)
                nc.vector.tensor_tensor(heads(fresh[:, b, :]), heads(at(keep["acc"], t))[:, :, 0:HD], spread(at(inverse, t), HD), ALU.mult).then_inc(s["gnn"], 1)

            def add_x(t, b):
                dve.wait_ge(s["gnn"], t + 1)
                dve.wait_ge(s["x_biased"], t + 1)
                nc.vector.tensor_tensor(at(x1, t), at(x1, t), fresh[:, b, :], ALU.add).then_inc(s["x1"], 1)

            def measure(t):
                dve.wait_ge(s["x1"], t + 1)
                nc.vector.bn_stats(at(stats, t), at(x1, t)).then_inc(s["stats"], 1)

            attend(0, 0, True)
            attend(1, 1, True)
            add_x(0, 0)
            with nc.vector.Fori(0, (NT - 2) // 2) as i:
                for u in range(2):
                    add_x(2 * i + 1 + u, 1 - u)
                    attend(2 * i + 2 + u, u)
                    measure(2 * i + u)
            add_x(NT - 1, 1)
            measure(NT - 2)
            measure(NT - 1)
            dve.wait_ge(s["stats"], NT)
            merge_moments(nc, dve, stats, halves, moments, s["moments"])
            dve.wait_ge(s["std"], 1)
            nc.vector.reciprocal(rstd[:, :, 0], std[:, :]).then_inc(s["rstd"], 1)
            dve.wait_ge(s["rstd"], 1)

            def normalize(t, b):
                if not (isinstance(t, int) and t < 2):
                    dve.wait_ge(s["x2T"], t - 1)
                    dve.wait_ge(s["x2_kept"], t - 1)
                mean_t = moments[:, t, 0:1] if isinstance(t, int) else moments[:, bass.ds(t, 1), 0]
                nc.vector.tensor_scalar(fresh[:, b, :], at(x1, t), mean_t, at(rstd, t), ALU.subtract, ALU.mult).then_inc(s["fresh"], 1)

            normalize(0, 0)
            normalize(1, 1)
            with nc.vector.Fori(0, (NT - 4) // 2) as i:
                for u in range(2):
                    normalize(2 * i + 2 + u, u)
            normalize(NT - 2, 0)
            dve.wait_ge(s["x2_kept"], NT - 2)
            dve.wait_ge(s["x2T"], NT - 2)
            nc.vector.tensor_scalar(fresh[:, 1, :], x1[:, NT - 1, :], moments[:, NT - 1, 0:1], rstd[:, NT - 1, :], ALU.subtract, ALU.mult).then_inc(s["fresh"], 1)

            dve.wait_ge(s["x2T_moved"], 2 * TILES)
            nc.vector.tensor_reduce(total[:, :], col_sums[:, :, :], AX.X, ALU.add).then_inc(s["total"], 1)
            dve.wait_ge(s["total"], 1)
            nc.vector.tensor_scalar(mean[:, :], total[:, :], 1.0 / N, None, ALU.mult).then_inc(s["mean"], 1)
            dve.wait_ge(s["logits"], 1)
            dve.wait_ge(s["wr"], 32)
            count = [0]

            def link(ins):
                count[0] += 1
                ins.then_inc(s["small"], 1)
                dve.wait_ge(s["small"], count[0])

            def softmax(to, of, w, n):
                link(nc.vector.tensor_reduce(r_["top"][:, :], of, AX.X, ALU.max))
                link(nc.vector.tensor_scalar(r_["d"][:, 0:w], of, r_["top"][:, 0:1], None, ALU.subtract))
                assert count[0] == EXP_AT[n]
                dve.wait_ge(s["expo"], n + 1)
                link(nc.vector.tensor_reduce(r_["sum"][:, :], r_["e"][:, 0:w], AX.X, ALU.add))
                link(nc.vector.reciprocal(r_["sum"][:, :], r_["sum"][:, :]))
                link(nc.vector.tensor_scalar(to, r_["e"][:, 0:w], r_["sum"][:, 0:1], None, ALU.mult))

            link(nc.vector.tensor_tensor(r_["logits"][:, :], p_r[0:1, 0:NX], r_["br"][:, :], ALU.add))
            softmax(r_["p"][:, :], r_["logits"][:, :], NX, 0)
            link(nc.vector.tensor_scalar(r_["load"][:, :], r_["p"][:, :], float(N), None, ALU.mult))
            link(nc.vector.reciprocal(r_["q"][:, :], r_["load"][:, :]))
            link(nc.vector.tensor_scalar(r_["q"][:, :], r_["q"][:, :], CAPACITY, None, ALU.mult))
            link(nc.vector.tensor_scalar(r_["over"][:, :], r_["load"][:, :], CAPACITY, None, ALU.is_gt))
            link(nc.vector.tensor_scalar(r_["under"][:, :], r_["load"][:, :], CAPACITY, None, ALU.is_le))
            link(nc.vector.tensor_scalar(r_["q"][:, :], r_["q"][:, :], 1.0, None, ALU.min))
            link(nc.vector.tensor_tensor(r_["q"][:, :], r_["q"][:, :], r_["over"][:, :], ALU.mult))
            link(nc.vector.tensor_tensor(r_["scale"][:, :], r_["q"][:, :], r_["under"][:, :], ALU.add))
            link(nc.vector.tensor_tensor(r_["t"][:, :], r_["p"][:, :], r_["scale"][:, :], ALU.mult))
            softmax(r_["p"][:, :], r_["t"][:, :], NX, 1)
            link(nc.vector.max(r_["best"][:, :], r_["p"][:, :]))
            link(nc.vector.max_index(r_["index"][:, :], r_["best"][:, :], r_["p"][:, :]))
            assert count[0] == INDEX_AT
            softmax(r_["w2"][:, :], r_["best"][:, 0:TOPK], TOPK, 2)
            dve.wait_ge(s["share"], 1)
            nc.vector.tensor_copy(share[:, :], p_r[:, 64:64 + TOPK]).then_inc(s["shared"], 1)
            dve.wait_ge(s["shared"], 1)
            dve.wait_ge(s["expert"], 64 * TOPK)
            for k in range(TOPK):
                nc.vector.tensor_scalar(w2[:, k, :, :], w2[:, k, :, :], share[:, k:k + 1], None, ALU.mult).then_inc(s["w2_scaled"], 1)
            nc.vector.tensor_scalar(b2_mix[:, :], b2[:, 0, :], share[:, 0:1], None, ALU.mult).then_inc(s["b2a"], 1)
            dve.wait_ge(s["b2a"], 1)
            nc.vector.scalar_tensor_tensor(b2_mix[:, :], b2[:, 1, :], share[:, 1:2], b2_mix[:, :], ALU.mult, ALU.add).then_inc(s["b2_mix"], 1)

            def gather_down(t, u):
                dve.wait_ge(s["down"], t + 1)
                dve.wait_ge(s["b2_added"], t + 1)
                nc.vector.tensor_tensor(at(moe, t), at(moe, t), p_y[u][:, :], ALU.add).then_inc(s["moe"], 1)
                dve.wait_ge(s["moe"], t + 1)
                nc.vector.bn_stats(at(stats, t), at(moe, t)).then_inc(s["stats2"], 1)

            with nc.vector.Fori(0, (TILES - 1) // 2) as i:
                for u in range(2):
                    gather_down(2 * i + u, u)
            gather_down(TILES - 1, 0)
            dve.wait_ge(s["stats2"], TILES)
            merge_moments(nc, dve, stats, halves, moments, s["moments2"])
            dve.wait_ge(s["std2"], 1)
            nc.vector.reciprocal(rstd[:, 0:TILES, 0], std[:, 0:TILES]).then_inc(s["rstd2"], 1)
            dve.wait_ge(s["rstd2"], 1)
            nc.vector.scalar_tensor_tensor(shift[:, 0:TILES, 0], moments[:, 0:TILES, 0], -1.0, rstd[:, 0:TILES, 0], ALU.mult, ALU.mult).then_inc(s["shift"], 1)
            dve.wait_ge(s["x1_beta"], NT)
            dve.wait_ge(s["x2_kept"], NT)

            def finish(t, b):
                dve.wait_ge(s["normed"], t + 1)
                if not (isinstance(t, int) and t < 2):
                    dve.wait_ge(s["result"], t - 1)
                nc.vector.tensor_tensor(fresh[:, b, :], normed[:, b, :], gamma[:, :], ALU.mult).then_inc(s["scaled"], 1)
                dve.wait_ge(s["scaled"], t + 1)
                nc.vector.tensor_tensor(at(x1, t), fresh[:, b, :], at(x1, t), ALU.add).then_inc(s["result"], 1)

            finish(0, 0)
            finish(1, 1)
            with nc.vector.Fori(0, (TILES - 3) // 2) as i:
                for u in range(2):
                    finish(2 * i + 2 + u, u)
            finish(TILES - 1, 0)


_INS = {"x": "x", "src": "src", "dst": "dst", "attr": "edge_attr_3", "W": "L0_gnn_W", "a_src": "L0_gnn_a_src",
        "a_dst": "L0_gnn_a_dst", "edge_W": "L0_gnn_edge_W", "edge_b": "L0_gnn_edge_b", "gnn_bias": "L0_gnn_bias",
        "Wr": "L0_ffn_Wr", "br": "L0_ffn_br", "W1": "L0_ffn_W1", "b1": "L0_ffn_b1", "W2": "L0_ffn_W2",
        "b2": "L0_ffn_b2", "gamma": "L0_ffn_gamma", "beta": "L0_ffn_beta"}


def build(nc, a, out):
    def dram(name, shape, dt):
        return nc.dram_tensor(name, shape, dt, kind="Internal").ap()

    scr = dict(rows=dram("node_rows", (NT * P, ROW), F32), parts=dram("node_parts", (NT, P, 3 * PART), BF16),
               edges=dram("edge_records", (NC, P, REC), F32), starts=dram("segment_starts", (NC, C * H, P), F32))
    with Scope(nc) as m:
        keep = dict(
            ident=m.sb("ident", [P, P]), identb=m.sb("identb", [P, P], BF16), node_at=m.sb("node_at", [P, P]),
            expander=m.sb("expander", [3 * KA, D], BF16), step_chunk=m.sb("step_chunk", [1, STEPS], I32),
            step_tile=m.sb("step_tile", [1, STEPS], I32), tile_base=m.sb("tile_base", [P, STEPS]),
            acc=m.sb("acc", [P, NT, ROW]), top=m.sb("top", [P, NT, H]),
        )
        prologue(nc, a, scr, keep)
        edge_loop(nc, scr, keep)
        epilogue(nc, a, keep, out)


def kernel(**inputs):
    import numpy as np
    import concourse.bacc as bacc
    from concourse.bass_utils import run_bass_kernel_spmd

    nc = bacc.Bacc("TRN2", target_bir_lowering=False, num_devices=1)
    arrays, args = {}, {}
    for short, name in _INS.items():
        v = np.ascontiguousarray(inputs[name])
        arrays["in_" + name] = v
        args[short] = nc.dram_tensor("in_" + name, v.shape, mybir.dt.from_np(v.dtype), kind="ExternalInput").ap()
    out = nc.dram_tensor("out_x", (N, D), F32, kind="ExternalOutput").ap()
    build(nc, args, out)
    r = run_bass_kernel_spmd(nc, [arrays], core_ids=[0])
    return r.results[0]["out_x"]
```

```python
from contextlib import ExitStack

import concourse.bass as bass
from concourse import mybir

F32, BF16, I32, U32 = mybir.dt.float32, mybir.dt.bfloat16, mybir.dt.int32, mybir.dt.uint32
ALU, ACT, AX = mybir.AluOpType, mybir.ActivationFunctionType, mybir.AxisListType

P = 128
N, E = 6250, 200000
D, H, HD = 256, 8, 32
EF = 3
FF, NX, TOPK = 512, 8, 2
LN_EPS = 1e-5
CAPACITY = float(-(-N * 5 // (4 * NX)))

NODE_RING = 4
TURN_A = 5
X_PIECES = 4

C = 8
CHUNK = P * C
NC = -(-E // CHUNK)
FULL = E // CHUNK
REST = E - FULL * CHUNK
TILES = -(-N // P)
STEPS = NC + TILES - 1
NT = TILES + TILES % 2
LASTROWS = N - (TILES - 1) * P
GROUPS = [(g, min(P, NC - g)) for g in range(0, NC, P)]

ROW = H * (HD + 1)
PART = D + H
KA = 12
KE = 3 * KA
REC = C * (3 + KE // 2)
DST, LAST, SRC, ATTR = 0, C, 2 * C, 3 * C
BIG = 1e30
PAD_DST = 1 << 20
assert C == 8 and len(GROUPS) == 2


def at(ap, t):
    return ap[:, t, :] if isinstance(t, int) else ap[:, bass.ds(t, 1), :].rearrange("p o n -> p (o n)")


def block_of(ap, t):
    return ap[t, :, :] if isinstance(t, int) else ap[bass.ds(t, 1), :, :].rearrange("o p n -> p (o n)")


def merge_moments(nc, dve, stats, halves, moments, made, rows=(0, NT), before=0):
    r = slice(*rows)
    m0, v0, m1, v1 = (stats[:, r, i] for i in (1, 2, 4, 5))
    nc.vector.tensor_tensor(halves[:, 0, r], m0, m1, ALU.add).then_inc(made, 1)
    nc.vector.tensor_tensor(halves[:, 1, r], m0, m1, ALU.subtract).then_inc(made, 1)
    nc.vector.tensor_tensor(halves[:, 2, r], v0, v1, ALU.add).then_inc(made, 1)
    dve.wait_ge(made, 6 * before + 3)
    nc.vector.tensor_scalar(moments[:, r, 0], halves[:, 0, r], 0.5, None, ALU.mult)
    nc.vector.scalar_tensor_tensor(halves[:, 3, r], halves[:, 1, r], 0.25, halves[:, 1, r], ALU.mult, ALU.mult).then_inc(made, 1)
    dve.wait_ge(made, 6 * before + 4)
    nc.vector.scalar_tensor_tensor(moments[:, r, 1], halves[:, 2, r], 1.0 / D, halves[:, 3, r], ALU.mult, ALU.add).then_inc(made, 2)


def spread(ap, n):
    return ap.unsqueeze(ap.ndim).broadcast_to([*ap.shape, n])


class Scope(ExitStack):

    def __init__(self, nc):
        super().__init__()
        self.nc = nc

    def sb(self, name, shape, dt=F32):
        return self.enter_context(self.nc.sbuf_tensor(name, shape, dt))

    def ps(self, name, shape, dt=F32):
        return self.enter_context(self.nc.psum_tensor(name, shape, dt))

    def sem(self, name):
        return self.enter_context(self.nc.semaphore(name))


def prologue(nc, a, scr, keep):
    with Scope(nc) as m:
        x_all = keep["acc"][:, :, 0:D]
        dst_rows = m.sb("dst_rows", [P, CHUNK], I32)
        src_rows = m.sb("src_rows", [P, CHUNK], I32)
        attr_rows = m.sb("attr_rows", [P, CHUNK * EF])
        rec = m.sb("rec", [P, P, REC])
        start_rows = m.sb("start_rows", [P, C, P])
        changed = m.sb("changed", [P, P, C])
        steps_at = m.sb("steps_at", [P, STEPS])
        started = m.sb("started", [P, 2, STEPS])
        tile_edges = m.sb("tile_edges", [P, TILES - 1])
        reached = m.sb("reached", [P, TILES - 1])
        chunk_tile = m.sb("chunk_tile", [P, 2])
        chunk_start = m.sb("chunk_start", [P, 2])
        chunk_no = m.sb("chunk_no", [P, 2])
        step_c = m.sb("step_c", [P, STEPS])
        step_t = m.sb("step_t", [P, STEPS])
        ones = m.sb("ones", [P, P])
        stats = m.sb("stats", [P, NT, 6])
        moments = m.sb("moments", [P, NT, 2])
        halves = m.sb("halves", [P, 4, NT])
        std = m.sb("std", [P, NT])
        rstd = m.sb("rstd", [P, NT, 1])
        eps = m.sb("eps", [P, 1])
        xn = m.sb("xn", [P, 2, D])
        xnT = m.sb("xnT", [P, 2, 2, P])
        w_nat = m.sb("w_nat", [P, 2, D])
        w_ext = m.sb("w_ext", [P, 2, D + 2 * H])
        a_diag = m.sb("a_diag", [P, 2, 2, H])
        a_col = m.sb("a_col", [P, 2, 2])
        out_rows = m.sb("out_rows", [P, NODE_RING, ROW])
        dst_score = m.sb("dst_score", [P, NODE_RING, H])
        out_parts = m.sb("out_parts", [P, NODE_RING, 3 * PART], BF16)
        part_left = m.sb("part_left", [P, PART])
        enc_f = m.sb("enc_f", [KA, D])
        enc_left = m.sb("enc_left", [KA, D])
        enc_p = m.sb("enc_p", [KA, 3, D], BF16)
        p_xT = [m.ps(f"p_xT{i}", [P, 2, P]) for i in range(2)]
        p_h = [m.ps(f"p_h{i}", [P, D + 2 * H]) for i in range(2)]
        p_w = m.ps("p_w", [P, 512])
        p_v = m.ps("p_v", [P, 4 * H])
        p_s = m.ps("p_s", [P, STEPS])

        names = """w_loaded enc_loaded zeros_made ones_made consts_made ident_made row_pad enc_split enc_moved rec_made
            rec_stored last_stored started_at counted rec_copied diag_made wT_made v_made
            wext_made stats_made moments_made std_made rstd_made xn_made xT_made xT_moved h_made rows_made
            hi_made left_made mid_made parts_made dst_made chg_made a_hi a_left a_mid reached_s ctile_s cfix_s cstart_s
            tables_s rec_const zero_acc""".split()
        s = {n: m.sem("s_" + n) for n in names}
        s_edges = [m.sem(f"s_edges_loaded{g}") for g in range(len(GROUPS))]
        s_stored = [m.sem(f"s_node_stored{i}") for i in range(NODE_RING)]
        s_x = [m.sem(f"s_x_loaded{i}") for i in range(X_PIECES)]
        piece = (TILES - 1) // X_PIECES
        assert piece * X_PIECES == TILES - 1 and piece % 4 == 0
        rec_i = rec[:, :, :].bitcast(I32)
        attr_w = rec[:, :, :].bitcast(BF16)[:, :, 2 * ATTR:].rearrange("c p (k j w) -> c p k j w", k=C, j=3)
        attr_p = rec[:, :, :].bitcast(BF16)[:, :, 2 * ATTR:].rearrange("c p (k j i f) -> c p k j i f", k=C, j=3, i=3)[:, :, :, 0, :, :]

        block = m.enter_context(nc.Block())

        def node_loop(engine, first, step, between, last_step):
            def turns(a, b):
                with engine.Fori(0, b - a) as i:
                    for u in range(NODE_RING):
                        step(i * NODE_RING + a * NODE_RING + u, u, i + a)

            first()
            for t in range(NODE_RING):
                step(t, t, 0)
            turns(1, 1 + TURN_A)
            between()
            turns(1 + TURN_A, last_step // NODE_RING)
            for t in range(last_step // NODE_RING * NODE_RING, last_step):
                step(t, t % NODE_RING, t // NODE_RING)

        def early(t, n):
            return isinstance(t, int) and t < n

        @block.sync
        def _(sp):
            def load_edges(g):
                c0, n = GROUPS[g]
                whole = min(n, FULL - c0)
                for rows, name, w in ((dst_rows, "dst", 1), (src_rows, "src", 1), (attr_rows, "attr", EF)):
                    flat = a[name] if w == 1 else a[name].rearrange("e f -> (e f)")
                    sp.dma_start(rows[0:whole, :], flat[c0 * CHUNK * w:(c0 + whole) * CHUNK * w]
                                 .rearrange("(c e) -> c e", c=whole)).then_inc(s_edges[g], 16)
                    if c0 + n > FULL:
                        sp.dma_start(rows[whole:whole + 1, 0:REST * w], flat[FULL * CHUNK * w:E * w]
                                     .rearrange("(c e) -> c e", c=1)).then_inc(s_edges[g], 16)

            sp.dma_start(w_nat[:, :, :], a["W"].rearrange("(c p) n -> p c n", p=P)).then_inc(s["w_loaded"], 16)
            for half in range(2):
                for i, name in enumerate(("a_src", "a_dst")):
                    v = a[name].rearrange("h (d o) -> (h d) o", o=1)[half * P:(half + 1) * P, :]
                    sp.dma_start(a_col[:, half, i:i + 1], v).then_inc(s["w_loaded"], 16)
            load_edges(0)
            for i in range(X_PIECES):
                t0, t1 = i * piece, (i + 1) * piece
                sp.dma_start(x_all[:, t0:t1, :], a["x"][t0 * P:t1 * P, :].rearrange("(t p) n -> p t n", p=P)).then_inc(s_x[i], 16)
            sp.wait_ge(s["zeros_made"], 1)
            sp.dma_start(x_all[0:LASTROWS, TILES - 1, :], a["x"][(TILES - 1) * P:N, :]).then_inc(s_x[X_PIECES - 1], 16)
            for g in range(1, len(GROUPS)):
                sp.wait_ge(s["row_pad"], 1)
                load_edges(g)

            def store(t, b, turn):
                sp.wait_ge(s["parts_made"], t + 1)
                sp.dma_start(block_of(scr["rows"].rearrange("(t p) n -> t p n", p=P), t), out_rows[:, b, :]).then_inc(s_stored[b], 16)
                sp.dma_start(block_of(scr["parts"], t), out_parts[:, b, :]).then_inc(s_stored[b], 16)

            node_loop(nc.sync, lambda: None, store, lambda: None, NT)
            for b in range(NODE_RING):
                sp.wait_ge(s_stored[b], 32 * len(range(b, NT, NODE_RING)))

        @block.gpsimd
        def _(pool):
            nc.gpsimd.memset(x_all[:, TILES - 1:NT, :], 0.0).then_inc(s["zeros_made"], 1)
            nc.gpsimd.memset(keep["ident"][:, :], 0.0).then_inc(s["ident_made"], 1)
            nc.gpsimd.memset(keep["identb"][:, :], 0.0).then_inc(s["ident_made"], 1)
            pool.wait_ge(s["ident_made"], 2)
            for one in (keep["ident"], keep["identb"]):
                nc.gpsimd.affine_select(out=one[:, :], in_=one[:, :], compare_op=ALU.not_equal, fill=1.0, base=0,
                                        pattern=[[-1, P]], channel_multiplier=1).then_inc(s["ident_made"], 1)
            nc.gpsimd.memset(ones[:, :], 1.0).then_inc(s["ones_made"], 1)
            nc.gpsimd.memset(eps[:, :], LN_EPS).then_inc(s["consts_made"], 1)
            for i in range(3):
                for f in range(EF):
                    pool.dma_start(enc_f[4 * i + f:4 * i + f + 1, :], a["edge_W"].rearrange("n f -> f n")[f:f + 1, :],
                                   allow_slow_non_contiguous=True).then_inc(s["enc_loaded"], 16)
                pool.dma_start(enc_f[4 * i + EF:4 * i + 4, :], a["edge_b"].rearrange("(o n) -> o n", o=1)).then_inc(s["enc_loaded"], 16)
            nc.gpsimd.iota(steps_at[:, :], pattern=[[1, STEPS]], base=0, channel_multiplier=0,
                           allow_small_or_imprecise_dtypes=True).then_inc(s["consts_made"], 1)
            nc.gpsimd.iota(tile_edges[:, :], pattern=[[P, TILES - 1]], base=P, channel_multiplier=0,
                           allow_small_or_imprecise_dtypes=True).then_inc(s["consts_made"], 1)
            nc.gpsimd.iota(keep["node_at"][:, :], pattern=[[1, P]], base=0, channel_multiplier=0,
                           allow_small_or_imprecise_dtypes=True).then_inc(s["consts_made"], 1)
            for g, (c0, n) in enumerate(GROUPS):
                nc.gpsimd.iota(chunk_no[:, g:g + 1], pattern=[[0, 1]], base=c0, channel_multiplier=1,
                               allow_small_or_imprecise_dtypes=True).then_inc(s["consts_made"], 1)
            pool.wait_ge(s["enc_split"], 4)
            for j in range(3):
                pool.dma_start(keep["expander"][KA * j:KA * (j + 1), :], enc_p[:, j, :]).then_inc(s["enc_moved"], 16)
            pool.wait_ge(s["enc_moved"], 48)
            c0, n = GROUPS[1]
            pool.wait_ge(s["rec_made"], 2)
            nc.gpsimd.tensor_copy(attr_w[0:n, :, :, 2, :], attr_w[0:n, :, :, 0, :]).then_inc(s["rec_copied"], 1)
            pool.wait_ge(s["rec_copied"], 4)
            pool.dma_start(scr["edges"][c0:c0 + n, :, :], rec[0:n, :, :]).then_inc(s["last_stored"], 16)
            for t0, t1 in ((0, NT // 2), (NT // 2, NT)):
                pool.wait_ge(s["xn_made"], t1)
                nc.gpsimd.memset(keep["acc"][:, t0:t1, :], 0.0).then_inc(s["zero_acc"], 1)
            pool.wait_ge(s["zero_acc"], 3)
            pool.wait_ge(s["last_stored"], 16)

        @block.tensor
        def _(pe):
            pe.wait_ge(s["w_loaded"], 80)
            pe.wait_ge(s["ident_made"], 4)
            for i in range(2):
                for o in range(2):
                    last = nc.tensor.transpose(p_w[:, (2 * i + o) * P:(2 * i + o + 1) * P],
                                               w_nat[:, o, i * P:(i + 1) * P], keep["ident"][:, :])
            last.then_inc(s["wT_made"], 1)
            pe.wait_ge(s["diag_made"], 2)
            for i in range(2):
                for o in range(2):
                    last = nc.tensor.matmul(p_v[:, i * 2 * H:(i + 1) * 2 * H], w_nat[:, o, i * P:(i + 1) * P],
                                            a_diag[:, o, :, :].rearrange("p i h -> p (i h)"), start=(o == 0), stop=(o == 1))
            last.then_inc(s["v_made"], 1)

            def transpose_tile(t, b):
                pe.wait_ge(s["xn_made"], t + 1)
                if not early(t, 2):
                    pe.wait_ge(s["xT_moved"], t - 1)
                for i in range(2):
                    last = nc.tensor.transpose(p_xT[b][:, i, :], xn[:, b, i * P:(i + 1) * P], keep["ident"][:, :])
                last.then_inc(s["xT_made"], 1)

            def project_tile(t, b):
                pe.wait_ge(s["xT_moved"], t + 1)
                if not early(t, 2):
                    pe.wait_ge(s["rows_made"], t - 1)
                for i in range(2):
                    last = nc.tensor.matmul(p_h[b][:, :], xnT[:, b, i, :], w_ext[:, i, :], start=(i == 0), stop=(i == 1))
                last.then_inc(s["h_made"], 1)

            def first():
                transpose_tile(0, 0)
                transpose_tile(1, 1)
                project_tile(0, 0)

            def step(t, b, turn):
                transpose_tile(t + 2, b % 2)
                project_tile(t + 1, 1 - b % 2)

            pe.wait_ge(s["wext_made"], 2)
            node_loop(nc.tensor, first, step, lambda: None, NT - 2)
            project_tile(NT - 1, (NT - 1) % 2)
            pe.wait_ge(s["ones_made"], 1)
            for g, (c0, n) in enumerate(GROUPS):
                pe.wait_ge(s["started_at"], g + 1)
                nc.tensor.matmul(p_s[:, :], ones[0:n, :], started[0:n, g, :], start=(g == 0),
                                 stop=(g == len(GROUPS) - 1)).then_inc(s["counted"], 1)

        @block.scalar
        def _(act):
            def records(g):
                c0, n = GROUPS[g]
                act.wait_ge(s["rec_made"], g + 1)
                for i in range(1, 3 - g):
                    nc.scalar.copy(attr_w[0:n, :, :, i, :], attr_w[0:n, :, :, 0, :]).then_inc(s["rec_copied"], 1)
                for h in range(H):
                    act.dma_start(scr["starts"][c0:c0 + n, :, :].rearrange("c (k h) p -> c k h p", h=H)[:, :, h, :],
                                  start_rows[0:n, :, :]).then_inc(s["rec_stored"], 16)
                if g == 0:
                    act.wait_ge(s["rec_copied"], 2)
                    act.dma_start(scr["edges"][c0:c0 + n, :, :], rec[0:n, :, :]).then_inc(s["rec_stored"], 16)

            def move_transposed(t, b):
                act.wait_ge(s["xT_made"], t + 1)
                if not early(t, 2):
                    act.wait_ge(s["h_made"], t - 1)
                nc.scalar.copy(xnT[:, b, :, :], p_xT[b][:, :, :]).then_inc(s["xT_moved"], 1)

            def make_rows(t, b, stored):
                act.wait_ge(s["h_made"], t + 1)
                if not early(t, NODE_RING):
                    act.wait_ge(s_stored[b], stored * 32)
                v = out_rows[:, b, :].rearrange("p (h d) -> p h d", h=H)
                nc.scalar.copy(v[:, :, 0:HD], p_h[b % 2][:, 0:D].rearrange("p (h d) -> p h d", h=H))
                nc.scalar.copy(v[:, :, HD], p_h[b % 2][:, D:D + H])
                nc.scalar.copy(dst_score[:, b, :], p_h[b % 2][:, D + H:D + 2 * H]).then_inc(s["rows_made"], 1)

            def first():
                move_transposed(0, 0)
                move_transposed(1, 1)
                make_rows(0, 0, 0)

            def step(t, b, turn):
                move_transposed(t + 2, b % 2)
                nxt = (b + 1) % NODE_RING
                make_rows(t + 1, nxt, turn + 1 if nxt == 0 else turn)

            records(0)
            act.wait_ge(s["moments_made"], 6)
            act.wait_ge(s["consts_made"], 1)
            nc.scalar.activation(std[:, :], moments[:, :, 1], ACT.Sqrt, bias=eps[:, 0:1]).then_inc(s["std_made"], 1)
            node_loop(nc.scalar, first, step, lambda: records(1), NT - 2)
            make_rows(NT - 1, (NT - 1) % NODE_RING, (NT - 1) // NODE_RING)
            act.wait_ge(s["rec_stored"], 16 * (1 + 2 * H))

        @block.vector
        def _(dve):
            nc.vector.memset(keep["top"][:, :, :], -BIG).then_inc(s["zero_acc"], 1)
            nc.vector.memset(a_diag[:, :, :, :], 0.0).then_inc(s["diag_made"], 1)
            dve.wait_ge(s["w_loaded"], 80)
            dve.wait_ge(s["diag_made"], 1)
            for half in range(2):
                for q in range(P // HD):
                    last = nc.vector.tensor_copy(a_diag[q * HD:(q + 1) * HD, half, :, half * (P // HD) + q],
                                                 a_col[q * HD:(q + 1) * HD, half, :])
            last.then_inc(s["diag_made"], 1)
            nc.vector.memset(attr_p[:, :, :, 1, EF], 0.0).then_inc(s["rec_const"], 1)
            nc.vector.memset(attr_p[:, :, :, 2, EF], 0.0).then_inc(s["rec_const"], 1)
            nc.vector.memset(attr_p[:, :, :, 0, EF], 1.0).then_inc(s["rec_const"], 1)
            dve.wait_ge(s["consts_made"], 4 + len(GROUPS))

            def edge_records(g):
                c0, n = GROUPS[g]
                dve.wait_ge(s_edges[g], 96 if c0 + n > FULL else 48)
                if g:
                    dve.wait_ge(s["rec_stored"], 16 * (1 + H) * g)
                dst = rec[0:n, :, DST:DST + C]
                nc.vector.tensor_copy(dst, dst_rows[0:n, :].rearrange("c (p k) -> c p k", k=C)).then_inc(s["dst_made"], 1)
                nc.vector.tensor_copy(rec_i[0:n, :, SRC:SRC + C], src_rows[0:n, :].rearrange("c (p k) -> c p k", k=C))
                dve.wait_ge(s["dst_made"], g + 1)
                ch = changed[0:n, 0:P - 1, :]
                nc.vector.tensor_tensor(ch, dst[:, 1:P, :], dst[:, 0:P - 1, :], ALU.not_equal).then_inc(s["chg_made"], 1)
                nc.vector.tensor_scalar(reached[0:n, :], tile_edges[0:n, :], rec[0:n, 0, 0:1], None, ALU.is_le).then_inc(s["reached_s"], 1)
                av = attr_rows[0:n, :].rearrange("c (p k f) -> c p k f", k=C, f=EF)
                nc.vector.tensor_copy(attr_p[0:n, :, :, 0, 0:EF], av).then_inc(s["a_hi"], 1)
                dve.wait_ge(s["chg_made"], g + 1)
                nc.vector.tensor_copy(rec[0:n, 0:P - 1, LAST:LAST + C], ch)
                nc.vector.memset(rec[0:n, P - 1, LAST:LAST + C], 1.0)
                nc.vector.memset(start_rows[0:n, :, 0:1], -BIG)
                nc.vector.tensor_scalar(start_rows[0:n, :, 1:P].rearrange("c k p -> c p k"), ch, -BIG, None, ALU.mult)
                dve.wait_ge(s["reached_s"], g + 1)
                nc.vector.tensor_reduce(chunk_tile[0:n, g:g + 1], reached[0:n, :], AX.X, ALU.add).then_inc(s["ctile_s"], 1)
                dve.wait_ge(s["ctile_s"], g + 1)
                if g == 0:
                    nc.vector.memset(chunk_tile[0:1, 0:1], 0.0).then_inc(s["cfix_s"], 1)
                    dve.wait_ge(s["cfix_s"], 1)
                nc.vector.tensor_tensor(chunk_start[0:n, g:g + 1], chunk_tile[0:n, g:g + 1], chunk_no[0:n, g:g + 1], ALU.add).then_inc(s["cstart_s"], 1)
                dve.wait_ge(s["a_hi"], g + 1)
                nc.vector.tensor_tensor(av, av, attr_p[0:n, :, :, 0, 0:EF], ALU.subtract).then_inc(s["a_left"], 1)
                dve.wait_ge(s["cstart_s"], g + 1)
                nc.vector.tensor_scalar(started[0:n, g, :], steps_at[0:n, :], chunk_start[0:n, g:g + 1], None, ALU.is_ge).then_inc(s["started_at"], 1)
                dve.wait_ge(s["a_left"], g + 1)
                nc.vector.tensor_copy(attr_p[0:n, :, :, 1, 0:EF], av).then_inc(s["a_mid"], 1)
                dve.wait_ge(s["a_mid"], g + 1)
                dve.wait_ge(s["rec_const"], 3)
                nc.vector.tensor_tensor(attr_p[0:n, :, :, 2, 0:EF], av, attr_p[0:n, :, :, 1, 0:EF], ALU.subtract).then_inc(s["rec_made"], 1)
                if g == 0:
                    dve.wait_ge(s["rec_made"], 1)
                    nc.vector.memset(dst_rows[:, :], PAD_DST)
                    nc.vector.memset(src_rows[:, :], 0)
                    nc.vector.memset(attr_rows[:, :], 0.0).then_inc(s["row_pad"], 1)
            edge_records(0)
            dve.wait_ge(s["wT_made"], 1)
            nc.vector.tensor_copy(w_ext[:, :, 0:D], p_w[:, :].rearrange("p (i n) -> p i n", i=2)).then_inc(s["wext_made"], 1)
            dve.wait_ge(s["v_made"], 1)
            nc.vector.tensor_copy(w_ext[:, :, D:D + 2 * H], p_v[:, :].rearrange("p (i n) -> p i n", i=2)).then_inc(s["wext_made"], 1)
            dve.wait_ge(s["enc_loaded"], 16 * 3 * (EF + 1))
            nc.vector.tensor_copy(enc_p[:, 0, :], enc_f[:, :]).then_inc(s["enc_split"], 1)
            dve.wait_ge(s["enc_split"], 1)
            nc.vector.tensor_tensor(enc_left[:, :], enc_f[:, :], enc_p[:, 0, :], ALU.subtract).then_inc(s["enc_split"], 1)
            dve.wait_ge(s["enc_split"], 2)
            nc.vector.tensor_copy(enc_p[:, 1, :], enc_left[:, :]).then_inc(s["enc_split"], 1)
            dve.wait_ge(s["enc_split"], 3)
            nc.vector.tensor_tensor(enc_p[:, 2, :], enc_left[:, :], enc_p[:, 1, :], ALU.subtract).then_inc(s["enc_split"], 1)

            def measure(t):
                nc.vector.bn_stats(at(stats, t), at(x_all, t)).then_inc(s["stats_made"], 1)

            for i in range(X_PIECES):
                dve.wait_ge(s_x[i], 16 if i < X_PIECES - 1 else 32)
                with nc.vector.Fori(0, piece // 4) as j:
                    for u in range(4):
                        measure(j * 4 + i * piece + u)
            for t in range(TILES - 1, NT):
                measure(t)
            dve.wait_ge(s["stats_made"], NT)
            merge_moments(nc, dve, stats, halves, moments, s["moments_made"])
            dve.wait_ge(s["std_made"], 1)
            nc.vector.reciprocal(rstd[:, :, 0], std[:, :]).then_inc(s["rstd_made"], 1)
            dve.wait_ge(s["rstd_made"], 1)

            def normalize(t, b):
                if not early(t, 2):
                    dve.wait_ge(s["xT_made"], t - 1)
                mean = moments[:, t, 0:1] if isinstance(t, int) else moments[:, bass.ds(t, 1), 0]
                nc.vector.tensor_scalar(xn[:, b, :], at(x_all, t), mean, at(rstd, t), ALU.subtract, ALU.mult).then_inc(s["xn_made"], 1)

            def make_parts(t, b, stored):
                dve.wait_ge(s["rows_made"], t + 1)
                if not early(t, NODE_RING):
                    dve.wait_ge(s_stored[b], stored * 32)
                o = out_parts[:, b, :].rearrange("p (i n) -> p i n", i=3)
                h_v = out_rows[:, b, :].rearrange("p (h d) -> p h d", h=H)[:, :, 0:HD]
                hi_v = o[:, 0, 0:D].rearrange("p (h d) -> p h d", h=H)
                nc.vector.tensor_copy(hi_v, h_v).then_inc(s["hi_made"], 1)
                nc.vector.tensor_copy(o[:, 0, D:PART], dst_score[:, b, :]).then_inc(s["hi_made"], 1)
                dve.wait_ge(s["hi_made"], 2 * t + 2)
                if not early(t, 1):
                    dve.wait_ge(s["parts_made"], t)
                nc.vector.tensor_tensor(part_left[:, 0:D].rearrange("p (h d) -> p h d", h=H), h_v, hi_v, ALU.subtract).then_inc(s["left_made"], 1)
                nc.vector.tensor_tensor(part_left[:, D:PART], dst_score[:, b, :], o[:, 0, D:PART], ALU.subtract).then_inc(s["left_made"], 1)
                dve.wait_ge(s["left_made"], 2 * t + 2)
                nc.vector.tensor_copy(o[:, 1, :], part_left[:, :]).then_inc(s["mid_made"], 1)
                dve.wait_ge(s["mid_made"], t + 1)
                nc.vector.tensor_tensor(o[:, 2, :], part_left[:, :], o[:, 1, :], ALU.subtract).then_inc(s["parts_made"], 1)

            def first():
                normalize(0, 0)
                normalize(1, 1)

            def step(t, b, turn):
                normalize(t + 2, b % 2)
                make_parts(t, b, turn)

            node_loop(nc.vector, first, step, lambda: edge_records(1), NT - 2)
            for t in range(NT - 2, NT):
                make_parts(t, t % NODE_RING, t // NODE_RING)

            dve.wait_ge(s["counted"], len(GROUPS))
            nc.vector.tensor_scalar(step_c[:, :], p_s[:, :], -1.0, None, ALU.add).then_inc(s["tables_s"], 1)
            dve.wait_ge(s["tables_s"], 1)
            nc.vector.tensor_tensor(step_t[:, :], steps_at[:, :], step_c[:, :], ALU.subtract).then_inc(s["tables_s"], 1)
            nc.vector.tensor_copy(keep["step_chunk"][:, :], step_c[0:1, :]).then_inc(s["tables_s"], 1)
            dve.wait_ge(s["tables_s"], 2)
            nc.vector.tensor_copy(keep["step_tile"][:, :], step_t[0:1, :]).then_inc(s["tables_s"], 1)
            nc.vector.tensor_scalar(keep["tile_base"][:, :], step_t[:, :], float(P), None, ALU.mult).then_inc(s["tables_s"], 1)
            dve.wait_ge(s["tables_s"], 5)
            dve.wait_ge(s["zero_acc"], 3)


RING = 4
PAIRS = C // 2


class Step:

    def __init__(self, s, slot, turn):
        self.s, self.slot, self.turn = s, slot, turn
        self.parity = slot % 2

    def next(self):
        wraps = self.slot == RING - 1
        return Step(self.s + 1, (self.slot + 1) % RING, self.turn + 1 if wraps else self.turn)

    def prev(self):
        wraps = self.slot == 0
        return Step(self.s - 1, (self.slot - 1) % RING, self.turn - 1 if wraps else self.turn)

    def column(self, ap):
        return ap[:, self.s:self.s + 1] if isinstance(self.s, int) else ap[:, bass.ds(self.s, 1)]

    def since(self, n):
        return not isinstance(self.s, int) or self.s >= n


def edge_loop(nc, a, scr, keep):
    with Scope(nc) as m:
        rec = m.sb("rec_in", [P, RING, REC])
        rec_i = rec[:, :, :].bitcast(I32)
        rec_b = rec[:, :, :].bitcast(BF16)
        starts = m.sb("starts_in", [C * H, RING, P])
        node = m.sb("node_in", [P, RING, 3 * PART], BF16)
        src = m.sb("src_in", [P, RING, C, ROW])
        local = m.sb("local", [P, 2, C])
        away = m.sb("away", [P, 4 * P])
        hot = m.sb("hot", [P, 2, C, P])
        hotb = m.sb("hotb", [P, RING, C, P], BF16)
        hotT = m.sb("hotT", [P, RING, C * P], BF16)
        attrT = m.sb("attrT", [KE, 2, C * P], BF16)
        enc = m.sb("enc", [P, 2, 2 * D])
        prod = m.sb("prod", [P, C, H, HD + 2])
        dots = m.sb("dots", [P, 2, C * H])
        score = m.sb("score", [P, 2, P])
        running = m.sb("running", [P, P])
        lasts = m.sb("lasts", [P, C, H])
        lasts_left = m.sb("lasts_left", [P, C, H])
        lasts_p = m.sb("lasts_p", [P, 3, C, H + 1], BF16)
        absent = m.sb("absent", [P, C])
        masked = m.sb("masked", [P, C, H])
        chunk_top = m.sb("chunk_top", [P, H])
        new_top = m.sb("new_top", [P, H])
        drop = m.sb("drop", [P, H])
        keep_by = m.sb("keep_by", [P, 2, H])
        top_left = m.sb("top_left", [P, H])
        top_p = m.sb("top_p", [P, 3, H], BF16)
        below = m.sb("below", [P, C * H])
        capped = m.sb("capped", [P, C * H])
        weight = m.sb("weight", [P, C * H])
        weighted = m.sb("weighted", [P, C, ROW])
        scaled = m.sb("scaled", [P, ROW])

        p_enc = [m.ps(f"p_enc{i}", [P, 2 * D]) for i in range(2)]
        p_dst = [m.ps(f"p_dst{i}", [P, 2 * D]) for i in range(2)]
        p_turned = m.ps("p_turned", [P, 2, 4, P], BF16)
        p_chain = m.ps("p_chain", [P, 512])
        p_scores = m.ps("p_scores", [P, 512])
        p_sums = m.ps("p_sums", [P, 512])
        p_score = p_scores[:, 0:C * H]
        p_turn, p_attrT = p_turned[:, 0, :, :], p_turned[0:KE, 1, :, :]
        p_scoreT, p_back = p_chain[:, 0:P], p_chain[:, P:2 * P]
        p_lasts = p_back[:, 0:C * H]
        p_top = p_chain[:, 256:256 + C * (H + 1)].rearrange("p (k h) -> p k h", k=C)
        p_sum, p_ref = p_sums[:, 0:ROW], p_sums[:, 384:384 + C * H]

        s_loaded = [m.sem(f"s_loaded{i}") for i in range(RING)]
        s_gathered = [m.sem(f"s_gathered{i}") for i in range(RING)]
        names = """x_pad waited_by_pe waited_by_pool zeros local away hotb hot turned attr_moved hot_moved enc dst_picked relu prod dst_score src_score dots score
            scoreT running lasts_back lasts lasts_hi lasts_left lasts_mid lasts_parts chunk_tops absent masked chunk_top new_top drop top_hi top_left top_mid
            top_parts top_kept kept refs below capped weight weight_row weighted sums scaled merged""".split()
        s = {n: m.sem("s_" + n) for n in names}

        block = m.enter_context(nc.Block())

        def loop(engine, body, first, last, last_steps=2):
            def straight(k):
                return Step(k, k % RING, k // RING)

            first()
            for k in range(1, RING):
                body(straight(k))
            turns = (STEPS - last_steps - RING) // RING
            with engine.Fori(0, turns) as i:
                for u in range(RING):
                    body(Step(i * RING + RING + u, u, i + 1))
            for k in range((turns + 1) * RING, STEPS - last_steps):
                body(straight(k))
            last(straight(STEPS - 1))

        first_step = Step(0, 0, 0)

        @block.sync
        def _(sp):
            def load(q):
                chunk = nc.sync.value_load(q.column(keep["step_chunk"]), min_val=0, max_val=NC - 1)
                tile = nc.sync.value_load(q.column(keep["step_tile"]), min_val=0, max_val=TILES - 1)
                if q.since(RING):
                    sp.wait_ge(s["refs"], q.s - RING + 1)
                sp.dma_start(rec[:, q.slot, :], block_of(scr["edges"], chunk)).then_inc(s_loaded[q.slot], 16)
                sp.dma_start(node[:, q.slot, :], block_of(scr["parts"], tile)).then_inc(s_loaded[q.slot], 16)
                sp.dma_start(starts[:, q.slot, :], block_of(scr["starts"], chunk)).then_inc(s_loaded[q.slot], 16)

            def last(q):
                load(q)
                full = (TILES - 1) * P
                sp.dma_start(keep["x1"][:, 0:TILES - 1, :], a["x"][0:full, :].rearrange("(t p) n -> p t n", p=P)).then_inc(keep["x_loaded"], 16)
                sp.wait_ge(s["x_pad"], 1)
                sp.dma_start(keep["x1"][0:LASTROWS, TILES - 1, :], a["x"][full:N, :]).then_inc(keep["x_loaded"], 16)

            loop(nc.sync, load, lambda: load(first_step), last, 1)

        @block.gpsimd
        def _(pool):
            def scale_sums(p):
                tile = nc.gpsimd.value_load(p.column(keep["step_tile"]), min_val=0, max_val=TILES - 1)
                acc = at(keep["acc"], tile)
                pool.wait_ge(s["weighted"], 2 * (p.s + 1))
                nc.gpsimd.sem_inc(s["waited_by_pool"], 1)
                pool.wait_ge(s["kept"], p.s + 1)
                nc.gpsimd.sem_inc(s["waited_by_pool"], 1)
                heads = lambda v: v.rearrange("p (h d) -> p h d", h=H)
                nc.gpsimd.tensor_tensor(heads(scaled[:, :]), heads(acc), spread(keep_by[:, p.parity, :], HD + 1),
                                        ALU.mult).then_inc(s["scaled"], 1)

            def gather(q):
                if q.since(RING):
                    scale_sums(Step(q.s - RING, q.slot, q.turn - 1))
                pool.wait_ge(s_loaded[q.slot], 48 * (q.turn + 1))
                nc.gpsimd.sem_inc(s["waited_by_pool"], 1)
                for k in range(C):
                    pool.indirect_dma_start(src[:, q.slot, k, :], None, scr["rows"],
                                            bass.IndirectOffsetOnAxis(ap=rec_i[:, q.slot, SRC + k:SRC + k + 1], axis=0)
                                            ).then_inc(s_gathered[q.slot], 16)

            nc.gpsimd.memset(keep["x1"][:, TILES - 1:NT, :], 0.0).then_inc(s["x_pad"], 1)
            def last(q):
                gather(q)
                for k in range(STEPS - RING, STEPS):
                    scale_sums(Step(k, k % RING, k // RING))

            loop(nc.gpsimd, gather, lambda: gather(first_step), last, 1)

        @block.tensor
        def _(pe):
            def turn_edges(q, half):
                n = 2 * q.s + half
                ks = range(4 * half, 4 * half + 4)
                if half == 0:
                    pe.wait_ge(s_loaded[q.slot], 48 * (q.turn + 1))
                if q.since(1) or half:
                    pe.wait_ge(s["attr_moved"], n)
                    pe.wait_ge(s["hot_moved"], n)
                nc.tensor.sem_inc(s["waited_by_pe"], 1)
                for j, k in enumerate(ks):
                    last = nc.tensor.transpose(p_attrT[:, j, :], rec_b[:, q.slot, 2 * ATTR + KE * k:2 * ATTR + KE * (k + 1)], keep["identb"][:, :])
                pe.wait_ge(s["hotb"], n + 1)
                for j, k in enumerate(ks):
                    last = nc.tensor.transpose(p_turn[:, j, :], hotb[:, q.slot, k, :], keep["identb"][:, :])
                last.then_inc(s["turned"], 1)

            def pair(q, r):
                b, n = q.slot, PAIRS * q.s + r
                pe.wait_ge(s["attr_moved"], 2 * q.s + (2 * r) // 4 + 1)
                if q.since(1) or r >= 2:
                    pe.wait_ge(s["relu"], n - 1)
                for j in range(2):
                    k = 2 * r + j
                    last = nc.tensor.matmul(p_enc[r % 2][:, j * D:(j + 1) * D], attrT[:, q.parity, k * P:(k + 1) * P],
                                            keep["expander"][:, :], start=True, stop=True)
                last.then_inc(s["enc"], 1)
                pe.wait_ge(s["hot_moved"], 2 * q.s + (2 * r) // 4 + 1)
                if q.since(1) or r >= 2:
                    pe.wait_ge(s["prod"], n - 1)
                if r == 0 and q.since(1):
                    pe.wait_ge(s["dst_score"], q.s)
                for j in range(2):
                    k = 2 * r + j
                    for i in range(3):
                        nc.tensor.matmul(p_dst[r % 2][:, j * D:(j + 1) * D], hotT[:, b, k * P:(k + 1) * P],
                                         node[:, q.slot, i * PART:i * PART + D], start=(i == 0), stop=(i == 2))
                    for i in range(3):
                        last = nc.tensor.matmul(p_score[:, k * H:(k + 1) * H], hotT[:, b, k * P:(k + 1) * P],
                                                node[:, q.slot, i * PART + D:(i + 1) * PART], start=(i == 0), stop=(i == 2))
                last.then_inc(s["dst_picked"], 1)

            def turn_scores(q):
                pe.wait_ge(s["score"], q.s + 1)
                if q.since(1):
                    pe.wait_ge(s["masked"], q.s)
                nc.tensor.transpose(p_scoreT, score[:, q.parity, :], keep["ident"][:, :]).then_inc(s["scoreT"], 1)

            def turn_back(q):
                pe.wait_ge(s["running"], q.s + 1)
                nc.tensor.transpose(p_back, running[:, :], keep["ident"][:, :]).then_inc(s["lasts_back"], 1)

            def tops(q):
                pe.wait_ge(s["lasts_parts"], q.s + 1)
                for k in range(C):
                    for i in range(3):
                        last = nc.tensor.matmul(p_top[:, k, :], hotb[:, q.slot, k, :], lasts_p[:, i, k, :], start=(i == 0), stop=(i == 2))
                last.then_inc(s["chunk_tops"], 1)

            def refs(q):
                b = q.slot
                pe.wait_ge(s["top_parts"], q.s + 1)
                if q.since(1):
                    pe.wait_ge(s["merged"], q.s)
                for k in range(C):
                    for i in range(3):
                        last = nc.tensor.matmul(p_ref[:, k * H:(k + 1) * H], hotT[:, b, k * P:(k + 1) * P], top_p[:, i, :],
                                                start=(i == 0), stop=(i == 2))
                last.then_inc(s["refs"], 1)

            def sums(q, half):
                pe.wait_ge(s["weight_row"], q.s + 1)
                pe.wait_ge(s["weighted"], 2 * q.s + half + 1)
                pe.wait_ge(s["hot"], q.s + 1)
                if half == 0:
                    pe.wait_ge(s["below"], q.s + 1)
                for k in range(4 * half, 4 * half + 4):
                    last = nc.tensor.matmul(p_sum, hot[:, q.parity, k, :], weighted[:, k, :], start=(k == 0), stop=(k == C - 1))
                if half:
                    last.then_inc(s["sums"], 1)

            def first():
                for half in range(2):
                    turn_edges(first_step, half)
                for r in range(PAIRS):
                    pair(first_step, r)
                second = first_step.next()
                for half in range(2):
                    turn_edges(second, half)
                pair(second, 0)
                pair(second, 1)
                body(first_step)

            def body(q, ahead=True):
                n = q.next()
                turn_scores(q)
                if q.since(1):
                    refs(q.prev())
                pair(n, 2)
                turn_back(q)
                pair(n, 3)
                if ahead:
                    turn_edges(n.next(), 0)
                if q.since(1):
                    sums(q.prev(), 0)
                tops(q)
                if ahead:
                    turn_edges(n.next(), 1)
                if q.since(1):
                    sums(q.prev(), 1)
                if ahead:
                    pair(n.next(), 0)
                    pair(n.next(), 1)

            def last(q):
                body(q.prev(), ahead=False)
                turn_scores(q)
                refs(q.prev())
                turn_back(q)
                tops(q)
                for p in (q.prev(), q):
                    if p is q:
                        refs(q)
                    sums(p, 0)
                    sums(p, 1)

            loop(nc.tensor, body, first, last)

        @block.scalar
        def _(act):
            def measure(q, half):
                if half == 0:
                    act.wait_ge(s_loaded[q.slot], 48 * (q.turn + 1))
                    nc.scalar.activation(local[:, q.parity, :], rec[:, q.slot, DST:DST + C], ACT.Identity,
                                         bias=q.column(keep["tile_base"]), scale=-1.0).then_inc(s["local"], 1)
                    act.wait_ge(s["local"], q.s + 1)
                if q.since(1) or half:
                    act.wait_ge(s["hotb"], 2 * q.s + half)
                for j in range(4):
                    k = 4 * half + j
                    last = nc.scalar.activation(away[:, j * P:(j + 1) * P], keep["node_at"][:, :], ACT.Abs, bias=local[:, q.parity, k:k + 1])
                last.then_inc(s["away"], 1)

            def make_hotb(q, half):
                if q.since(RING):
                    act.wait_ge(s["hot"], q.s - RING + 1)
                    act.wait_ge(s["chunk_tops"], q.s - RING + 1)
                act.wait_ge(s["away"], 2 * q.s + half + 1)
                nc.scalar.activation(hotb[:, q.slot, 4 * half:4 * half + 4, :].rearrange("p k n -> p (k n)"), away[:, :],
                                     ACT.Relu, scale=-1.0, bias=1.0).then_inc(s["hotb"], 1)

            def make_hot(q):
                if q.since(2):
                    act.wait_ge(s["sums"], q.s - 1)
                act.wait_ge(s["hotb"], 2 * q.s + 2)
                nc.scalar.copy(hot[:, q.parity, :, :], hotb[:, q.slot, :, :]).then_inc(s["hot"], 1)

            def move_turned(q, half):
                b, n = q.slot, 2 * q.s + half
                cols = slice(half * 4 * P, (half + 1) * 4 * P)
                act.wait_ge(s["turned"], n + 1)
                if q.since(RING):
                    act.wait_ge(s["refs"], q.s - RING + 1)
                if q.since(2):
                    act.wait_ge(s["enc"], PAIRS * (q.s - 1))
                nc.scalar.copy(attrT[:, q.parity, cols], p_attrT.rearrange("p j n -> p (j n)")).then_inc(s["attr_moved"], 1)
                nc.scalar.copy(hotT[:, b, cols], p_turn.rearrange("p j n -> p (j n)")).then_inc(s["hot_moved"], 1)

            def move_scores(q):
                if q.since(1):
                    act.wait_ge(s["dots"], 2 * q.s)
                act.wait_ge(s["dst_picked"], PAIRS * (q.s + 1))
                nc.scalar.copy(prod[:, :, :, HD], p_score.rearrange("p (k h) -> p k h", k=C)).then_inc(s["dst_score"], 1)
                act.wait_ge(s_gathered[q.slot], 16 * C * (q.turn + 1))
                nc.scalar.copy(prod[:, :, :, HD + 1], src[:, q.slot, :, :].rearrange("p k (h d) -> p k h d", h=H)[:, :, :, HD]).then_inc(s["src_score"], 1)

            def relu(q, r):
                n = PAIRS * q.s + r
                act.wait_ge(s["enc"], n + 1)
                if q.since(1) or r >= 2:
                    act.wait_ge(s["prod"], n - 1)
                nc.scalar.activation(enc[:, r % 2, :], p_enc[r % 2][:, :], ACT.Relu).then_inc(s["relu"], 1)

            def rescale(q):
                act.wait_ge(s["drop"], q.s + 1)
                nc.scalar.activation(keep_by[:, q.parity, :], drop[:, :], ACT.Exp).then_inc(s["kept"], 1)

            def weights(q):
                act.wait_ge(s["capped"], q.s + 1)
                if q.since(1):
                    act.wait_ge(s["weighted"], 2 * q.s)
                nc.scalar.activation(weight[:, :], capped[:, :], ACT.Exp).then_inc(s["weight"], 1)
                if q.since(1):
                    act.wait_ge(s["sums"], q.s)
                nc.scalar.activation(weighted[:, :, :].rearrange("p k (h d) -> p k h d", h=H)[:, :, :, HD],
                                     capped[:, :].rearrange("p (k h) -> p k h", k=C), ACT.Exp).then_inc(s["weight_row"], 1)

            def first():
                second = first_step.next()
                for q in (first_step, second, second.next()):
                    for half in range(2 if q.s < 2 else 1):
                        measure(q, half)
                        make_hotb(q, half)
                for half in range(2):
                    move_turned(first_step, half)
                for r in range(PAIRS):
                    relu(first_step, r)
                move_scores(first_step)
                for half in range(2):
                    move_turned(second, half)
                relu(second, 0)
                relu(second, 1)
                body(first_step)

            def body(q, ahead=2):
                n = q.next()
                m2 = n.next()
                relu(n, 2)
                if q.since(1):
                    weights(q.prev())
                    rescale(q.prev())
                relu(n, 3)
                move_scores(n)
                if ahead:
                    measure(m2, 1)
                    make_hotb(m2, 1)
                    move_turned(m2, 0)
                make_hot(q)
                if ahead > 1:
                    measure(m2.next(), 0)
                if ahead:
                    move_turned(m2, 1)
                if ahead > 1:
                    make_hotb(m2.next(), 0)
                if ahead:
                    relu(m2, 0)
                    relu(m2, 1)

            def last(q):
                body(q.prev().prev(), 1)
                body(q.prev(), 0)
                weights(q.prev())
                rescale(q.prev())
                make_hot(q)
                rescale(q)
                weights(q)

            loop(nc.scalar, body, first, last, 3)

        @block.vector
        def _(dve):
            def product(q, r):
                n = PAIRS * q.s + r
                dve.wait_ge(s["relu"], n + 1)
                dve.wait_ge(s["dst_picked"], n + 1)
                if q.since(1):
                    dve.wait_ge(s["dots"], 2 * q.s - 1 + r // 2)
                by_head = lambda v: v.rearrange("p (k h d) -> p k h d", k=2, h=H)
                nc.vector.tensor_tensor(prod[:, 2 * r:2 * r + 2, :, 0:HD], by_head(enc[:, r % 2, :]), by_head(p_dst[r % 2][:, :]),
                                        ALU.mult).then_inc(s["prod"], 1)

            def sum_heads(q, half):
                dve.wait_ge(s["prod"], PAIRS * q.s + 2 * half + 2)
                dve.wait_ge(s["src_score"], q.s + 1)
                n, ks = C * H // 2, slice(4 * half, 4 * half + 4)
                nc.vector.tensor_reduce(dots[:, q.parity, half * n:(half + 1) * n], prod[:, ks, :, :].rearrange("p k h d -> p (k h) d"),
                                        AX.X, ALU.add).then_inc(s["dots"], 1)

            def scores(q):
                dve.wait_ge(s["dots"], 2 * q.s + 2)
                if q.since(2):
                    dve.wait_ge(s["below"], q.s - 1)
                d = dots[:, q.parity, :]
                nc.vector.scalar_tensor_tensor(score[:, q.parity, 0:C * H], d, 0.2, d, ALU.mult, ALU.max).then_inc(s["score"], 1)

            def scan(q):
                dve.wait_ge(s["scoreT"], q.s + 1)
                nc.vector.tensor_tensor_scan(running[0:C * H, :], starts[:, q.slot, :], p_scoreT[0:C * H, :], -BIG, ALU.add, ALU.max).then_inc(s["running"], 1)

            def mask_lasts(q):
                last_v = rec[:, q.slot, LAST:LAST + C]
                if q.since(1):
                    dve.wait_ge(s["chunk_tops"], q.s)
                nc.vector.tensor_copy(lasts_p[:, 0, :, H], last_v)
                dve.wait_ge(s["lasts_back"], q.s + 1)
                nc.vector.tensor_tensor(lasts[:, :, :], p_lasts.rearrange("p (k h) -> p k h", k=C),
                                        spread(last_v, H), ALU.mult).then_inc(s["lasts"], 1)

            def split_lasts(q, stage):
                if stage == 0:
                    dve.wait_ge(s["lasts"], q.s + 1)
                    nc.vector.tensor_copy(lasts_p[:, 0, :, 0:H], lasts[:, :, :]).then_inc(s["lasts_hi"], 1)
                    dve.wait_ge(s["lasts_hi"], q.s + 1)
                    nc.vector.tensor_tensor(lasts_left[:, :, :], lasts[:, :, :], lasts_p[:, 0, :, 0:H], ALU.subtract).then_inc(s["lasts_left"], 1)
                elif stage == 1:
                    dve.wait_ge(s["lasts_left"], q.s + 1)
                    nc.vector.tensor_copy(lasts_p[:, 1, :, 0:H], lasts_left[:, :, :]).then_inc(s["lasts_mid"], 1)
                else:
                    dve.wait_ge(s["lasts_mid"], q.s + 1)
                    nc.vector.tensor_tensor(lasts_p[:, 2, :, 0:H], lasts_left[:, :, :], lasts_p[:, 1, :, 0:H], ALU.subtract).then_inc(s["lasts_parts"], 1)

            def top_of_chunk(q, stage):
                if stage == 0:
                    dve.wait_ge(s["chunk_tops"], q.s + 1)
                    nc.vector.tensor_scalar(absent[:, :], p_top[:, :, H], BIG, -BIG, ALU.mult, ALU.add).then_inc(s["absent"], 1)
                elif stage == 1:
                    dve.wait_ge(s["absent"], q.s + 1)
                    nc.vector.tensor_tensor(masked[:, :, :], p_top[:, :, 0:H], spread(absent[:, :], H), ALU.add).then_inc(s["masked"], 1)
                else:
                    dve.wait_ge(s["masked"], q.s + 1)
                    nc.vector.tensor_reduce(chunk_top[:, :], masked[:, :, :].rearrange("p k h -> p h k"), AX.X, ALU.max).then_inc(s["chunk_top"], 1)

            def update_top(q, tile, stage):
                top = at(keep["top"], tile)
                if stage == 0:
                    dve.wait_ge(s["chunk_top"], q.s + 1)
                    nc.vector.tensor_tensor(new_top[:, :], chunk_top[:, :], top, ALU.max).then_inc(s["new_top"], 1)
                elif stage == 1:
                    dve.wait_ge(s["new_top"], q.s + 1)
                    nc.vector.tensor_copy(top_p[:, 0, :], new_top[:, :]).then_inc(s["top_hi"], 1)
                    if q.since(1):
                        dve.wait_ge(s["kept"], q.s)
                    nc.vector.tensor_tensor(drop[:, :], top, new_top[:, :], ALU.subtract).then_inc(s["drop"], 1)
                else:
                    dve.wait_ge(s["drop"], q.s + 1)
                    nc.vector.tensor_scalar(top, new_top[:, :], 1.0, None, ALU.mult).then_inc(s["top_kept"], 1)

            def split_top(q, stage):
                if stage == 0:
                    dve.wait_ge(s["top_hi"], q.s + 1)
                    nc.vector.tensor_tensor(top_left[:, :], new_top[:, :], top_p[:, 0, :], ALU.subtract).then_inc(s["top_left"], 1)
                elif stage == 1:
                    dve.wait_ge(s["top_left"], q.s + 1)
                    nc.vector.tensor_copy(top_p[:, 1, :], top_left[:, :]).then_inc(s["top_mid"], 1)
                else:
                    dve.wait_ge(s["top_mid"], q.s + 1)
                    nc.vector.tensor_tensor(top_p[:, 2, :], top_left[:, :], top_p[:, 1, :], ALU.subtract).then_inc(s["top_parts"], 1)

            def exponents(q, stage):
                if stage == 0:
                    dve.wait_ge(s["refs"], q.s + 1)
                    nc.vector.tensor_tensor(below[:, :], score[:, q.parity, 0:C * H], p_ref, ALU.subtract).then_inc(s["below"], 1)
                else:
                    dve.wait_ge(s["below"], q.s + 1)
                    if q.since(1):
                        dve.wait_ge(s["weight_row"], q.s)
                    nc.vector.tensor_scalar(capped[:, :], below[:, :], 0.0, None, ALU.min).then_inc(s["capped"], 1)

            def apply_weights(q, half):
                if half == 0:
                    dve.wait_ge(s["weight"], q.s + 1)
                    if q.since(1):
                        dve.wait_ge(s["sums"], q.s)
                ks = slice(4 * half, 4 * half + 4)
                w = weight[:, :].rearrange("p (k h) -> p k h", k=C)[:, ks, :].rearrange("p k h -> p (k h)")
                nc.vector.tensor_tensor(weighted[:, ks, :].rearrange("p k (h d) -> p (k h) d", h=H)[:, :, 0:HD],
                                        src[:, q.slot, ks, :].rearrange("p k (h d) -> p (k h) d", h=H)[:, :, 0:HD],
                                        spread(w, HD), ALU.mult).then_inc(s["weighted"], 1)

            def add_sums(q, tile):
                acc = at(keep["acc"], tile)
                dve.wait_ge(s["scaled"], q.s + 1)
                dve.wait_ge(s["sums"], q.s + 1)
                nc.vector.tensor_tensor(acc, scaled[:, :], p_sum, ALU.add).then_inc(s["merged"], 1)

            def load_tile(q):
                return nc.vector.value_load(q.column(keep["step_tile"]), min_val=0, max_val=TILES - 1)

            def first():
                nc.vector.memset(score[:, :, :], 0.0).then_inc(s["zeros"], 1)
                nc.vector.memset(running[:, :], 0.0).then_inc(s["zeros"], 1)
                nc.vector.memset(lasts_p[:, 1:3, :, H], 0.0).then_inc(s["zeros"], 1)
                dve.wait_ge(s["zeros"], 3)
                for r in range(PAIRS):
                    product(first_step, r)
                sum_heads(first_step, 0)
                sum_heads(first_step, 1)
                scores(first_step)
                body(first_step)

            def body(q):
                n = q.next()
                before = q.prev() if q.since(1) else None
                product(n, 0)
                scan(q)
                if before:
                    exponents(before, 0)
                product(n, 1)
                if before:
                    exponents(before, 1)
                mask_lasts(q)
                split_lasts(q, 0)
                if before:
                    apply_weights(before, 0)
                    tile_before = load_tile(before)
                tile = load_tile(q)
                split_lasts(q, 1)
                product(n, 2)
                split_lasts(q, 2)
                if before:
                    apply_weights(before, 1)
                product(n, 3)
                top_of_chunk(q, 0)
                top_of_chunk(q, 1)
                sum_heads(n, 0)
                top_of_chunk(q, 2)
                sum_heads(n, 1)
                update_top(q, tile, 0)
                scores(n)
                if before:
                    add_sums(before, tile_before)
                update_top(q, tile, 1)
                split_top(q, 0)
                update_top(q, tile, 2)
                split_top(q, 1)
                split_top(q, 2)

            def last(q):
                body(q.prev())
                tile_before, tile = load_tile(q.prev()), load_tile(q)
                scan(q)
                for stage in range(2):
                    exponents(q.prev(), stage)
                mask_lasts(q)
                for stage in range(3):
                    split_lasts(q, stage)
                for half in range(2):
                    apply_weights(q.prev(), half)
                for stage in range(3):
                    top_of_chunk(q, stage)
                update_top(q, tile, 0)
                update_top(q, tile, 1)
                split_top(q, 0)
                update_top(q, tile, 2)
                split_top(q, 1)
                split_top(q, 2)
                add_sums(q.prev(), tile_before)
                for stage in range(2):
                    exponents(q, stage)
                for half in range(2):
                    apply_weights(q, half)
                add_sums(q, tile)
                dve.wait_ge(s["merged"], STEPS)

            loop(nc.vector, body, first, last)


EXP_AT = (3, 17, 24)
INDEX_AT = 22


def epilogue(nc, a, keep, out):
    hidden = FF // P
    blocks = -(-N // (2 * P))
    last_cols = N - (blocks - 1) * 2 * P
    assert last_cols <= P and NT == 2 * blocks and TOPK == 2 and NT % 10 == 0 and (TILES - 1) % 8 == 0
    firsts = [(t0, t0 + 10) for t0 in range(0, NT, 10)]
    lasts = [(t0, t0 + 8 if t0 + 9 < TILES else TILES) for t0 in range(0, TILES - 1, 8)]
    with Scope(nc) as m:
        x1 = keep["x1"]
        moe = keep["acc"][:, :, 0:D]
        x2T = m.sb("x2T", [P, 2, NT * P])
        fresh = m.sb("fresh", [P, 2, D])
        denom = m.sb("denom", [P, NT, H])
        inverse = m.sb("inverse", [P, NT, H])
        bias = m.sb("bias", [P, D])
        gamma = m.sb("gamma", [P, D])
        beta = m.sb("beta", [P, D])
        stats = m.sb("e_stats", [P, NT, 6])
        halves = m.sb("e_halves", [P, 4, NT])
        moments = m.sb("e_moments", [P, NT, 2])
        std = m.sb("e_std", [P, NT])
        rstd = m.sb("e_rstd", [P, NT, 1])
        eps = m.sb("e_eps", [P, 1])
        col_sums = m.sb("col_sums", [P, 2, TILES])
        mean = m.sb("mean", [P, 2])
        total = m.sb("total", [P, 2])
        wr = m.sb("wr", [P, 2, NX])
        share = m.sb("share", [P, TOPK])
        w1 = m.sb("w1", [P, TOPK, 2, FF])
        w2 = m.sb("w2", [P, TOPK, hidden, D])
        b1 = m.sb("b1", [P, TOPK, hidden])
        b2 = m.sb("b2", [P, TOPK, D])
        b2_mix = m.sb("b2_mix", [P, D])
        act_h = m.sb("act_h", [P, 2, TOPK * hidden, 2 * P])
        normed = m.sb("normed", [P, 2, D])
        r_ = {n: m.sb("r_" + n, [1, w], dt) for n, w, dt in (
            ("br", NX, F32), ("logits", NX, F32), ("top", 1, F32), ("d", NX, F32), ("e", NX, F32), ("sum", 1, F32),
            ("p", NX, F32), ("load", NX, F32), ("q", NX, F32), ("over", NX, F32), ("under", NX, F32),
            ("scale", NX, F32), ("t", NX, F32), ("best", NX, F32), ("index", NX, U32), ("w2", TOPK, F32), ("ones", P, F32))}

        p_T = [m.ps(f"p_T{i}", [P, 2, P]) for i in range(2)]
        p_up = [m.ps(f"p_up{i}", [P, 2 * P]) for i in range(4)]
        p_y = [m.ps(f"p_y{i}", [P, D]) for i in range(2)]
        p_r = p_y[0]

        names = """eps std std2 ones bias vec x_biased denom inverse gnn x1 stats moments rstd x2 x2_kept x2T x2T_moved pad
            wr total mean logits share expert b2a b2_mix w2_scaled x1_beta b2_added up act_h down moe stats2
            moments2 rstd2 normed scaled result small stored expo shared""".split()
        s = {n: m.sem("e_" + n) for n in names}
        heads = lambda v: v.rearrange("p (h d) -> p h d", h=H)
        block = m.enter_context(nc.Block())

        @block.sync
        def _(sp):
            sp.dma_start(bias[:, :], a["gnn_bias"].partition_broadcast(P)).then_inc(s["bias"], 16)
            sp.dma_start(gamma[:, :], a["gamma"].partition_broadcast(P)).then_inc(s["vec"], 16)
            sp.dma_start(beta[:, :], a["beta"].partition_broadcast(P)).then_inc(s["vec"], 16)
            sp.dma_start(wr[:, :, :], a["Wr"].rearrange("(c p) n -> p c n", p=P)).then_inc(s["wr"], 16)
            sp.dma_start(r_["br"][:, :], a["br"].rearrange("(o n) -> o n", o=1)).then_inc(s["wr"], 16)
            sp.wait_ge(s["small"], INDEX_AT)
            for k in range(TOPK):
                e = nc.sync.value_load(r_["index"][0:1, k:k + 1], min_val=0, max_val=NX - 1)
                one = lambda v: v[bass.ds(e, 1)]
                sp.dma_start(w1[:, k, :, :], one(a["W1"]).rearrange("o (c p) f -> p (o c) f", p=P)).then_inc(s["expert"], 16)
                sp.dma_start(w2[:, k, :, :], one(a["W2"]).rearrange("o (c p) f -> p (o c) f", p=P)).then_inc(s["expert"], 16)
                sp.dma_start(b1[:, k, :], one(a["b1"]).rearrange("o (c p) -> p (o c)", p=P), allow_slow_non_contiguous=True).then_inc(s["expert"], 16)
                sp.dma_start(b2[:, k, :], one(a["b2"]).rearrange("o n -> (o n)").partition_broadcast(P)).then_inc(s["expert"], 16)
            def store(t, rows=P):
                dst = out[t * P:t * P + rows, :] if isinstance(t, int) else out[bass.ds(t * P, P), :]
                sp.wait_ge(s["result"], t + 1)
                sp.dma_start(dst, at(x1, t)[0:rows, :]).then_inc(s["stored"], 16)

            with nc.sync.Fori(0, TILES - 1) as t:
                store(t)
            store(TILES - 1, LASTROWS)
            sp.wait_ge(s["stored"], 16 * TILES)

        @block.gpsimd
        def _(pool):
            def add_bias(rows):
                t0, t1 = rows
                with nc.gpsimd.Fori(0, (t1 - t0) // 5) as i:
                    for u in range(5):
                        t = i * 5 + t0 + u
                        nc.gpsimd.tensor_tensor(at(x1, t), at(x1, t), bias[:, :], ALU.add).then_inc(s["x_biased"], 1)

            nc.gpsimd.memset(x2T[:, :, (TILES - 1) * P:], 0.0).then_inc(s["pad"], 1)
            nc.gpsimd.memset(eps[:, :], LN_EPS).then_inc(s["eps"], 1)
            nc.gpsimd.memset(r_["ones"][:, :], 1.0).then_inc(s["ones"], 1)
            pool.wait_ge(keep["x_loaded"], 32)
            pool.wait_ge(s["bias"], 16)
            for rows in firsts:
                add_bias(rows)
            def add_vectors(t0, t1):
                with nc.gpsimd.Fori(0, (t1 - t0) // 5) as i:
                    for u in range(5):
                        t = i * 5 + t0 + u
                        nc.gpsimd.tensor_tensor(at(moe, t), at(moe, t), b2_mix[:, :], ALU.add).then_inc(s["b2_added"], 1)
                        nc.gpsimd.tensor_tensor(at(x1, t), at(x1, t), beta[:, :], ALU.add).then_inc(s["x1_beta"], 1)

            pool.wait_ge(s["b2_mix"], 1)
            pool.wait_ge(s["x2_kept"], NT)
            pool.wait_ge(s["x2"], NT)
            pool.wait_ge(s["vec"], 32)
            add_vectors(0, NT)

        @block.tensor
        def _(pe):
            def turn(t, b):
                pe.wait_ge(s["x2"], t + 1)
                if not (isinstance(t, int) and t < 2):
                    pe.wait_ge(s["x2T_moved"], 2 * (t - 1))
                for i in range(2):
                    last = nc.tensor.transpose(p_T[b][:, i, :], normed[:, b, i * P:(i + 1) * P], keep["ident"][:, :])
                last.then_inc(s["x2T"], 1)

            turn(0, 0)
            turn(1, 1)
            with nc.tensor.Fori(0, (TILES - 3) // 2) as i:
                for u in range(2):
                    turn(2 * i + 2 + u, u)
            turn(TILES - 1, 0)
            pe.wait_ge(s["mean"], 1)
            pe.wait_ge(s["wr"], 32)
            for i in range(2):
                last = nc.tensor.matmul(p_r[0:1, 0:NX], mean[:, i:i + 1], wr[:, i, :], start=(i == 0), stop=(i == 1))
            last.then_inc(s["logits"], 1)
            pe.wait_ge(s["ones"], 1)
            pe.wait_ge(s["small"], EXP_AT[2] + 3)
            nc.tensor.matmul(p_r[:, 64:64 + TOPK], r_["ones"][:, :], r_["w2"][:, :], start=True, stop=True).then_inc(s["share"], 1)

            def up(j, cols=2 * P):
                for n in range(TOPK * hidden):
                    k, f = n // hidden, n % hidden
                    if not (isinstance(j, int) and j == 0 and n < 4):
                        pe.wait_ge(s["act_h"], TOPK * hidden * j + n - 3)
                    for i in range(2):
                        x = x2T[:, i, j * 2 * P:j * 2 * P + cols] if isinstance(j, int) else x2T[:, i, bass.ds(j * 2 * P, cols)]
                        last = nc.tensor.matmul(p_up[n % 4][:, 0:cols], w1[:, k, i, f * P:(f + 1) * P], x, start=(i == 0), stop=(i == 1))
                    last.then_inc(s["up"], 1)

            def down(j, b, tiles=2):
                for u in range(tiles):
                    pe.wait_ge(s["act_h"], TOPK * hidden * (j + 1))
                    if not (isinstance(j, int) and j == 0):
                        pe.wait_ge(s["moe"], 2 * j + u - 1)
                    for n in range(TOPK * hidden):
                        k, f = n // hidden, n % hidden
                        last = nc.tensor.matmul(p_y[u][:, :], act_h[:, b, n, u * P:(u + 1) * P], w2[:, k, f, :], start=(n == 0), stop=(n == TOPK * hidden - 1))
                    last.then_inc(s["down"], 1)

            pe.wait_ge(s["expert"], 64 * TOPK)
            up(0)
            up(1)
            pe.wait_ge(s["w2_scaled"], TOPK)
            down(0, 0)
            with nc.tensor.Fori(0, (blocks - 3) // 2) as i:
                for u in range(2):
                    up(2 * i + 2 + u)
                    down(2 * i + 1 + u, 1 - u)
            up(blocks - 1, last_cols)
            down(blocks - 2, 1)
            down(blocks - 1, 0, 1)

        @block.scalar
        def _(act):
            def move(t, b, cols=P):
                act.wait_ge(s["x2T"], t + 1)
                for i in range(2):
                    to = x2T[:, i, t * P:t * P + cols] if isinstance(t, int) else x2T[:, i, bass.ds(t * P, P)]
                    total_at = col_sums[:, i, t:t + 1] if isinstance(t, int) else col_sums[:, i, bass.ds(t, 1)]
                    nc.scalar.activation(to, p_T[b][:, i, 0:cols], ACT.Copy, accum_out=total_at).then_inc(s["x2T_moved"], 1)
                nc.scalar.copy(at(moe, t), normed[:, b, :]).then_inc(s["x2_kept"], 1)

            def deviations(rows, merged, groups, made):
                t0, t1 = rows
                act.wait_ge(s[merged], 6 * groups)
                nc.scalar.activation(std[:, t0:t1], moments[:, t0:t1, 1], ACT.Sqrt, bias=eps[:, 0:1]).then_inc(s[made], 1)

            act.wait_ge(s["pad"], 1)
            act.wait_ge(s["eps"], 1)
            deviations(firsts[0], "moments", 1, "std")
            for g in range(len(firsts)):
                t0, t1 = firsts[g][0], min(firsts[g][1], TILES - 1)
                turns = (t1 - t0) // 2
                with nc.scalar.Fori(0, turns) as i:
                    for u in range(2):
                        move(2 * i + t0 + u, u)
                if g + 1 < len(firsts):
                    deviations(firsts[g + 1], "moments", g + 2, "std")
            move(TILES - 1, 0, LASTROWS)
            act.wait_ge(s["x2"], NT)
            nc.scalar.copy(moe[:, NT - 1, :], normed[:, 1, :]).then_inc(s["x2_kept"], 1)
            for n in range(3):
                act.wait_ge(s["small"], EXP_AT[n])
                w = NX if n < 2 else TOPK
                nc.scalar.activation(r_["e"][:, 0:w], r_["d"][:, 0:w], ACT.Exp).then_inc(s["expo"], 1)

            def gelu(j, b, cols=2 * P):
                for n in range(TOPK * hidden):
                    act.wait_ge(s["up"], TOPK * hidden * j + n + 1)
                    if n == 0 and not (isinstance(j, int) and j < 2):
                        act.wait_ge(s["down"], 2 * (j - 1))
                    k, f = n // hidden, n % hidden
                    nc.scalar.activation(act_h[:, b, n, 0:cols], p_up[n % 4][:, 0:cols], ACT.Gelu,
                                         bias=b1[:, k, f:f + 1]).then_inc(s["act_h"], 1)

            act.wait_ge(s["expert"], 64 * TOPK)
            gelu(0, 0)
            gelu(1, 1)
            for g in range(len(lasts) - 1):
                with nc.scalar.Fori(0, 2) as i:
                    for u in range(2):
                        gelu(2 * i + 4 * g + 2 + u, u)
                deviations(lasts[g], "moments2", g + 1, "std2")
            for j in range(4 * len(lasts) - 2, blocks):
                gelu(j, j % 2, last_cols if j == blocks - 1 else 2 * P)
            deviations(lasts[-1], "moments2", len(lasts), "std2")

        @block.vector
        def _(dve):
            nc.vector.tensor_scalar(denom[:, :, :], keep["acc"][:, :, :].rearrange("p t (h d) -> p t h d", h=H)[:, :, :, HD], 1e-10, None, ALU.max).then_inc(s["denom"], 1)
            dve.wait_ge(s["denom"], 1)
            nc.vector.reciprocal(inverse[:, :, :], denom[:, :, :]).then_inc(s["inverse"], 1)
            dve.wait_ge(s["inverse"], 1)

            def attend(t, b):
                nc.vector.tensor_tensor(heads(fresh[:, b, :]), heads(at(keep["acc"], t))[:, :, 0:HD],
                                        spread(at(inverse, t), HD), ALU.mult).then_inc(s["gnn"], 1)

            def add_x(t, b):
                dve.wait_ge(s["gnn"], t + 1)
                dve.wait_ge(s["x_biased"], t + 1)
                nc.vector.tensor_tensor(at(x1, t), at(x1, t), fresh[:, b, :], ALU.add).then_inc(s["x1"], 1)

            def measure(t):
                dve.wait_ge(s["x1"], t + 1)
                nc.vector.bn_stats(at(stats, t), at(x1, t)).then_inc(s["stats"], 1)

            def first_norm(t, b):
                if not (isinstance(t, int) and t < 2):
                    dve.wait_ge(s["x2T"], t - 1)
                    dve.wait_ge(s["x2_kept"], t - 1)
                nc.vector.tensor_scalar(normed[:, b, :], at(x1, t), moments[:, bass.ds(t, 1), 0], at(rstd, t),
                                        ALU.subtract, ALU.mult).then_inc(s["x2"], 1)

            for g in range(len(firsts) + 1):
                t0 = 10 * g
                if g:
                    dve.wait_ge(s["std"], g)
                    nc.vector.reciprocal(rstd[:, t0 - 10:t0, 0], std[:, t0 - 10:t0]).then_inc(s["rstd"], 1)
                    dve.wait_ge(s["rstd"], g)
                def two(t):
                    if g < len(firsts):
                        for b in range(2):
                            attend(t + b, b)
                    for b in range(2):
                        if g:
                            first_norm(t - 10 + b, b)
                        if g < len(firsts):
                            add_x(t + b, b)
                    if g < len(firsts):
                        for b in range(2):
                            measure(t + b)

                peeled = 1 if g == 1 else 0
                if peeled:
                    two(t0)
                with nc.vector.Fori(0, 5 - peeled) as i:
                    two(i * 2 + t0 + 2 * peeled)
                if g < len(firsts):
                    dve.wait_ge(s["stats"], t0 + 10)
                    merge_moments(nc, dve, stats, halves, moments, s["moments"], firsts[g], g)

            dve.wait_ge(s["x2T_moved"], 2 * TILES)
            nc.vector.tensor_reduce(total[:, :], col_sums[:, :, :], AX.X, ALU.add).then_inc(s["total"], 1)
            dve.wait_ge(s["total"], 1)
            nc.vector.tensor_scalar(mean[:, :], total[:, :], 1.0 / N, None, ALU.mult).then_inc(s["mean"], 1)
            dve.wait_ge(s["logits"], 1)
            dve.wait_ge(s["wr"], 32)
            count = [0]

            def link(ins):
                count[0] += 1
                ins.then_inc(s["small"], 1)
                dve.wait_ge(s["small"], count[0])

            def softmax(to, of, w, n):
                link(nc.vector.tensor_reduce(r_["top"][:, :], of, AX.X, ALU.max))
                link(nc.vector.tensor_scalar(r_["d"][:, 0:w], of, r_["top"][:, 0:1], None, ALU.subtract))
                assert count[0] == EXP_AT[n]
                dve.wait_ge(s["expo"], n + 1)
                link(nc.vector.tensor_reduce(r_["sum"][:, :], r_["e"][:, 0:w], AX.X, ALU.add))
                link(nc.vector.reciprocal(r_["sum"][:, :], r_["sum"][:, :]))
                link(nc.vector.tensor_scalar(to, r_["e"][:, 0:w], r_["sum"][:, 0:1], None, ALU.mult))

            link(nc.vector.tensor_tensor(r_["logits"][:, :], p_r[0:1, 0:NX], r_["br"][:, :], ALU.add))
            softmax(r_["p"][:, :], r_["logits"][:, :], NX, 0)
            link(nc.vector.tensor_scalar(r_["load"][:, :], r_["p"][:, :], float(N), None, ALU.mult))
            link(nc.vector.reciprocal(r_["q"][:, :], r_["load"][:, :]))
            link(nc.vector.tensor_scalar(r_["q"][:, :], r_["q"][:, :], CAPACITY, None, ALU.mult))
            link(nc.vector.tensor_scalar(r_["over"][:, :], r_["load"][:, :], CAPACITY, None, ALU.is_gt))
            link(nc.vector.tensor_scalar(r_["under"][:, :], r_["load"][:, :], CAPACITY, None, ALU.is_le))
            link(nc.vector.tensor_scalar(r_["q"][:, :], r_["q"][:, :], 1.0, None, ALU.min))
            link(nc.vector.tensor_tensor(r_["q"][:, :], r_["q"][:, :], r_["over"][:, :], ALU.mult))
            link(nc.vector.tensor_tensor(r_["scale"][:, :], r_["q"][:, :], r_["under"][:, :], ALU.add))
            link(nc.vector.tensor_tensor(r_["t"][:, :], r_["p"][:, :], r_["scale"][:, :], ALU.mult))
            softmax(r_["p"][:, :], r_["t"][:, :], NX, 1)
            link(nc.vector.max(r_["best"][:, :], r_["p"][:, :]))
            link(nc.vector.max_index(r_["index"][:, :], r_["best"][:, :], r_["p"][:, :]))
            assert count[0] == INDEX_AT
            softmax(r_["w2"][:, :], r_["best"][:, 0:TOPK], TOPK, 2)
            dve.wait_ge(s["share"], 1)
            nc.vector.tensor_copy(share[:, :], p_r[:, 64:64 + TOPK]).then_inc(s["shared"], 1)
            dve.wait_ge(s["shared"], 1)
            dve.wait_ge(s["expert"], 64 * TOPK)
            for k in range(TOPK):
                nc.vector.tensor_scalar(w2[:, k, :, :], w2[:, k, :, :], share[:, k:k + 1], None, ALU.mult).then_inc(s["w2_scaled"], 1)
            nc.vector.tensor_scalar(b2_mix[:, :], b2[:, 0, :], share[:, 0:1], None, ALU.mult).then_inc(s["b2a"], 1)
            dve.wait_ge(s["b2a"], 1)
            nc.vector.scalar_tensor_tensor(b2_mix[:, :], b2[:, 1, :], share[:, 1:2], b2_mix[:, :], ALU.mult, ALU.add).then_inc(s["b2_mix"], 1)

            def gather_down(t, u):
                dve.wait_ge(s["down"], t + 1)
                dve.wait_ge(s["b2_added"], t + 1)
                nc.vector.tensor_tensor(at(moe, t), at(moe, t), p_y[u][:, :], ALU.add).then_inc(s["moe"], 1)
                dve.wait_ge(s["moe"], t + 1)
                nc.vector.bn_stats(at(stats, t), at(moe, t)).then_inc(s["stats2"], 1)

            def finish(tiles):
                for b, t in enumerate(tiles):
                    mean_t = moments[:, t, 0:1] if isinstance(t, int) else moments[:, bass.ds(t, 1), 0]
                    if not (isinstance(t, int) and t < 2):
                        dve.wait_ge(s["result"], t - 1)
                    nc.vector.tensor_scalar(normed[:, b, :], at(moe, t), mean_t, at(rstd, t), ALU.subtract, ALU.mult).then_inc(s["normed"], 1)
                for b, t in enumerate(tiles):
                    dve.wait_ge(s["normed"], t + 1)
                    nc.vector.tensor_tensor(normed[:, b, :], normed[:, b, :], gamma[:, :], ALU.mult).then_inc(s["scaled"], 1)
                for b, t in enumerate(tiles):
                    dve.wait_ge(s["scaled"], t + 1)
                    nc.vector.tensor_tensor(at(x1, t), normed[:, b, :], at(x1, t), ALU.add).then_inc(s["result"], 1)

            def invert(g):
                t0, t1 = lasts[g]
                dve.wait_ge(s["std2"], g + 1)
                nc.vector.reciprocal(rstd[:, t0:t1, 0], std[:, t0:t1]).then_inc(s["rstd2"], 1)
                dve.wait_ge(s["rstd2"], g + 1)

            def merge_group(g):
                dve.wait_ge(s["stats2"], lasts[g][1])
                merge_moments(nc, dve, stats, halves, moments, s["moments2"], lasts[g], g)

            for g, (t0, t1) in enumerate(lasts):
                if g == 1:
                    dve.wait_ge(s["x1_beta"], NT // 2)
                if g == 3:
                    dve.wait_ge(s["x1_beta"], NT)
                if g:
                    invert(g - 1)

                def two(t):
                    for u in range(2):
                        gather_down(t + u, u)
                    if g:
                        finish([t - 8, t - 7])

                peeled = 1 if g == 1 else 0
                if peeled:
                    two(t0)
                with nc.vector.Fori(0, 4 - peeled) as i:
                    two(2 * i + t0 + 2 * peeled)
                if t1 == TILES:
                    gather_down(TILES - 1, 0)
                merge_group(g)
            invert(len(lasts) - 1)
            t0 = lasts[-1][0]
            with nc.vector.Fori(0, 4) as i:
                finish([2 * i + t0 + u for u in range(2)])
            finish([TILES - 1])


_INS = {"x": "x", "src": "src", "dst": "dst", "attr": "edge_attr_3", "W": "L0_gnn_W", "a_src": "L0_gnn_a_src",
        "a_dst": "L0_gnn_a_dst", "edge_W": "L0_gnn_edge_W", "edge_b": "L0_gnn_edge_b", "gnn_bias": "L0_gnn_bias",
        "Wr": "L0_ffn_Wr", "br": "L0_ffn_br", "W1": "L0_ffn_W1", "b1": "L0_ffn_b1", "W2": "L0_ffn_W2",
        "b2": "L0_ffn_b2", "gamma": "L0_ffn_gamma", "beta": "L0_ffn_beta"}


def build(nc, a, out):
    def dram(name, shape, dt):
        return nc.dram_tensor(name, shape, dt, kind="Internal").ap()

    scr = dict(rows=dram("node_rows", (NT * P, ROW), F32), parts=dram("node_parts", (NT, P, 3 * PART), BF16),
               edges=dram("edge_records", (NC, P, REC), F32), starts=dram("segment_starts", (NC, C * H, P), F32))
    with Scope(nc) as m:
        keep = dict(
            ident=m.sb("ident", [P, P]), identb=m.sb("identb", [P, P], BF16), node_at=m.sb("node_at", [P, P]),
            expander=m.sb("expander", [3 * KA, D], BF16), step_chunk=m.sb("step_chunk", [1, STEPS], I32),
            step_tile=m.sb("step_tile", [1, STEPS], I32), tile_base=m.sb("tile_base", [P, STEPS]),
            acc=m.sb("acc", [P, NT, ROW]), top=m.sb("top", [P, NT, H]),
        )
        prologue(nc, a, scr, keep)
        keep["x1"], keep["x_loaded"] = m.sb("x1", [P, NT, D]), m.sem("x_loaded")
        edge_loop(nc, a, scr, keep)
        epilogue(nc, a, keep, out)


def kernel(**inputs):
    import numpy as np
    import concourse.bacc as bacc
    from concourse.bass_utils import run_bass_kernel_spmd

    nc = bacc.Bacc("TRN2", target_bir_lowering=False, num_devices=1)
    arrays, args = {}, {}
    for short, name in _INS.items():
        v = np.ascontiguousarray(inputs[name])
        arrays["in_" + name] = v
        args[short] = nc.dram_tensor("in_" + name, v.shape, mybir.dt.from_np(v.dtype), kind="ExternalInput").ap()
    out = nc.dram_tensor("out_x", (N, D), F32, kind="ExternalOutput").ap()
    build(nc, args, out)
    r = run_bass_kernel_spmd(nc, [arrays], core_ids=[0])
    return r.results[0]["out_x"]
```
